# Optimizing a Trainium2 kernel written in Bass

```python
import numpy as np
import jax
import jax.numpy as jnp

def _softmax(x, axis=-1):
    return jax.nn.softmax(x, axis=axis)

def _gelu(x):
    return jax.nn.gelu(x, approximate=True)

def _silu(x):
    return jax.nn.silu(x)

def _sigmoid(x):
    return jax.nn.sigmoid(x)

def _layernorm(x, axis=-1, eps=1e-05):
    m = jnp.mean(x, axis=axis, keepdims=True)
    v = jnp.var(x, axis=axis, keepdims=True)
    return (x - m) / jnp.sqrt(v + eps)

def _scatter_add(tgt, idx, src, axis=0):
    return tgt.at[idx].add(src)

def _segment_sum(src, seg, n):
    return jax.ops.segment_sum(src, seg, n)
kernel_name = 'mk_flamingo_gated_d2_seqx_r8_26478d'

def setup_inputs(seed: int=0):
    np.random.seed(seed)
    _w = jnp.asarray

    def _rec_inputs():
        import jax
        import jax.numpy as jnp
        _rk = jax.random.key(seed)
        x = -0.0002928 + 1 * jax.random.normal(jax.random.fold_in(_rk, 1), (2, 512, 128), jnp.float32)
        _lenS = 512 - jax.random.randint(jax.random.fold_in(_rk, 7), (2,), 0, max(1, 512 // 4) + 1, jnp.int32)
        _lenS2 = 77 - jax.random.randint(jax.random.fold_in(_rk, 8), (2,), 0, max(1, 77 // 4) + 1, jnp.int32)
        _ctx_1024P = jax.random.normal(jax.random.fold_in(_rk, 11), (2, 16, 128), jnp.float32)
        _ctx_1024c = jax.random.dirichlet(jax.random.fold_in(_rk, 511), 0.3 * jnp.ones((16,), jnp.float32), (2, 77))
        _ctx_1024t = jnp.einsum('bsk,bkd->bsd', _ctx_1024c, _ctx_1024P)
        _ctx_1024t = _ctx_1024t * jax.lax.rsqrt(jnp.mean(jnp.square(_ctx_1024t)) + 1e-12) * 0.953939
        ctx_1024 = 0.00222621 + 0.99962 * (_ctx_1024t + 0.3 * jax.random.normal(jax.random.fold_in(_rk, 611), (2, 77, 128), jnp.float32))
        itok_BxS_0_255 = jax.random.randint(jax.random.fold_in(_rk, 12), (2, 512), 0, 32, jnp.int32)
        _g = jax.random.normal(jax.random.fold_in(_rk, 9001), (2, 2), jnp.float32)
        _g = jnp.sign(_g) * jnp.maximum(jnp.abs(_g), 1.0) + (_g == 0) * 1.0
        g_xattn = _g[0]
        g_ffn = _g[1]
        return (x, ctx_1024, itok_BxS_0_255, g_xattn, g_ffn)
    x, ctx_1024, itok_BxS_0_255, g_xattn, g_ffn = _rec_inputs()

    def _L0_xattn_setup():
        import jax, jax.numpy as jnp
        import numpy as np
        N_LAYERS = 4
        H = 16
        LOOKBACK = 128
        EPS = 1e-06
        ROPE_BASE = 10000.0
        NEG = jnp.float32(-1e+30)

        def rmsnorm(x, w):
            return x * jax.lax.rsqrt(jnp.mean(x * x, axis=-1, keepdims=True) + EPS) * w

        def rope_cache(L, hd):
            inv = 1.0 / ROPE_BASE ** (jnp.arange(0, hd, 2, dtype=jnp.float32) / hd)
            t = jnp.arange(L, dtype=jnp.float32)
            f = t[:, None] * inv[None, :]
            emb = jnp.concatenate([f, f], axis=-1)
            return (jnp.cos(emb), jnp.sin(emb))

        def apply_rope(x, cos, sin):
            d = x.shape[-1]
            x1, x2 = (x[..., :d // 2], x[..., d // 2:])
            rot = jnp.concatenate([-x2, x1], axis=-1)
            return x * cos + rot * sin

        def split_heads(x, n_heads):
            B, L, D = x.shape
            return x.reshape(B, L, n_heads, D // n_heads).transpose(0, 2, 1, 3)

        def merge_heads(x):
            B, h, L, d = x.shape
            return x.transpose(0, 2, 1, 3).reshape(B, L, h * d)

        def sdpa(q, k, v, bias):
            scale = q.shape[-1] ** (-0.5)
            s = jnp.einsum('bhqd,bhkd->bhqk', q, k) * scale + bias
            p = jax.nn.softmax(s, axis=-1)
            return jnp.einsum('bhqk,bhkd->bhqd', p, v)

        def forward(x, memory, seg_ids, Wqkv, bqkv, Wo, bo, Wq_c, Wkv_c, Wo_c, Wg, Wu, Wd, n1, n2, n3, nf):
            B, L, D = x.shape
            S = memory.shape[1]
            hd = D // H
            cos, sin = rope_cache(L, hd)
            i = jnp.arange(L)
            causal_bias = jnp.where(i[None, :] <= i[:, None], 0.0, NEG)[None, None]
            j = jnp.arange(S)
            allowed = (j[None, None, :] <= seg_ids[:, :, None]) & (j[None, None, :] > seg_ids[:, :, None] - LOOKBACK)
            cross_bias = jnp.where(allowed, 0.0, NEG)[:, None]
            for l in range(N_LAYERS):
                h = rmsnorm(x, n1[l])
                qkv = h @ Wqkv[l].T + bqkv[l]
                q, k, v = jnp.split(qkv, 3, axis=-1)
                q = apply_rope(split_heads(q, H), cos, sin)
                k = apply_rope(split_heads(k, H), cos, sin)
                v = split_heads(v, H)
                o = merge_heads(sdpa(q, k, v, causal_bias)) @ Wo[l].T + bo[l]
                x = x + o
                h2 = rmsnorm(x, n2[l])
                qc = split_heads(h2 @ Wq_c[l].T, H)
                kv = memory @ Wkv_c[l].T
                kc, vc = jnp.split(kv, 2, axis=-1)
                kc, vc = (split_heads(kc, H), split_heads(vc, H))
                oc = merge_heads(sdpa(qc, kc, vc, cross_bias)) @ Wo_c[l].T
                x = x + oc
                h3 = rmsnorm(x, n3[l])
                x = x + jax.nn.silu(h3 @ Wg[l].T) * (h3 @ Wu[l].T) @ Wd[l].T
            return rmsnorm(x, nf)
        key = jax.random.key(seed)
        ks = jax.random.split(key, 16)
        B, L, S, D, F = (2, 256, 32, 128, 512)
        w = 0.02
        inp = {'x': jax.random.normal(ks[0], (B, L, D), jnp.float32), 'memory': jax.random.normal(ks[1], (B, S, D), jnp.float32), 'seg_ids': jnp.sort(jax.random.randint(ks[2], (B, L), 0, S), axis=-1), 'Wqkv': jax.random.normal(ks[3], (N_LAYERS, 3 * D, D), jnp.float32) * w, 'bqkv': jnp.zeros((N_LAYERS, 3 * D), jnp.float32), 'Wo': jax.random.normal(ks[4], (N_LAYERS, D, D), jnp.float32) * w, 'bo': jnp.zeros((N_LAYERS, D), jnp.float32), 'Wq_c': jax.random.normal(ks[5], (N_LAYERS, D, D), jnp.float32) * w, 'Wkv_c': jax.random.normal(ks[6], (N_LAYERS, 2 * D, D), jnp.float32) * w, 'Wo_c': jax.random.normal(ks[7], (N_LAYERS, D, D), jnp.float32) * w, 'Wg': jax.random.normal(ks[8], (N_LAYERS, F, D), jnp.float32) * w, 'Wu': jax.random.normal(ks[9], (N_LAYERS, F, D), jnp.float32) * w, 'Wd': jax.random.normal(ks[10], (N_LAYERS, D, F), jnp.float32) * w, 'n1': jnp.ones((N_LAYERS, D), jnp.float32), 'n2': jnp.ones((N_LAYERS, D), jnp.float32), 'n3': jnp.ones((N_LAYERS, D), jnp.float32), 'nf': jnp.ones((D,), jnp.float32)}
        return inp
    _L0_xattn_all = _L0_xattn_setup()
    _L0_xattn_in = {k: v for k, v in _L0_xattn_all.items() if k in ('Wqkv', 'bqkv', 'Wo', 'bo', 'Wq_c', 'Wkv_c', 'Wo_c', 'Wg', 'Wu', 'Wd', 'n1', 'n2', 'n3', 'nf')}
    del _L0_xattn_all

    def _L0_ffn_setup():
        import jax, jax.numpy as jnp
        import numpy as np
        FEATURES = 128
        D_IN = 128

        def fp8_gemm_optimized(x, input_scale, kernel, kernel_scale):
            s_in = input_scale[0]
            s_k = kernel_scale[0]
            x_q = (x.astype(jnp.float32) / s_in).astype(jnp.float8_e4m3fn)
            k_q = (kernel.astype(jnp.float32) / s_k).astype(jnp.float8_e4m3fn)
            y = jnp.dot(x_q.astype(jnp.float32), k_q.astype(jnp.float32), preferred_element_type=jnp.float32)
            return y * (s_in * s_k)
        key = jax.random.key(seed)
        kx, kk, kb = jax.random.split(key, 3)
        x = jax.random.normal(kx, (4, 1024, D_IN), dtype=jnp.float32)
        limit = np.sqrt(6.0 / (D_IN + FEATURES)).astype(np.float32)
        kernel = jax.random.uniform(kk, (D_IN, FEATURES), dtype=jnp.float32, minval=-limit, maxval=limit).astype(jnp.bfloat16)
        input_scale = jnp.ones((1,), dtype=jnp.float32)
        kernel_scale = jnp.ones((1,), dtype=jnp.float32)
        bias = jnp.zeros((FEATURES,), dtype=jnp.bfloat16)
        return {'x': x, 'kernel': kernel, 'input_scale': input_scale, 'kernel_scale': kernel_scale, 'bias': bias}
    _L0_ffn_all = _L0_ffn_setup()
    _L0_ffn_in = {k: v for k, v in _L0_ffn_all.items() if k in ('kernel', 'input_scale', 'kernel_scale', 'bias')}
    del _L0_ffn_all

    def _L1_xattn_setup():
        import jax, jax.numpy as jnp
        import numpy as np
        H = 128
        B = 8
        L_CHAR = 256
        L_SUB = 128

        def _linear(x, W, b):
            return jnp.einsum('blh,oh->blo', x, W) + b

        def _interp_linear(x, out_len):
            L_in = x.shape[1]
            pos = (jnp.arange(out_len, dtype=x.dtype) + 0.5) * (L_in / out_len) - 0.5
            pos = jnp.clip(pos, 0.0, L_in - 1)
            lo = jnp.floor(pos).astype(jnp.int32)
            hi = jnp.minimum(lo + 1, L_in - 1)
            w = (pos - lo.astype(x.dtype))[None, :, None]
            return x[:, lo] * (1 - w) + x[:, hi] * w
        key = jax.random.key(seed)
        ks = jax.random.split(key, 18)
        s = 0.02
        inp = {'char_emb': jax.random.normal(ks[0], (B, L_CHAR, H), jnp.float32), 'subword_emb': jax.random.normal(ks[1], (B, L_SUB, H), jnp.float32)}
        names = ['Wq_c', 'Wk_s', 'Wv_s', 'Wq_s', 'Wk_c', 'Wv_c']
        for i, n in enumerate(names):
            inp[n] = jax.random.normal(ks[2 + 2 * i], (H, H), jnp.float32) * s
            inp['b' + n[1:]] = jax.random.normal(ks[3 + 2 * i], (H,), jnp.float32) * s
        inp['Wg'] = jax.random.normal(ks[14], (H, 2 * H), jnp.float32) * s
        inp['bg'] = jax.random.normal(ks[15], (H,), jnp.float32) * s
        return inp
    _L1_xattn_all = _L1_xattn_setup()
    _L1_xattn_in = {k: v for k, v in _L1_xattn_all.items() if k in ('Wq_c', 'bq_c', 'Wk_s', 'bk_s', 'Wv_s', 'bv_s', 'Wq_s', 'bq_s', 'Wk_c', 'bk_c', 'Wv_c', 'bv_c', 'Wg', 'bg')}
    del _L1_xattn_all

    def _L1_ffn_setup():
        import jax, jax.numpy as jnp
        import numpy as np
        B, S, D = (2, 256, 128)
        E = 4
        H = 4 * D
        key = jax.random.key(seed)
        k_x, k_r, k_wv, k_wp = jax.random.split(key, 4)
        x = jax.random.normal(k_x, (B, S, D), dtype=jnp.float32)
        w_router = jax.random.normal(k_r, (D, E), dtype=jnp.float32) * 0.02
        w_v = jax.random.normal(k_wv, (E, D, 2 * H), dtype=jnp.float32) * 0.02
        w_proj = jax.random.normal(k_wp, (E, H, D), dtype=jnp.float32) * 0.02
        return {'x': x, 'w_router': w_router, 'w_v': w_v, 'w_proj': w_proj}
    _L1_ffn_all = _L1_ffn_setup()
    _L1_ffn_in = {k: v for k, v in _L1_ffn_all.items() if k in ('w_router', 'w_v', 'w_proj')}
    del _L1_ffn_all
    return {'x': x, 'ctx_1024': ctx_1024, 'itok_BxS_0_255': itok_BxS_0_255, 'g_xattn': g_xattn, 'g_ffn': g_ffn, 'L0_xattn_Wqkv': _L0_xattn_in['Wqkv'], 'L0_xattn_bqkv': _L0_xattn_in['bqkv'], 'L0_xattn_Wo': _L0_xattn_in['Wo'], 'L0_xattn_bo': _L0_xattn_in['bo'], 'L0_xattn_Wq_c': _L0_xattn_in['Wq_c'], 'L0_xattn_Wkv_c': _L0_xattn_in['Wkv_c'], 'L0_xattn_Wo_c': _L0_xattn_in['Wo_c'], 'L0_xattn_Wg': _L0_xattn_in['Wg'], 'L0_xattn_Wu': _L0_xattn_in['Wu'], 'L0_xattn_Wd': _L0_xattn_in['Wd'], 'L0_xattn_n1': _L0_xattn_in['n1'], 'L0_xattn_n2': _L0_xattn_in['n2'], 'L0_xattn_n3': _L0_xattn_in['n3'], 'L0_xattn_nf': _L0_xattn_in['nf'], 'L0_ffn_kernel': _L0_ffn_in['kernel'], 'L0_ffn_input_scale': _L0_ffn_in['input_scale'], 'L0_ffn_kernel_scale': _L0_ffn_in['kernel_scale'], 'L0_ffn_bias': _L0_ffn_in['bias'], 'L1_xattn_Wq_c': _L1_xattn_in['Wq_c'], 'L1_xattn_bq_c': _L1_xattn_in['bq_c'], 'L1_xattn_Wk_s': _L1_xattn_in['Wk_s'], 'L1_xattn_bk_s': _L1_xattn_in['bk_s'], 'L1_xattn_Wv_s': _L1_xattn_in['Wv_s'], 'L1_xattn_bv_s': _L1_xattn_in['bv_s'], 'L1_xattn_Wq_s': _L1_xattn_in['Wq_s'], 'L1_xattn_bq_s': _L1_xattn_in['bq_s'], 'L1_xattn_Wk_c': _L1_xattn_in['Wk_c'], 'L1_xattn_bk_c': _L1_xattn_in['bk_c'], 'L1_xattn_Wv_c': _L1_xattn_in['Wv_c'], 'L1_xattn_bv_c': _L1_xattn_in['bv_c'], 'L1_xattn_Wg': _L1_xattn_in['Wg'], 'L1_xattn_bg': _L1_xattn_in['bg'], 'L1_ffn_w_router': _L1_ffn_in['w_router'], 'L1_ffn_w_v': _L1_ffn_in['w_v'], 'L1_ffn_w_proj': _L1_ffn_in['w_proj']}

def reference(x, ctx_1024, itok_BxS_0_255, g_xattn, g_ffn, L0_xattn_Wqkv, L0_xattn_bqkv, L0_xattn_Wo, L0_xattn_bo, L0_xattn_Wq_c, L0_xattn_Wkv_c, L0_xattn_Wo_c, L0_xattn_Wg, L0_xattn_Wu, L0_xattn_Wd, L0_xattn_n1, L0_xattn_n2, L0_xattn_n3, L0_xattn_nf, L0_ffn_kernel, L0_ffn_input_scale, L0_ffn_kernel_scale, L0_ffn_bias, L1_xattn_Wq_c, L1_xattn_bq_c, L1_xattn_Wk_s, L1_xattn_bk_s, L1_xattn_Wv_s, L1_xattn_bv_s, L1_xattn_Wq_s, L1_xattn_bq_s, L1_xattn_Wk_c, L1_xattn_bk_c, L1_xattn_Wv_c, L1_xattn_bv_c, L1_xattn_Wg, L1_xattn_bg, L1_ffn_w_router, L1_ffn_w_v, L1_ffn_w_proj):
    import jax
    import jax.numpy as jnp

    def _L0_xattn_ref(x, memory, seg_ids, Wqkv, bqkv, Wo, bo, Wq_c, Wkv_c, Wo_c, Wg, Wu, Wd, n1, n2, n3, nf):
        import jax, jax.numpy as jnp
        import numpy as np
        N_LAYERS = 4
        H = 16
        LOOKBACK = 128
        EPS = 1e-06
        ROPE_BASE = 10000.0
        NEG = jnp.float32(-1e+30)

        def rmsnorm(x, w):
            return x * jax.lax.rsqrt(jnp.mean(x * x, axis=-1, keepdims=True) + EPS) * w

        def rope_cache(L, hd):
            inv = 1.0 / ROPE_BASE ** (jnp.arange(0, hd, 2, dtype=jnp.float32) / hd)
            t = jnp.arange(L, dtype=jnp.float32)
            f = t[:, None] * inv[None, :]
            emb = jnp.concatenate([f, f], axis=-1)
            return (jnp.cos(emb), jnp.sin(emb))

        def apply_rope(x, cos, sin):
            d = x.shape[-1]
            x1, x2 = (x[..., :d // 2], x[..., d // 2:])
            rot = jnp.concatenate([-x2, x1], axis=-1)
            return x * cos + rot * sin

        def split_heads(x, n_heads):
            B, L, D = x.shape
            return x.reshape(B, L, n_heads, D // n_heads).transpose(0, 2, 1, 3)

        def merge_heads(x):
            B, h, L, d = x.shape
            return x.transpose(0, 2, 1, 3).reshape(B, L, h * d)

        def sdpa(q, k, v, bias):
            scale = q.shape[-1] ** (-0.5)
            s = jnp.einsum('bhqd,bhkd->bhqk', q, k) * scale + bias
            p = jax.nn.softmax(s, axis=-1)
            return jnp.einsum('bhqk,bhkd->bhqd', p, v)

        def forward(x, memory, seg_ids, Wqkv, bqkv, Wo, bo, Wq_c, Wkv_c, Wo_c, Wg, Wu, Wd, n1, n2, n3, nf):
            B, L, D = x.shape
            S = memory.shape[1]
            hd = D // H
            cos, sin = rope_cache(L, hd)
            i = jnp.arange(L)
            causal_bias = jnp.where(i[None, :] <= i[:, None], 0.0, NEG)[None, None]
            j = jnp.arange(S)
            allowed = (j[None, None, :] <= seg_ids[:, :, None]) & (j[None, None, :] > seg_ids[:, :, None] - LOOKBACK)
            cross_bias = jnp.where(allowed, 0.0, NEG)[:, None]
            for l in range(N_LAYERS):
                h = rmsnorm(x, n1[l])
                qkv = h @ Wqkv[l].T + bqkv[l]
                q, k, v = jnp.split(qkv, 3, axis=-1)
                q = apply_rope(split_heads(q, H), cos, sin)
                k = apply_rope(split_heads(k, H), cos, sin)
                v = split_heads(v, H)
                o = merge_heads(sdpa(q, k, v, causal_bias)) @ Wo[l].T + bo[l]
                x = x + o
                h2 = rmsnorm(x, n2[l])
                qc = split_heads(h2 @ Wq_c[l].T, H)
                kv = memory @ Wkv_c[l].T
                kc, vc = jnp.split(kv, 2, axis=-1)
                kc, vc = (split_heads(kc, H), split_heads(vc, H))
                oc = merge_heads(sdpa(qc, kc, vc, cross_bias)) @ Wo_c[l].T
                x = x + oc
                h3 = rmsnorm(x, n3[l])
                x = x + jax.nn.silu(h3 @ Wg[l].T) * (h3 @ Wu[l].T) @ Wd[l].T
            return rmsnorm(x, nf)
        return forward(x, memory, seg_ids, Wqkv, bqkv, Wo, bo, Wq_c, Wkv_c, Wo_c, Wg, Wu, Wd, n1, n2, n3, nf)

    def _L0_ffn_ref(x, kernel, input_scale, kernel_scale, bias):
        import jax, jax.numpy as jnp
        import numpy as np
        FEATURES = 128
        D_IN = 128

        def fp8_gemm_optimized(x, input_scale, kernel, kernel_scale):
            s_in = input_scale[0]
            s_k = kernel_scale[0]
            x_q = (x.astype(jnp.float32) / s_in).astype(jnp.float8_e4m3fn)
            k_q = (kernel.astype(jnp.float32) / s_k).astype(jnp.float8_e4m3fn)
            y = jnp.dot(x_q.astype(jnp.float32), k_q.astype(jnp.float32), preferred_element_type=jnp.float32)
            return y * (s_in * s_k)
        dtype = jnp.bfloat16
        x = x.astype(dtype)
        orig_shape = x.shape
        x2 = x.reshape(-1, x.shape[-1])
        y = fp8_gemm_optimized(x2, input_scale, kernel, kernel_scale)
        y = y.astype(dtype) + bias
        return y.reshape(orig_shape[:-1] + (FEATURES,))

    def _L1_xattn_ref(char_emb, subword_emb, Wq_c, bq_c, Wk_s, bk_s, Wv_s, bv_s, Wq_s, bq_s, Wk_c, bk_c, Wv_c, bv_c, Wg, bg):
        import jax, jax.numpy as jnp
        import numpy as np
        H = 128
        B = 8
        L_CHAR = 256
        L_SUB = 128

        def _linear(x, W, b):
            return jnp.einsum('blh,oh->blo', x, W) + b

        def _interp_linear(x, out_len):
            L_in = x.shape[1]
            pos = (jnp.arange(out_len, dtype=x.dtype) + 0.5) * (L_in / out_len) - 0.5
            pos = jnp.clip(pos, 0.0, L_in - 1)
            lo = jnp.floor(pos).astype(jnp.int32)
            hi = jnp.minimum(lo + 1, L_in - 1)
            w = (pos - lo.astype(x.dtype))[None, :, None]
            return x[:, lo] * (1 - w) + x[:, hi] * w
        h = char_emb.shape[-1]
        scale = 1.0 / jnp.sqrt(jnp.asarray(h, char_emb.dtype))
        Q_char = _linear(char_emb, Wq_c, bq_c)
        K_sub = _linear(subword_emb, Wk_s, bk_s)
        V_sub = _linear(subword_emb, Wv_s, bv_s)
        scores = jnp.einsum('bqh,bkh->bqk', Q_char, K_sub) * scale
        char2sub = jnp.einsum('bqk,bkh->bqh', jax.nn.softmax(scores, axis=-1), V_sub)
        Q_sub = _linear(subword_emb, Wq_s, bq_s)
        K_char = _linear(char_emb, Wk_c, bk_c)
        V_char = _linear(char_emb, Wv_c, bv_c)
        scores2 = jnp.einsum('bqh,bkh->bqk', Q_sub, K_char) * scale
        sub2char = jnp.einsum('bqk,bkh->bqh', jax.nn.softmax(scores2, axis=-1), V_char)
        L_char = char_emb.shape[1]
        if sub2char.shape[1] != L_char:
            sub2char = _interp_linear(sub2char, L_char)
        gate_in = jnp.concatenate([char2sub, sub2char], axis=-1)
        gate = jax.nn.sigmoid(jnp.einsum('blh,oh->blo', gate_in, Wg) + bg)
        return gate * char2sub + (1 - gate) * sub2char

    def _L1_ffn_ref(x, w_router, w_v, w_proj):
        import jax, jax.numpy as jnp
        import numpy as np
        B, S, D = (2, 256, 128)
        E = 4
        H = 4 * D
        logits = jnp.einsum('bsd,de->bse', x, w_router)
        probs = jax.nn.softmax(logits, axis=-1)
        expert_idx = jnp.argmax(probs, axis=-1)
        gv = jnp.einsum('bsd,edh->ebsh', x, w_v)
        gate_raw, value = jnp.split(gv, 2, axis=-1)
        h = gate_raw * jax.nn.sigmoid(gate_raw) * value
        y = jnp.einsum('ebsh,ehd->ebsd', h, w_proj)
        onehot = jax.nn.one_hot(expert_idx, w_v.shape[0], dtype=x.dtype)
        return jnp.einsum('bse,ebsd->bsd', onehot, y)
    x = x + jnp.tanh(g_xattn[0]) * _L0_xattn_ref(_layernorm(x, axis=-1), ctx_1024, itok_BxS_0_255, L0_xattn_Wqkv, L0_xattn_bqkv, L0_xattn_Wo, L0_xattn_bo, L0_xattn_Wq_c, L0_xattn_Wkv_c, L0_xattn_Wo_c, L0_xattn_Wg, L0_xattn_Wu, L0_xattn_Wd, L0_xattn_n1, L0_xattn_n2, L0_xattn_n3, L0_xattn_nf)
    x = x + jnp.tanh(g_ffn[0]) * _L0_ffn_ref(_layernorm(x, axis=-1), L0_ffn_kernel, L0_ffn_input_scale, L0_ffn_kernel_scale, L0_ffn_bias)
    x = x + jnp.tanh(g_xattn[1]) * _L1_xattn_ref(_layernorm(x, axis=-1), ctx_1024, L1_xattn_Wq_c, L1_xattn_bq_c, L1_xattn_Wk_s, L1_xattn_bk_s, L1_xattn_Wv_s, L1_xattn_bv_s, L1_xattn_Wq_s, L1_xattn_bq_s, L1_xattn_Wk_c, L1_xattn_bk_c, L1_xattn_Wv_c, L1_xattn_bv_c, L1_xattn_Wg, L1_xattn_bg)
    x = x + jnp.tanh(g_ffn[1]) * _L1_ffn_ref(_layernorm(x, axis=-1), L1_ffn_w_router, L1_ffn_w_v, L1_ffn_w_proj)
    return x

_drawn_inputs = setup_inputs


def setup_inputs(seed=0):
    import zlib

    import numpy as np

    out = dict(_drawn_inputs(seed))
    spreads = {'g_ffn': (-1.0, 0.6),
     'L0_xattn_bqkv': (0.0, 0.397),
     'L0_xattn_bo': (0.0, 0.1),
     'L0_xattn_n1': (1.0, 0.6),
     'L0_xattn_n2': (1.0, 0.6),
     'L0_xattn_n3': (1.0, 0.6),
     'L0_xattn_nf': (1.0, 0.2),
     'L0_ffn_bias': (0.0, 0.1)}
    factors = {'L0_xattn_Wqkv': 5.954,
     'L0_xattn_Wo': 2.7,
     'L0_xattn_Wq_c': 8.0,
     'L0_xattn_Wg': 4.369,
     'L0_xattn_Wu': 4.395,
     'L0_xattn_Wd': 4.374,
     'L1_xattn_Wq_c': 8.0,
     'L1_xattn_bq_c': 8.0,
     'L1_xattn_Wk_s': 8.0,
     'L1_xattn_bk_s': 8.0,
     'L1_xattn_bv_s': 8.0,
     'L1_xattn_Wq_s': 8.0,
     'L1_xattn_bq_s': 8.0,
     'L1_xattn_Wk_c': 8.0,
     'L1_xattn_bk_c': 8.0,
     'L1_xattn_Wv_c': 8.0,
     'L1_xattn_bv_c': 8.0,
     'L1_xattn_Wg': 8.0,
     'L1_xattn_bg': 8.0,
     'L1_ffn_w_router': 8.0,
     'L1_ffn_w_v': 8.0,
     'L1_ffn_w_proj': 8.0}
    for name, (base, spread) in spreads.items():
        noise = np.random.default_rng([zlib.crc32(name.encode()), seed]).standard_normal(out[name].shape)
        drawn = base * np.exp(spread * noise) if base else spread * noise
        out[name] = jnp.asarray(drawn.astype(out[name].dtype))
    for name, factor in factors.items():
        out[name] = (out[name] * factor).astype(out[name].dtype)
    return out
```

```python
from contextlib import ExitStack

import numpy as np
import concourse.bass as bass
from concourse import mybir

F32 = mybir.dt.float32
BF16 = mybir.dt.bfloat16
FP8 = mybir.dt.float8e4
I32 = mybir.dt.int32
ALU = mybir.AluOpType
ACT = mybir.ActivationFunctionType
AX = mybir.AxisListType

P = 128
B = 2
L = 512
NT = L // P
S = 77
H = 16
HD = P // H
HG = 4
NG = H // HG
LAYERS = 4
FC = 4
NE = 4
PARTS = 3
PP = PARTS * PARTS
KZ = 96
KM = KZ + PARTS
VW = 2 * HD
NEG = -1e30
LOOKBACK = 128
RMS_EPS = 1e-6
LN_EPS = 1e-5
SCALE = float(HD) ** -0.5
SCALE1 = float(P) ** -0.5
FP8_MAX = 240.0

V_N1, V_N2, V_N3, V_BO, V_BQ, V_BQR, V_BK, V_BKR = range(8)
NV = 8
W_Q, W_QR, W_K, W_KR, W_V = range(5)
W_O, W_QC, W_KC, W_VC = range(4)
W_OC, W_G, W_U, W_D = 0, 1, 1 + FC, 1 + 2 * FC
NW1, NW2, NW3 = 5, 4, 1 + 3 * FC
X_QC, X_KS, X_VS, X_QS, X_KC, X_VC, X_G1, X_G2 = range(8)
U_NF, U_BQC, U_BKS, U_BQS, U_BKC, U_BG = range(6)

S_UNITS = [(t, h, n) for t, n in ((0, 4), (1, 2), (2, 1), (3, 1)) for h in range(0, H, n)]
C_UNITS = [(t, h, n) for t in range(NT) for h, n in ((0, 6), (6, 5), (11, 5))]
A_SLOTS, C_SLOTS = 5, 2

STEPS = [("norm1", 0), ("norm1", 1), ("qkv", 0), ("qkv", 1), ("kvc", 0),
         ("smax", 0), ("mrow", 0), ("smax", 1), ("attn", 0), ("mrow", 1), ("attn", 1),
         ("oproj", 0), ("norm2", 0), ("qc", 0), ("oproj", 1), ("norm2", 1), ("qc", 1),
         ("csmax", 0), ("cmrow", 0), ("csmax", 1), ("cattn", 0), ("cmrow", 1), ("cattn", 1),
         ("ocproj", 0), ("norm3", 0), ("ocproj", 1), ("norm3", 1), ("ffn", 0), ("ffn", 1)]


class Ring:

    def __init__(self, slots, filled, freed, before, layer, after):
        self.slots, self.filled, self.freed = slots, filled, freed
        n = len(slots)
        assert len(before) % n == 0 and len(layer) % n == 0
        self.where = {u: (i, 0) for i, u in enumerate(before)}
        self.where.update({u: (len(before) + i, len(layer) // n) for i, u in enumerate(layer)})
        self.where.update({u: (len(before) + LAYERS * len(layer) + i, 0) for i, u in enumerate(after)})

    def at(self, u):
        return self.slots[self.where[u][0] % len(self.slots)]

    def full(self, u):
        return self.filled[self.where[u][0] % len(self.slots)]

    def free(self, u):
        return self.freed[self.where[u][0] % len(self.slots)]

    def count(self, u, l=0):
        n, per = self.where[u]
        own = n // len(self.slots) + 1
        return l * per + own if per else own

    def read(self, u, l=0):
        return self.count(u, l) + 1


def general_uses():
    before = [(s, b, 0) for s in ("mean", "var") for b in range(B)]
    layer, after = [], []
    for s, b in STEPS:
        if s in ("norm1", "norm2", "norm3", "oproj", "ocproj", "qc", "mrow", "cmrow"):
            layer.append((s, b))
        elif s == "qkv":
            layer.append(("v", b))
        elif s == "kvc":
            layer += [("kc", 0), ("vc", 0)]
        elif s == "ffn":
            layer.append(("down", b))
    after += [("nf", b) for b in range(B)]
    after += [(w, b, 1) for w in ("mean", "var") for b in range(B)] + [("dense", b) for b in range(B)]
    after += [(w, b, 2) for w in ("mean", "var") for b in range(B)]
    for b in range(B):
        after += [(w, b) for w in XATTN]
    after += [(w, b, 3) for w in ("mean", "var") for b in range(B)]
    for b in range(B):
        after += [("router", b)] + [("spread", b, e) for e in range(NE)] + [("edown", b, e) for e in range(NE)]
    return before, layer, after


XATTN = ("xqc", "xks", "xvs", "xqs", "xkc", "xvc", "s1", "s2", "p1t", "p2t", "c2s", "s2c0", "s2c", "gate")


def build(nc, d, out):
    with ExitStack() as ctx:
        def sb(name, shape, dt=F32):
            return ctx.enter_context(nc.sbuf_tensor(name, shape, dt))

        def sem(name):
            return ctx.enter_context(nc.semaphore(name))

        def sems(name, n=B):
            return [sem(f"{name}{i}") for i in range(n)]

        def ring(name, n, width, before, layer, after=()):
            slots = [ctx.enter_context(nc.psum_tensor(f"{name}{i}", [P, width], F32)) for i in range(n)]
            return Ring(slots, sems(f"{name}_filled", n), sems(f"{name}_freed", n), before, layer, after)

        G = ring("general", 1, 512, *general_uses())
        Q = ring("scores", 2, 512, [], [(s, b, i) for s, b in STEPS if s in ("smax", "csmax")
                                        for i in range(len(S_UNITS if s == "smax" else C_UNITS))])
        wide = []
        for s, b in STEPS:
            if s == "qkv":
                wide += [("rope", b, 0), ("rope", b, 1)]
            elif s == "attn":
                wide += [(s, b, g, u) for g in range(NG) for u in range(A_SLOTS)]
            elif s == "cattn":
                wide += [(s, b, g, u) for g in range(NG) for u in range(C_SLOTS)]
            elif s == "ffn":
                wide += [(s, b, c) for c in range(FC)]
        T = ring("wide", 2, 1024, [], wide, [("moe", b, c) for b in range(B) for c in range(FC)])
        O = ring("headout", 1, 512, [], [(s, b, g) for s, b in STEPS if s in ("attn", "cattn") for g in range(NG)])

        X = [sb(f"x{b}", [P, L]) for b in range(B)]
        HN = [sb(f"hn{b}", [P, L]) for b in range(B)]
        RA = [[sb(f"ra{b}{i}", [P, L]) for i in range(2)] for b in range(B)]
        RB = [[sb(f"rb{b}{i}", [P, L]) for i in range(2)] for b in range(B)]
        RS = [RA[b][0] for b in range(B)]
        PART = [[sb(f"part{b}{i}", [P, PARTS, L], BF16) for i in range(2)] for b in range(B)]
        QST = [sb(f"qstack{b}", [P, H, L], BF16) for b in range(B)]
        KST = [sb(f"kstack{b}", [P, H, L], BF16) for b in range(B)]
        KC32 = sb("kc32", [P, B * S])
        KCREST = sb("kcrest", [P, B * S])
        KCPART = sb("kcpart", [P, PARTS, B * S], BF16)
        KCST = sb("kcstack", [KM, H, B * S], BF16)
        VA = [sb(f"va{b}", [P, NT, H + 1, VW]) for b in range(B)]
        VCA = sb("vca", [S, B, H + 1, VW])
        MX = [sb(f"mx{b}", [P, NT, H]) for b in range(B)]
        MREST = [sb(f"mrest{b}", [P, NT, H]) for b in range(B)]
        MPART = [sb(f"mpart{b}", [P, NT, PARTS, H], BF16) for b in range(B)]
        MT = [sb(f"mt{b}", [PARTS * H, L], BF16) for b in range(B)]
        PR = [sb(f"prob{i}", [P, A_SLOTS, 1024]) for i in range(2)]
        OA = [sb(f"oa{b}", [P, NG, L]) for b in range(B)]
        ON = [sb(f"on{b}", [P, L]) for b in range(B)]
        OD = [sb(f"od{b}", [P, L]) for b in range(B)]
        SQR = ON
        SG = OA
        W1 = sb("w1", [P, NW1 * P])
        W2 = sb("w2", [P, NW2 * P])
        W3 = sb("w3", [P, NW3 * P])
        BV = sb("bv", [P, P])
        VEC = sb("vec", [P, LAYERS * NV])
        COS = sb("cos_t", [P, L])
        SIN = sb("sin_t", [P, L])
        IDB = sb("ident_bf", [P, P], BF16)
        IDF = sb("ident_f", [P, P])
        ONESD = sb("ones_d", [P, P])
        TRIQ = sb("tri_q", [P, P], BF16)
        TRIK = sb("tri_k", [P, P], BF16)
        CBQ = sb("cross_bias_q", [P, B * NT, S], BF16)
        CBK = sb("cross_bias_k", [S, B * L], BF16)
        SEGR = PR[1][0:S, 2, :].bitcast(I32)
        SEGC = sb("seg_cols", [P, B * NT], I32)
        SEGF = sb("seg_f", [P, 2, B * NT])
        IOTA = sb("iota", [P, S])
        KIDX = sb("kidx", [P, 2])
        CTX = sb("ctx", [P, B * S])
        EPS = sb("eps", [P, 2])
        GATES = sb("gates", [P, 4])
        TG = sb("tanh_gates", [P, 4])
        UV = sb("uvec", [P, 6])
        TILES = dict(cos=COS, sin=SIN, idb=IDB, idf=IDF, onesd=ONESD, triq=TRIQ, trik=TRIK, iota=IOTA,
                     kidx=KIDX, ctx=CTX, segc=SEGC, segr=SEGR, gates=GATES, uv=UV, vec=VEC)

        def carve(tile):
            flat = tile[:, :, :].rearrange("p h t -> p (h t)").bitcast(F32)
            at = [0]

            def take(rows, *shape, dt=F32):
                n = int(np.prod(shape)) * (4 if dt == F32 else 2 if dt == BF16 else 1) // 4
                v = flat[0:rows, at[0]:at[0] + n]
                v = v if dt == F32 else v.bitcast(dt)
                at[0] += n
                assert at[0] <= H * L // 2
                return v.rearrange("p (a c) -> p a c", a=shape[0]) if len(shape) == 2 else v
            return take
        in_q = [carve(QST[b]) for b in range(B)]
        in_k = [carve(KST[b]) for b in range(B)]
        in_x = [carve(QST[b]) for b in range(B)]
        XM = [in_q[b](P, NE, L) for b in range(B)]
        KW = in_x[1](P, P, dt=BF16)
        QBIAS = sb("qbias", [P, 1], BF16)
        XO = [in_k[1](P, L) for b in range(B)]
        XSC = sb("xscales", [P, 2])
        SC = sb("scales", [P, 3])
        QT = [in_x[0](P, L) for i in range(2)]
        Q8 = [in_x[0](P, L, dt=FP8) for i in range(2)]
        QK8 = [in_x[1](P, P, dt=FP8) for i in range(2)]
        XQ = [in_x[b](P, L, dt=BF16) for b in range(B)]
        KQ = in_x[1](P, P, dt=BF16)
        YB = [in_x[b](P, L, dt=BF16) for b in range(B)]
        HB = [in_x[b](P, L, dt=BF16) for b in range(B)]
        WX = in_k[1](P, 8 * P)
        in_x2 = [carve(QST[b]) for b in range(B)]
        INTERP = in_x2[1](S, L)
        BVS, BVC = in_x2[0](P, P), in_x2[0](P, P)
        KS1 = [in_q[b](P, S) for b in range(B)]
        QS1 = [in_q[b](P, S) for b in range(B)]
        VS1 = [in_x2[b](S, P) for b in range(B)]
        VC1 = [in_x2[b](P, NT, P) for b in range(B)]
        P1 = [in_q[b](P, NT, S) for b in range(B)]
        P1T = [in_q[b](S, L) for b in range(B)]
        P2 = [in_q[b](S, L) for b in range(B)]
        P2T = [in_q[b](P, NT, S) for b in range(B)]
        S2C0 = [in_q[b](S, P) for b in range(B)]
        ST1 = [sb(f"st1{b}", [P, 4, NT]) for b in range(B)]
        ST2 = [sb(f"st2{b}", [P, 4]) for b in range(B)]
        WR = sb("wr", [P, NE])
        WV = in_k[0](P, NE * 2 * FC * P)
        WP = in_k[1](P, NE * FC * P)
        RT = [in_q[b](P, 5 * NT * NE).rearrange("p (w t e) -> p w t e", t=NT, e=NE) for b in range(B)]
        OH = [sb(f"oh{b}", [P, NT, NE], BF16) for b in range(B)]
        ME = [PR[b][:, 0:2, :].rearrange("p a (c t) -> p (a c) t", c=2) for b in range(B)]
        

        s_const, s_init, s_mask = sem("const_loaded"), sem("buffers_set"), sem("mask_steps")
        s_w1, s_w2, s_w3, s_late = sem("w1_loaded"), sem("w2_loaded"), sem("w3_loaded"), sem("late_loaded")
        s_interp = sem("interp_loaded")
        x_ready, xo_ready = sems("x_ready"), sems("xo_ready")
        sq_ready, rs_ready, h_ready = sems("squares_ready"), sems("rstd_ready"), sems("h_ready")
        rope_ready = sems("rope_ready")
        part1, rest1, part2, part3 = (sems(n) for n in ("part1_ready", "rest1_ready", "part2_ready", "part3_ready"))
        kc_part1, kc_rest1, kc_part2, kc_part3 = (sem(n) for n in ("kcpart1", "kcrest1", "kcpart2", "kcpart3"))
        q_landed, k_landed, kc_landed = sems("q_landed"), sems("k_landed"), sem("kc_landed")
        m_split, m_landed = sems("maximum_split"), sems("maximum_landed")
        o_landed, den_step, o_ready = sems("heads_landed"), sems("denominator_step"), sems("heads_ready")
        silu_ready, hid_ready = sems("silu_ready"), sems("hidden_ready")
        ln_sq, ln_rs, ln_out = sems("ln_squares"), sems("ln_rstd"), sems("ln_out")
        tg_ready, nf_ready = sem("tanh_ready"), sems("nf_ready")
        q_step, y_step, s_kq = sem("quantise_step"), sems("dense_step"), sem("kq_ready")
        x_q = sems("xq_ready")
        st_step, p1_ready, p2_ready = sems("softmax_step"), sems("p1_ready"), sems("p2_ready")
        exp1_ready, exp2_ready = sems("exp1_ready"), sems("exp2_ready")
        gate_ready, mix_step = sems("gate_ready"), sems("mix_step")
        rt_step, xm_ready, es_ready = sems("router_step"), sems("masked_ready"), sems("expert_silu_ready")
        eh_ready, ey_step = sems("expert_hidden_ready"), sems("expert_out_step")
        s_out = sem("out_stored")

        block = ctx.enter_context(nc.Block())

        def w1(i):
            return W1[:, i * P:(i + 1) * P]

        def w2(i):
            return W2[:, i * P:(i + 1) * P]

        def w3(i):
            return W3[:, i * P:(i + 1) * P]

        def wx(i):
            return WX[:, i * P:(i + 1) * P]

        def uv(i):
            return UV[:, i:i + 1]

        def vec(l, i):
            return VEC[:, bass.ds(l * NV + i, 1)]

        def ctx_b(b):
            return CTX[:, b * S:(b + 1) * S]

        late = [(KW, "kw"), (QBIAS, "qbias"), (XSC, "xsc"), (WX, "wx"), 
                (WR, "wr"), (WV, "wv"), (WP, "wp")]
        N_CONST = 16 * (B + len(TILES))
        N_LATE = 16 * (B + len(late))

        @block.sync
        def _(sp):
            for b in range(B):
                sp.dma_start(RB[b][0][:, :], d["x"][b]).then_inc(s_const, 16)
            for name, tile in TILES.items():
                sp.dma_start(tile[:, :], d[name]).then_inc(s_const, 16)
            sp.dma_start(W1[:, :], d["w1"][0]).then_inc(s_w1, 16)
            sp.dma_start(BV[:, :], d["bv"][0]).then_inc(s_w1, 16)
            sp.wait_ge(s_init, 9)

            def restack(part, stack, query, landed, ready, n):
                for i in range(PARTS):
                    sp.wait_ge(ready[i], n)
                    for j in range(PARTS):
                        r = (PARTS * i + j if query else PARTS * j + i) * HD
                        sp.dma_start(stack[r:r + HD, :, :], part[:, i, :]).then_inc(landed, 16)

            with sp.Fori(0, LAYERS) as l:
                for s, b in STEPS:
                    parts_ready = (part1[b], part2[b], part3[b])
                    if s == "qkv":
                        restack(PART[b][0], QST[b], True, q_landed[b], parts_ready, 3 * l + 1)
                        restack(PART[b][1], KST[b], False, k_landed[b], parts_ready, 3 * l + 2)
                        if b == 0:
                            sp.dma_start(W2[:, :], d["w2"][bass.ds(l, 1)]).then_inc(s_w2, 16)
                        else:
                            sp.dma_start(W3[:, :], d["w3"][bass.ds(l, 1)]).then_inc(s_w3, 16)
                    elif s == "kvc":
                        restack(KCPART, KCST, False, kc_landed, (kc_part1, kc_part2, kc_part3), l + 1)
                        sp.wait_ge(G.free(("v", 1)), G.read(("v", 1), l))
                        sp.dma_start(W1[:, :], d["w1"][bass.ds(l + 1, 1)]).then_inc(s_w1, 16)
                        sp.dma_start(BV[:, :], d["bv"][bass.ds(l + 1, 1)]).then_inc(s_w1, 16)
                    elif s in ("mrow", "cmrow"):
                        sp.wait_ge(G.free((s, b)), G.read((s, b), l))
                        sp.dma_start(QST[b][KZ:KM, :, :], MT[b][:, :]).then_inc(m_landed[b], 16)
                    elif s in ("attn", "cattn"):
                        sp.wait_ge(O.free((s, b, NG - 1)), O.read((s, b, NG - 1), l))
                        for j in range(HG):
                            for tile, r in ((ON, 32 * j), (OD, 32 * j + HD)):
                                sp.dma_start(tile[b][32 * j:32 * j + 32, :],
                                             OA[b][r:r + HD, :, :]).then_inc(o_landed[b], 16)
                    elif s == "qc":
                        restack(PART[b][0], QST[b], True, q_landed[b], parts_ready, 3 * l + 3)
            for b in range(B):
                sp.dma_start(XO[b], d["x"][b]).then_inc(s_late, 16)
            for tile, name in late:
                sp.dma_start(tile[:, :], d[name]).then_inc(s_late, 16)
            for b in range(B):
                sp.wait_ge(xo_ready[b], 2)
            for tile, name in ((BVS, "bvs"), (BVC, "bvc"), (INTERP, "interp")):
                sp.dma_start(tile, d[name]).then_inc(s_interp, 16)
            for b in range(B):
                sp.wait_ge(xo_ready[b], 4)
                sp.dma_start(out[b], XO[b][:, :]).then_inc(s_out, 16)
            sp.wait_ge(s_out, 16 * B)
            sp.wait_ge(s_w1, 32 * (LAYERS + 1))

        @block.tensor
        def _(pe):
            for r in (G, Q, T, O):
                for k in r.freed:
                    pe.sem_inc(k, 1)
            pe.wait_ge(s_const, N_CONST)

            def general(u, l, lhsT, rhs, width=512):
                pe.wait_ge(G.free(u), G.count(u, l))
                pe.matmul(G.at(u)[0:lhsT.shape[1], 0:width], lhsT, rhs, start=True, stop=True)\
                  .then_inc(G.full(u), 1)

            def layer_norm(b, n, src, ready, value):
                pe.wait_ge(ready, value)
                general(("mean", b, n), 0, ONESD[:, :], src[:, :])

            def layer_var(b, n):
                pe.wait_ge(ln_sq[b], n + 1)
                general(("var", b, n), 0, ONESD[:, :], SQR[b][:, :])

            for b in range(B):
                layer_norm(b, 0, RB[b][0], s_const, N_CONST)
            for b in range(B):
                layer_var(b, 0)
            pe.wait_ge(s_init, 9)
            pe.wait_ge(s_mask, 7)

            def norm(u, b, l, n):
                pe.wait_ge(sq_ready[b], 3 * l + n)
                general(u, l, ONESD[:, :], SQR[b][:, :])

            def qkv(b, l):
                pe.wait_ge(h_ready[b], 3 * l + 1)
                pe.wait_ge(s_w1, 32 * (l + 1))
                for i, w in enumerate((W_Q, W_K)):
                    u = ("rope", b, i)
                    pe.wait_ge(T.free(u), T.count(u, l))
                    pe.matmul(T.at(u)[:, 0:512], w1(w), HN[b][:, :], start=True, stop=True)
                    pe.matmul(T.at(u)[:, 512:1024], w1(w + 1), HN[b][:, :], start=True, stop=True)\
                      .then_inc(T.full(u), 1)
                u = ("v", b)
                pe.wait_ge(G.free(u), G.count(u, l))
                for t in range(NT):
                    mm = pe.matmul(G.at(u)[:, t * P:(t + 1) * P], HN[b][:, t * P:(t + 1) * P], w1(W_V),
                                   start=True, stop=True)
                mm.then_inc(G.full(u), 1)

            def kvc(l):
                pe.wait_ge(s_w2, 16 * (l + 1))
                general(("kc", 0), l, w2(W_KC), CTX[:, :], B * S)
                u = ("vc", 0)
                pe.wait_ge(G.free(u), G.count(u, l))
                for b in range(B):
                    mm = pe.matmul(G.at(u)[0:S, b * P:(b + 1) * P], ctx_b(b), w2(W_VC), start=True, stop=True)
                mm.then_inc(G.full(u), 1)

            def smax(b, l):
                pe.wait_ge(q_landed[b], 16 * PP * (2 * l + 1))
                pe.wait_ge(k_landed[b], 16 * PP * (l + 1))
                for i, (t, h0, n) in enumerate(S_UNITS):
                    u = ("smax", b, i)
                    keys = (t + 1) * P
                    pe.wait_ge(Q.free(u), Q.count(u, l))
                    for k in range(n):
                        o = k * keys
                        pe.matmul(Q.at(u)[:, o:o + keys], QST[b][0:KZ, h0 + k, t * P:(t + 1) * P],
                                  KST[b][0:KZ, h0 + k, 0:keys], start=True, stop=False)
                        mm = pe.matmul(Q.at(u)[:, o + keys - P:o + keys], IDB[:, :], TRIQ[:, :],
                                       start=False, stop=True)
                    mm.then_inc(Q.full(u), 1)

            def csmax(b, l):
                pe.wait_ge(q_landed[b], 16 * PP * (2 * l + 2))
                pe.wait_ge(kc_landed, 16 * PP * (l + 1))
                for i, (t, h0, n) in enumerate(C_UNITS):
                    u = ("csmax", b, i)
                    pe.wait_ge(Q.free(u), Q.count(u, l))
                    for k in range(n):
                        pe.matmul(Q.at(u)[:, k * S:(k + 1) * S], QST[b][0:KZ, h0 + k, t * P:(t + 1) * P],
                                  KCST[0:KZ, h0 + k, b * S:(b + 1) * S], start=(k == 0), stop=False,
                                  skip_group_check=True)
                    pe.matmul(Q.at(u)[:, 0:n * S].rearrange("p (h k) -> p h k", k=S), IDB[:, :],
                              CBQ[:, b * NT + t:b * NT + t + 1, :].broadcast_to([P, n, S]),
                              start=False, stop=True, skip_group_check=True).then_inc(Q.full(u), 1)

            def mrow(u, b, l, n):
                pe.wait_ge(m_split[b], 8 * l + 4 * n)
                pe.wait_ge(G.free(u), G.count(u, l))
                for t in range(NT):
                    mm = pe.matmul(G.at(u)[0:PARTS * H, t * P:(t + 1) * P],
                                   MPART[b][:, t, :, :].rearrange("p a h -> p (a h)"), IDB[:, :],
                                   start=True, stop=True)
                mm.then_inc(G.full(u), 1)

            def self_scores(b, l, g):
                def product(bank, h, kt, mm=None):
                    pe.matmul(bank[:, 0:L - kt * P], KST[b][0:KM, h, kt * P:(kt + 1) * P],
                              QST[b][0:KM, h, kt * P:L], start=True, stop=False)
                    return pe.matmul(bank[:, 0:P], IDB[:, :], TRIK[:, :], start=False, stop=True)

                for v in range(A_SLOTS):
                    u = ("attn", b, g, v)
                    slot = T.at(u)
                    pe.wait_ge(T.free(u), T.count(u, l))
                    for j in range(2) if v < 4 else range(4):
                        h = HG * g + (2 * (v % 2) + j if v < 4 else j)
                        if v < 2:
                            mm = product(slot[:, j * 512:(j + 1) * 512], h, 0)
                        elif v < 4:
                            product(slot[:, j * 512:j * 512 + 384], h, 1)
                            mm = product(slot[:, j * 512 + 384:(j + 1) * 512], h, 3)
                        else:
                            mm = product(slot[:, j * 256:(j + 1) * 256], h, 2)
                    mm.then_inc(T.full(u), 1)

            def cross_scores(b, l, g):
                for v in range(C_SLOTS):
                    u = ("cattn", b, g, v)
                    pe.wait_ge(T.free(u), T.count(u, l))
                    for j in range(2):
                        bank = T.at(u)[0:S, j * 512:(j + 1) * 512]
                        h = HG * g + 2 * v + j
                        pe.matmul(bank, KCST[0:KM, h, b * S:(b + 1) * S], QST[b][0:KM, h, :],
                                  start=True, stop=False)
                        mm = pe.matmul(bank, IDB[0:S, 0:S], CBK[:, b * L:(b + 1) * L], start=False, stop=True)
                    mm.then_inc(T.full(u), 1)

            def where(j, kt):
                if kt == 0:
                    return j // 2, (j % 2) * 512
                if kt == 2:
                    return 4, j * 256
                return 2 + j // 2, (j % 2) * 512 + (0 if kt == 1 else 384)

            def value_products(s, b, l, g):
                u = (s, b, g)
                slots = A_SLOTS if s == "attn" else C_SLOTS
                probs = PR[g % 2]
                for v in range(max(0, slots - 2), slots):
                    w = (s, b, g, v)
                    pe.wait_ge(T.free(w), T.read(w, l))
                pe.wait_ge(O.free(u), O.count(u, l))
                for kt in range(NT if s == "attn" else 1):
                    for j in range(HG):
                        h = HG * g + j
                        if s == "attn":
                            v, c = where(j, kt)
                            mm = pe.matmul(O.at(u)[32 * j:32 * j + 32, kt * P:L],
                                           VA[b][:, kt, h:h + 2, :].rearrange("p h c -> p (h c)"),
                                           probs[:, v, c:c + L - kt * P], start=(kt == 0), stop=(kt == NT - 1))
                        else:
                            mm = pe.matmul(O.at(u)[32 * j:32 * j + 32, :],
                                           VCA[:, b, h:h + 2, :].rearrange("p h c -> p (h c)"),
                                           probs[0:S, j // 2, (j % 2) * 512:(j % 2 + 1) * 512],
                                           start=True, stop=True)
                mm.then_inc(O.full(u), 1)

            def attention(s, b, l):
                pe.wait_ge(m_landed[b], 16 * (2 * l + (1 if s == "attn" else 2)))
                for g in range(NG):
                    (self_scores if s == "attn" else cross_scores)(b, l, g)
                    if g == 0:
                        v = ("v", b) if s == "attn" else ("vc", 0)
                        pe.wait_ge(G.free(v), G.read(v, l))
                    else:
                        value_products(s, b, l, g - 1)
                value_products(s, b, l, NG - 1)

            def project(u, b, l, w, n):
                pe.wait_ge(o_ready[b], 2 * l + n)
                general(u, l, w, ON[b][:, :])

            def ffn(b, l):
                pe.wait_ge(h_ready[b], 3 * l + 3)
                for c in range(FC):
                    u = ("ffn", b, c)
                    pe.wait_ge(T.free(u), T.count(u, l))
                    pe.matmul(T.at(u)[:, 0:512], w3(W_G + c), HN[b][:, :], start=True, stop=True)
                    pe.matmul(T.at(u)[:, 512:1024], w3(W_U + c), HN[b][:, :], start=True, stop=True)\
                      .then_inc(T.full(u), 1)
                u = ("down", b)
                pe.wait_ge(G.free(u), G.count(u, l))
                for c in range(FC):
                    pe.wait_ge(T.free(("ffn", b, c)), T.read(("ffn", b, c), l))
                    mm = pe.matmul(G.at(u)[:, :], w3(W_D + c), SG[b][:, c, :], start=(c == 0), stop=(c == FC - 1))
                mm.then_inc(G.full(u), 1)

            with pe.Fori(0, LAYERS) as l:
                for s, b in STEPS:
                    if s in ("norm1", "norm2", "norm3"):
                        norm((s, b), b, l, int(s[-1]))
                    elif s == "qkv":
                        qkv(b, l)
                    elif s == "kvc":
                        kvc(l)
                    elif s == "smax":
                        smax(b, l)
                    elif s == "csmax":
                        csmax(b, l)
                    elif s in ("mrow", "cmrow"):
                        mrow((s, b), b, l, 1 if s == "mrow" else 2)
                    elif s in ("attn", "cattn"):
                        attention(s, b, l)
                    elif s == "oproj":
                        project((s, b), b, l, w2(W_O), 1)
                    elif s == "qc":
                        pe.wait_ge(h_ready[b], 3 * l + 2)
                        general((s, b), l, w2(W_QC), HN[b][:, :])
                    elif s == "ocproj":
                        if b == 0:
                            pe.wait_ge(s_w3, 16 * (l + 1))
                        project((s, b), b, l, w3(W_OC), 2)
                    elif s == "ffn":
                        ffn(b, l)

            for b in range(B):
                pe.wait_ge(sq_ready[b], 3 * LAYERS + 1)
                general(("nf", b), 0, ONESD[:, :], SQR[b][:, :])
            for b in range(B):
                layer_norm(b, 1, XO[b], xo_ready[b], 1)
            for b in range(B):
                layer_var(b, 1)
            pe.wait_ge(s_kq, 1)
            for b in range(B):
                pe.wait_ge(x_q[b], 1)
                general(("dense", b), 0, KQ[:, :], XQ[b][:, :])
            for b in range(B):
                layer_norm(b, 2, XO[b], xo_ready[b], 2)
            for b in range(B):
                layer_var(b, 2)
            for b in range(B):
                qct, kct = RA[b][1], RB[b][1]
                pe.wait_ge(ln_out[b], 2)
                general(("xqc", b), 0, wx(X_QC), HN[b][:, :])
                general(("xks", b), 0, wx(X_KS), ctx_b(b), S)
                general(("xvs", b), 0, ctx_b(b), wx(X_VS), P)
                general(("xqs", b), 0, wx(X_QS), ctx_b(b), S)
                general(("xkc", b), 0, wx(X_KC), HN[b][:, :])
                u = ("xvc", b)
                pe.wait_ge(G.free(u), G.count(u))
                for t in range(NT):
                    mm = pe.matmul(G.at(u)[:, t * P:(t + 1) * P], HN[b][:, t * P:(t + 1) * P], wx(X_VC),
                                   start=True, stop=True)
                mm.then_inc(G.full(u), 1)
                u = ("s1", b)
                pe.wait_ge(G.free(u), G.count(u))
                for t in range(NT):
                    mm = pe.matmul(G.at(u)[:, t * S:(t + 1) * S], qct[:, t * P:(t + 1) * P], KS1[b][:, :],
                                   start=True, stop=True)
                mm.then_inc(G.full(u), 1)
                general(("s2", b), 0, QS1[b][:, :], kct[:, :])
                u = ("p1t", b)
                pe.wait_ge(p1_ready[b], 1)
                pe.wait_ge(G.free(u), G.count(u))
                for t in range(NT):
                    mm = pe.transpose(G.at(u)[0:S, t * P:(t + 1) * P], P1[b][:, t, :], IDF[:, :])
                mm.then_inc(G.full(u), 1)
                u = ("p2t", b)
                pe.wait_ge(p2_ready[b], 1)
                pe.wait_ge(G.free(u), G.count(u))
                for t in range(NT):
                    mm = pe.transpose(G.at(u)[:, t * S:(t + 1) * S], P2[b][:, t * P:(t + 1) * P], IDF[0:S, 0:S])
                mm.then_inc(G.full(u), 1)
                general(("c2s", b), 0, VS1[b][:, :], P1T[b][:, :])
                u = ("s2c0", b)
                pe.wait_ge(G.free(u), G.count(u))
                for t in range(NT):
                    mm = pe.matmul(G.at(u)[0:S, 0:P], P2T[b][:, t, :], VC1[b][:, t, :],
                                   start=(t == 0), stop=(t == NT - 1))
                mm.then_inc(G.full(u), 1)
                pe.wait_ge(G.free(u), G.read(u))
                pe.wait_ge(s_interp, 48)
                general(("s2c", b), 0, S2C0[b][:, :], INTERP[:, :])
                u = ("gate", b)
                pe.wait_ge(G.free(u), G.count(u))
                pe.matmul(G.at(u)[:, :], wx(X_G1), RA[b][0][:, :], start=True, stop=False)
                pe.matmul(G.at(u)[:, :], wx(X_G2), RB[b][0][:, :], start=False, stop=True).then_inc(G.full(u), 1)
            for b in range(B):
                layer_norm(b, 3, XO[b], xo_ready[b], 3)
            for b in range(B):
                layer_var(b, 3)
            for b in range(B):
                u = ("router", b)
                pe.wait_ge(ln_out[b], 3)
                pe.wait_ge(G.free(u), G.count(u))
                for t in range(NT):
                    mm = pe.matmul(G.at(u)[:, t * NE:(t + 1) * NE], HN[b][:, t * P:(t + 1) * P], WR[:, :],
                                   start=True, stop=True)
                mm.then_inc(G.full(u), 1)
                pe.wait_ge(rt_step[b], 9)
                for e in range(NE):
                    u = ("spread", b, e)
                    pe.wait_ge(G.free(u), G.count(u))
                    for t in range(NT):
                        mm = pe.matmul(G.at(u)[:, t * P:(t + 1) * P],
                                       OH[b][:, t, e:e + 1].broadcast_to([P, P]), IDB[:, :], start=True, stop=True)
                    mm.then_inc(G.full(u), 1)
                pe.wait_ge(xm_ready[b], NE)
                for c in range(FC):
                    u = ("moe", b, c)
                    pe.wait_ge(T.free(u), T.count(u))
                    for half in range(2):
                        for e in range(NE):
                            o = (e * 2 * FC + half * FC + c) * P
                            mm = pe.matmul(T.at(u)[:, half * 512:(half + 1) * 512], WV[:, o:o + P],
                                           XM[b][:, e, :], start=(e == 0), stop=(e == NE - 1))
                    mm.then_inc(T.full(u), 1)
                for c in range(FC):
                    pe.wait_ge(T.free(("moe", b, c)), T.read(("moe", b, c)))
                for e in range(NE):
                    u = ("edown", b, e)
                    pe.wait_ge(G.free(u), G.count(u))
                    for c in range(FC):
                        o = (e * FC + c) * P
                        mm = pe.matmul(G.at(u)[:, :], WP[:, o:o + P], SG[b][:, c, :],
                                       start=(c == 0), stop=(c == FC - 1))
                    mm.then_inc(G.full(u), 1)

        @block.scalar
        def _(act):
            act.wait_ge(s_const, N_CONST)
            act.wait_ge(s_init, 9)
            nc.scalar.activation(TG[:, :], GATES[:, :], ACT.Tanh).then_inc(tg_ready, 1)

            def root(u, b, l, eps, ready, before):
                act.wait_ge(G.full(u), G.count(u, l))
                nc.scalar.activation(RS[b][:, :], G.at(u)[:, :], ACT.Ln, bias=EPS[:, eps:eps + 1])\
                    .then_inc(G.free(u), 1)
                act.wait_ge(G.free(u), G.read(u, l))
                nc.scalar.activation(RS[b][:, :], RS[b][:, :], ACT.Exp, scale=-0.5).then_inc(ready, 1)

            def copy(u, l, dst, rows=P, width=512, view=None):
                act.wait_ge(G.full(u), G.count(u, l))
                src = view(G.at(u)) if view else G.at(u)[0:rows, 0:width]
                nc.scalar.activation(dst, src, ACT.Copy).then_inc(G.free(u), 1)

            def exponentials(s, b, l):
                slots = A_SLOTS if s == "attn" else C_SLOTS
                rows = P if s == "attn" else S
                for g in range(NG):
                    if g >= 2:
                        act.wait_ge(O.full((s, b, g - 2)), O.count((s, b, g - 2), l))
                    for v in range(slots):
                        u = (s, b, g, v)
                        act.wait_ge(T.full(u), T.count(u, l))
                        nc.scalar.activation(PR[g % 2][0:rows, v, :], T.at(u)[0:rows, :], ACT.Exp, scale=SCALE)\
                            .then_inc(T.free(u), 1)

            def denominators(b, l, n):
                act.wait_ge(o_landed[b], 16 * 2 * HG * (2 * l + n))
                nc.scalar.activation(OD[b][:, :], OD[b][:, :], ACT.Ln).then_inc(den_step[b], 1)
                act.wait_ge(den_step[b], 4 * l + 2 * n - 1)
                nc.scalar.activation(OD[b][:, :], OD[b][:, :], ACT.Exp, scale=-1.0).then_inc(den_step[b], 1)

            for b in range(B):
                root(("var", b, 0), b, 0, 1, ln_rs[b], 0)
            with act.Fori(0, LAYERS) as l:
                for s, b in STEPS:
                    if s in ("norm1", "norm2", "norm3"):
                        root((s, b), b, l, 0, rs_ready[b], 0)
                    elif s == "kvc":
                        copy(("kc", 0), l, KC32[:, :], P, B * S)
                        copy(("vc", 0), l, VCA[:, :, 0:H, 0:HD],
                             view=lambda bank: bank[0:S, 0:B * P].rearrange("p (b h d) -> p b h d", b=B, h=H))
                    elif s in ("mrow", "cmrow"):
                        copy((s, b), l, MT[b][:, :], PARTS * H, L)
                    elif s in ("attn", "cattn"):
                        exponentials(s, b, l)
                    elif s == "oproj":
                        denominators(b, l, 1)
                    elif s == "ocproj":
                        denominators(b, l, 2)
                    elif s == "qc":
                        copy((s, b), l, RA[b][0][:, :])
                    elif s == "ffn":
                        for c in range(FC):
                            u = (s, b, c)
                            act.wait_ge(T.full(u), T.count(u, l))
                            nc.scalar.activation(SG[b][:, c, :], T.at(u)[:, 0:512], ACT.Silu)\
                                .then_inc(silu_ready[b], 1)
            for b in range(B):
                root(("nf", b), b, 0, 0, rs_ready[b], 0)
            for b in range(B):
                root(("var", b, 1), b, 0, 1, ln_rs[b], 0)
            for b in range(B):
                root(("var", b, 2), b, 0, 1, ln_rs[b], 0)
            for b in range(B):
                def biased(u, dst, bias, width):
                    act.wait_ge(G.full(u), G.count(u))
                    nc.scalar.activation(dst, G.at(u)[:, 0:width], ACT.Identity, bias=uv(bias))\
                        .then_inc(G.free(u), 1)

                biased(("xqc", b), RA[b][1][:, :], U_BQC, L)
                biased(("xks", b), KS1[b][:, :], U_BKS, S)
                biased(("xqs", b), QS1[b][:, :], U_BQS, S)
                biased(("xkc", b), RB[b][1][:, :], U_BKC, L)
                act.wait_ge(st_step[b], 1)
                for t in range(NT):
                    ins = nc.scalar.activation(P1[b][:, t, :], G.at(("s1", b))[:, t * S:(t + 1) * S], ACT.Exp,
                                               scale=SCALE1, bias=ST1[b][:, 1, t:t + 1],
                                               accum_out=ST1[b][:, 2, t:t + 1])
                    ins.then_inc(exp1_ready[b], 1)
                act.wait_ge(st_step[b], 3)
                nc.scalar.activation(P2[b][:, :], G.at(("s2", b))[0:S, :], ACT.Exp, scale=SCALE1,
                                     bias=ST2[b][0:S, 1:2], accum_out=ST2[b][0:S, 2:3]).then_inc(exp2_ready[b], 1)
                copy(("p1t", b), 0, P1T[b][:, :], S, L)
                copy(("p2t", b), 0, P2T[b][:, :, :],
                     view=lambda bank: bank[:, 0:NT * S].rearrange("p (t k) -> p t k", t=NT))
                copy(("c2s", b), 0, RA[b][0][:, :])
                copy(("s2c0", b), 0, S2C0[b][:, :], S, P)
                copy(("s2c", b), 0, RB[b][0][:, :])
                u = ("gate", b)
                act.wait_ge(G.full(u), G.count(u))
                nc.scalar.activation(ON[b][:, :], G.at(u)[:, :], ACT.Sigmoid, bias=uv(U_BG))\
                    .then_inc(G.free(u), 1)
            for b in range(B):
                root(("var", b, 3), b, 0, 1, ln_rs[b], 0)
            for b in range(B):
                for e in range(NE):
                    copy(("spread", b, e), 0, ME[b][:, e, :])
                for c in range(FC):
                    u = ("moe", b, c)
                    act.wait_ge(T.full(u), T.count(u))
                    nc.scalar.activation(SG[b][:, c, :], T.at(u)[:, 0:512], ACT.Silu).then_inc(es_ready[b], 1)

        @block.gpsimd
        def _(pool):
            for b in range(B):
                pool.memset(QST[b][64:KZ, :, :], 0.0).then_inc(s_init, 1)
                pool.memset(KST[b][64:KZ, :, :], 0.0).then_inc(s_init, 1)
            pool.memset(KCST[64:KZ, :, :], 0.0).then_inc(s_init, 1)
            pool.wait_ge(s_init, 9)

            def tt(out_, a, b_, op, done):
                nc.gpsimd.tensor_tensor(out_, a, b_, op).then_inc(done, 1)

            def centred(b, n):
                u = ("mean", b, n)
                pool.wait_ge(G.free(u), G.read(u))
                tt(SQR[b][:, :], OD[b][:, :], OD[b][:, :], ALU.mult, ln_sq[b])

            for b in range(B):
                centred(b, 0)

            def split(b, i, l, n):
                pool.wait_ge(part1[b], 3 * l + n)
                tt(RB[b][i][:, :], RA[b][i][:, :], PART[b][i][:, 0, :], ALU.subtract, rest1[b])
                pool.wait_ge(part2[b], 3 * l + n)
                pool.wait_ge(rest1[b], 3 * l + n)
                tt(PART[b][i][:, 2, :], RB[b][i][:, :], PART[b][i][:, 1, :], ALU.subtract, part3[b])

            with pool.Fori(0, LAYERS) as l:
                for s, b in STEPS:
                    if s in ("norm1", "norm2", "norm3"):
                        pool.wait_ge(x_ready[b], 3 * l + int(s[-1]))
                        tt(SQR[b][:, :], X[b][:, :], X[b][:, :], ALU.mult, sq_ready[b])
                    elif s == "qkv":
                        for i in range(2):
                            u = ("rope", b, i)
                            pool.wait_ge(T.free(u), T.read(u, l))
                            tt(RA[b][i][:, :], RA[b][i][:, :], RB[b][i][:, :], ALU.add, rope_ready[b])
                        for i in range(2):
                            split(b, i, l, i + 1)
                    elif s == "kvc":
                        pool.wait_ge(kc_part1, l + 1)
                        tt(KCREST[:, :], KC32[:, :], KCPART[:, 0, :], ALU.subtract, kc_rest1)
                        pool.wait_ge(kc_part2, l + 1)
                        pool.wait_ge(kc_rest1, l + 1)
                        tt(KCPART[:, 2, :], KCREST[:, :], KCPART[:, 1, :], ALU.subtract, kc_part3)
                    elif s == "qc":
                        split(b, 0, l, 3)
            for b in range(B):
                pool.wait_ge(x_ready[b], 3 * LAYERS + 1)
                tt(SQR[b][:, :], X[b][:, :], X[b][:, :], ALU.mult, sq_ready[b])
            for n in (1, 2):
                for b in range(B):
                    centred(b, n)
            for b in range(B):
                pool.wait_ge(mix_step[b], 1)
                tt(OD[b][:, :], OD[b][:, :], ON[b][:, :], ALU.mult, gate_ready[b])
            for b in range(B):
                centred(b, 3)
            for b in range(B):
                for e in range(NE):
                    u = ("spread", b, e)
                    pool.wait_ge(G.free(u), G.read(u))
                    tt(XM[b][:, e, :], HN[b][:, :], ME[b][:, e, :], ALU.mult, xm_ready[b])

        @block.vector
        def _(dve):
            v = nc.vector
            for b in range(B):
                v.memset(KST[b][KZ:KM, :, :], 1.0)
                v.memset(VA[b][:, :, 0:H, HD:VW], 1.0)
                v.memset(VA[b][:, :, H, :], 0.0)
            v.memset(KCST[KZ:KM, :, :], 1.0)
            v.memset(VCA[:, :, 0:H, HD:VW], 1.0)
            v.memset(VCA[:, :, H, :], 0.0)
            v.memset(EPS[:, 0:1], RMS_EPS).then_inc(s_init, 1)
            v.memset(EPS[:, 1:2], LN_EPS).then_inc(s_init, 1)
            v.memset(ST2[0][:, :], 0.0).then_inc(s_init, 1)
            v.memset(ST2[1][:, :], 0.0).then_inc(s_init, 1)
            dve.wait_ge(s_const, N_CONST)

            def centre(b, n, src):
                u = ("mean", b, n)
                dve.wait_ge(G.full(u), G.count(u))
                v.tensor_tensor(OD[b][:, :], src[:, :], G.at(u)[:, :], ALU.subtract).then_inc(G.free(u), 1)

            def normed(b, n, dst, done):
                dve.wait_ge(ln_rs[b], n + 1)
                v.tensor_tensor(dst[:, :], OD[b][:, :], RS[b][:, :], ALU.mult).then_inc(done, 1)

            for b in range(B):
                centre(b, 0, RB[b][0])
            allow = PR[0][0:S, 0, :]
            allow2 = PR[0][0:S, 1, :]
            v.tensor_scalar(allow, SEGR[:, :], KIDX[0:S, 0:1], None, ALU.is_ge).then_inc(s_mask, 1)
            v.tensor_scalar(SEGF[:, 0, :], SEGC[:, :], 1.0, None, ALU.mult).then_inc(s_mask, 1)
            dve.wait_ge(s_mask, 1)
            v.scalar_tensor_tensor(out=allow2, in0=SEGR[:, :], scalar=KIDX[0:S, 1:2], in1=allow,
                                   op0=ALU.is_lt, op1=ALU.mult).then_inc(s_mask, 1)
            dve.wait_ge(s_mask, 3)
            v.tensor_scalar(CBK[:, :], allow2, -1.0, -NEG, ALU.add, ALU.mult).then_inc(s_mask, 1)
            tiles = B * NT
            qa = PR[1][:, 0, 0:tiles * S].rearrange("p (t k) -> p t k", t=tiles)
            qb = PR[1][:, 1, 0:tiles * S].rearrange("p (t k) -> p t k", t=tiles)
            seg = SEGF[:, 0, :].rearrange("p (t o) -> p t o", o=1).broadcast_to([P, tiles, S])
            idx = IOTA[:, :].rearrange("p (o k) -> p o k", o=1).broadcast_to([P, tiles, S])
            v.tensor_tensor(qa, idx, seg, ALU.is_le).then_inc(s_mask, 1)
            dve.wait_ge(s_mask, 5)
            v.tensor_tensor(qb, seg, idx, ALU.subtract).then_inc(s_mask, 1)
            dve.wait_ge(s_mask, 6)
            v.scalar_tensor_tensor(out=qb, in0=qb, scalar=float(LOOKBACK), in1=qa,
                                   op0=ALU.is_lt, op1=ALU.mult).then_inc(s_mask, 1)
            dve.wait_ge(s_mask, 7)
            v.tensor_scalar(CBQ[:, :, :], qb, -1.0, -NEG, ALU.add, ALU.mult).then_inc(s_mask, 1)
            for b in range(B):
                normed(b, 0, X[b], x_ready[b])

            def normed_rms(b, l, n, col):
                dve.wait_ge(rs_ready[b], 3 * l + n)
                v.scalar_tensor_tensor(out=HN[b][:, :], in0=X[b][:, :], scalar=col, in1=RS[b][:, :],
                                       op0=ALU.mult, op1=ALU.mult).then_inc(h_ready[b], 1)

            def split(b, i, l, n, ready, value):
                dve.wait_ge(ready, value)
                v.tensor_copy(PART[b][i][:, 0, :], RA[b][i][:, :]).then_inc(part1[b], 1)

            def split2(b, i, l, n):
                dve.wait_ge(rest1[b], 3 * l + n)
                v.tensor_copy(PART[b][i][:, 1, :], RB[b][i][:, :]).then_inc(part2[b], 1)

            def qkv(b, l):
                for i, (c0, c1) in enumerate(((V_BQ, V_BQR), (V_BK, V_BKR))):
                    u = ("rope", b, i)
                    dve.wait_ge(T.full(u), T.count(u, l))
                    v.scalar_tensor_tensor(out=RA[b][i][:, :], in0=T.at(u)[:, 0:512], scalar=vec(l, c0),
                                           in1=COS[:, :], op0=ALU.add, op1=ALU.mult)
                    v.scalar_tensor_tensor(out=RB[b][i][:, :], in0=T.at(u)[:, 512:1024], scalar=vec(l, c1),
                                           in1=SIN[:, :], op0=ALU.add, op1=ALU.mult).then_inc(T.free(u), 1)
                u = ("v", b)
                dve.wait_ge(G.full(u), G.count(u, l))
                for t in range(NT):
                    ins = v.tensor_tensor(VA[b][:, t, 0:H, 0:HD],
                                          G.at(u)[:, t * P:(t + 1) * P].rearrange("p (h d) -> p h d", h=H),
                                          BV[:, :].rearrange("p (h d) -> p h d", h=H), ALU.add)
                ins.then_inc(G.free(u), 1)
                for i in range(2):
                    split(b, i, l, i + 1, rope_ready[b], 2 * l + i + 1)
                for i in range(2):
                    split2(b, i, l, i + 1)

            def maxima(s, b, l, units, width):
                for i, (t, h0, n) in enumerate(units):
                    u = (s, b, i)
                    k = width or (t + 1) * P
                    dve.wait_ge(Q.full(u), Q.count(u, l))
                    v.tensor_reduce(MX[b][:, t, h0:h0 + n],
                                    Q.at(u)[:, 0:n * k].rearrange("p (h k) -> p h k", k=k),
                                    AX.X, ALU.max).then_inc(Q.free(u), 1)

            def split_maxima(s, b, l, n):
                units = len(S_UNITS if s == "mrow" else C_UNITS)
                for i in (units - 2, units - 1):
                    u = ("smax" if s == "mrow" else "csmax", b, i)
                    dve.wait_ge(Q.free(u), Q.read(u, l))
                base = 8 * l + 4 * n - 4
                v.tensor_scalar(MPART[b][:, :, 0, :], MX[b][:, :, :], -1.0, None, ALU.mult).then_inc(m_split[b], 1)
                dve.wait_ge(m_split[b], base + 1)
                v.scalar_tensor_tensor(out=MREST[b][:, :, :], in0=MX[b][:, :, :], scalar=-1.0,
                                       in1=MPART[b][:, :, 0, :], op0=ALU.mult, op1=ALU.subtract)\
                    .then_inc(m_split[b], 1)
                dve.wait_ge(m_split[b], base + 2)
                v.tensor_copy(MPART[b][:, :, 1, :], MREST[b][:, :, :]).then_inc(m_split[b], 1)
                dve.wait_ge(m_split[b], base + 3)
                v.tensor_tensor(MPART[b][:, :, 2, :], MREST[b][:, :, :], MPART[b][:, :, 1, :], ALU.subtract)\
                    .then_inc(m_split[b], 1)

            def copy_out(s, b, l):
                for g in range(NG):
                    u = (s, b, g)
                    dve.wait_ge(O.full(u), O.count(u, l))
                    v.tensor_copy(OA[b][:, g, :], O.at(u)[:, :]).then_inc(O.free(u), 1)

            def normalise(b, l, n):
                dve.wait_ge(den_step[b], 4 * l + 2 * n)
                v.tensor_tensor(ON[b][:, :], ON[b][:, :], OD[b][:, :], ALU.mult).then_inc(o_ready[b], 1)

            with dve.Fori(0, LAYERS) as l:
                for s, b in STEPS:
                    if s in ("norm1", "norm2", "norm3"):
                        n = int(s[-1])
                        normed_rms(b, l, n, vec(l, (V_N1, V_N2, V_N3)[n - 1]))
                    elif s == "qkv":
                        qkv(b, l)
                    elif s == "kvc":
                        u = ("kc", 0)
                        dve.wait_ge(G.free(u), G.read(u, l))
                        v.tensor_copy(KCPART[:, 0, :], KC32[:, :]).then_inc(kc_part1, 1)
                        dve.wait_ge(kc_rest1, l + 1)
                        v.tensor_copy(KCPART[:, 1, :], KCREST[:, :]).then_inc(kc_part2, 1)
                    elif s == "smax":
                        maxima(s, b, l, S_UNITS, None)
                    elif s == "csmax":
                        maxima(s, b, l, C_UNITS, S)
                    elif s in ("mrow", "cmrow"):
                        split_maxima(s, b, l, 1 if s == "mrow" else 2)
                    elif s in ("attn", "cattn"):
                        copy_out(s, b, l)
                    elif s == "oproj":
                        normalise(b, l, 1)
                        dve.wait_ge(G.full((s, b)), G.count((s, b), l))
                        v.scalar_tensor_tensor(out=X[b][:, :], in0=G.at((s, b))[:, :], scalar=vec(l, V_BO),
                                               in1=X[b][:, :], op0=ALU.add, op1=ALU.add).then_inc(G.free((s, b)), 1)
                        dve.wait_ge(G.free((s, b)), G.read((s, b), l))
                        dve.sem_inc(x_ready[b], 1)
                    elif s == "ocproj":
                        normalise(b, l, 2)
                        dve.wait_ge(G.full((s, b)), G.count((s, b), l))
                        v.tensor_tensor(X[b][:, :], X[b][:, :], G.at((s, b))[:, :], ALU.add)\
                            .then_inc(G.free((s, b)), 1)
                        dve.wait_ge(G.free((s, b)), G.read((s, b), l))
                        dve.sem_inc(x_ready[b], 1)
                    elif s == "qc":
                        split(b, 0, l, 3, G.free((s, b)), G.read((s, b), l))
                        split2(b, 0, l, 3)
                    elif s == "ffn":
                        for c in range(FC):
                            dve.wait_ge(silu_ready[b], FC * l + c + 1)
                            u = (s, b, c)
                            v.tensor_tensor(SG[b][:, c, :], SG[b][:, c, :], T.at(u)[:, 512:1024], ALU.mult)\
                                .then_inc(T.free(u), 1)
                        u = ("down", b)
                        dve.wait_ge(G.full(u), G.count(u, l))
                        v.tensor_tensor(X[b][:, :], X[b][:, :], G.at(u)[:, :], ALU.add).then_inc(G.free(u), 1)
                        dve.wait_ge(G.free(u), G.read(u, l))
                        dve.sem_inc(x_ready[b], 1)

            dve.wait_ge(tg_ready, 1)
            dve.wait_ge(s_late, N_LATE)
            for b in range(B):
                normed_rms(b, LAYERS, 1, uv(U_NF))
                dve.wait_ge(h_ready[b], 3 * LAYERS + 1)
                v.scalar_tensor_tensor(out=XO[b][:, :], in0=HN[b][:, :], scalar=TG[:, 0:1], in1=XO[b][:, :],
                                       op0=ALU.mult, op1=ALU.add).then_inc(xo_ready[b], 1)

            dve.wait_ge(s_late, N_LATE)
            qs = [0]

            def step(ins):
                ins.then_inc(q_step, 1)
                qs[0] += 1
                dve.wait_ge(q_step, qs[0])

            step(v.reciprocal(SC[:, 0:2], XSC[:, :]))
            step(v.tensor_tensor(SC[:, 2:3], XSC[:, 0:1], XSC[:, 1:2], ALU.mult))

            def quantise(dst, src, scale, width, q8, done):
                a, m = QT[0][:, 0:width], QT[1][:, 0:width]
                lo, hi = q8[0][:, 0:width], q8[1][:, 0:width]
                step(v.tensor_scalar(a, src, scale, None, ALU.mult))
                step(v.tensor_scalar(hi, a, 0.5, None, ALU.mult, saturate=False))
                step(v.tensor_scalar(m, a, -1.0, None, ALU.mult))
                step(v.tensor_tensor(m, a, m, ALU.max))
                step(v.tensor_scalar(m, m, FP8_MAX, None, ALU.is_gt))
                step(v.tensor_scalar(a, a, FP8_MAX, -FP8_MAX, ALU.min, ALU.max))
                step(v.tensor_copy(lo, a, saturate=False))
                step(v.scalar_tensor_tensor(out=a, in0=hi, scalar=2.0, in1=lo, op0=ALU.mult, op1=ALU.subtract))
                step(v.tensor_tensor(a, a, m, ALU.mult))
                ins = v.tensor_tensor(dst, a, lo, ALU.add)
                ins.then_inc(done, 1)
                dve.wait_ge(done, 1)

            quantise(KQ[:, :], KW[:, :], SC[:, 1:2], P, QK8, s_kq)
            for b in range(B):
                centre(b, 1, XO[b])
            for b in range(B):
                normed(b, 1, HB[b], ln_out[b])
                dve.wait_ge(ln_out[b], 1)
                quantise(XQ[b][:, :], HB[b][:, :], SC[:, 0:1], L, Q8, x_q[b])
            for b in range(B):
                u = ("dense", b)
                dve.wait_ge(G.full(u), G.count(u))
                v.tensor_scalar(YB[b][:, :], G.at(u)[:, :], SC[:, 2:3], None, ALU.mult).then_inc(G.free(u), 1)
                dve.wait_ge(G.free(u), G.read(u))
                v.tensor_scalar(YB[b][:, :], YB[b][:, :], QBIAS[:, 0:1], None, ALU.add).then_inc(y_step[b], 1)
                dve.wait_ge(y_step[b], 1)
                v.scalar_tensor_tensor(out=XO[b][:, :], in0=YB[b][:, :], scalar=TG[:, 2:3], in1=XO[b][:, :],
                                       op0=ALU.mult, op1=ALU.add).then_inc(xo_ready[b], 1)

            dve.wait_ge(s_interp, 48)
            for b in range(B):
                centre(b, 2, XO[b])
            for b in range(B):
                normed(b, 2, HN[b], ln_out[b])
            for b in range(B):
                u = ("xvs", b)
                dve.wait_ge(G.full(u), G.count(u))
                v.tensor_tensor(VS1[b][:, :], G.at(u)[0:S, 0:P], BVS[0:S, :], ALU.add).then_inc(G.free(u), 1)
                u = ("xvc", b)
                dve.wait_ge(G.full(u), G.count(u))
                for t in range(NT):
                    ins = v.tensor_tensor(VC1[b][:, t, :], G.at(u)[:, t * P:(t + 1) * P], BVC[:, :], ALU.add)
                ins.then_inc(G.free(u), 1)
                u = ("s1", b)
                dve.wait_ge(G.full(u), G.count(u))
                v.tensor_reduce(ST1[b][:, 0, :], G.at(u)[:, 0:NT * S].rearrange("p (t k) -> p t k", t=NT),
                                AX.X, ALU.max).then_inc(y_step[b], 1)
                dve.wait_ge(y_step[b], 2)
                v.tensor_scalar(ST1[b][:, 1, :], ST1[b][:, 0, :], -SCALE1, None, ALU.mult).then_inc(st_step[b], 1)
                dve.wait_ge(exp1_ready[b], NT)
                v.reciprocal(ST1[b][:, 3, :], ST1[b][:, 2, :]).then_inc(G.free(u), 1)
                dve.wait_ge(G.free(u), G.read(u))
                v.tensor_tensor(P1[b][:, :, :], P1[b][:, :, :],
                                ST1[b][:, 3, :].rearrange("p (t o) -> p t o", o=1).broadcast_to([P, NT, S]),
                                ALU.mult).then_inc(p1_ready[b], 1)
                u = ("s2", b)
                dve.wait_ge(G.full(u), G.count(u))
                v.tensor_reduce(ST2[b][0:S, 0:1], G.at(u)[0:S, :], AX.X, ALU.max).then_inc(st_step[b], 1)
                dve.wait_ge(st_step[b], 2)
                v.tensor_scalar(ST2[b][0:S, 1:2], ST2[b][0:S, 0:1], -SCALE1, None, ALU.mult).then_inc(st_step[b], 1)
                dve.wait_ge(exp2_ready[b], 1)
                v.reciprocal(ST2[b][0:S, 3:4], ST2[b][0:S, 2:3]).then_inc(G.free(u), 1)
                dve.wait_ge(G.free(u), G.read(u))
                v.tensor_scalar(P2[b][:, :], P2[b][:, :], ST2[b][0:S, 3:4], None, ALU.mult).then_inc(p2_ready[b], 1)
                u = ("s2c", b)
                dve.wait_ge(G.free(u), G.read(u))
                v.tensor_tensor(OD[b][:, :], RA[b][0][:, :], RB[b][0][:, :], ALU.subtract)\
                    .then_inc(y_step[b], 1)
                u = ("gate", b)
                dve.wait_ge(G.free(u), G.read(u))
                dve.wait_ge(y_step[b], 3)
                dve.sem_inc(mix_step[b], 1)
                dve.wait_ge(gate_ready[b], 1)
                v.tensor_tensor(HN[b][:, :], OD[b][:, :], RB[b][0][:, :], ALU.add).then_inc(y_step[b], 1)
                dve.wait_ge(y_step[b], 4)
                v.scalar_tensor_tensor(out=XO[b][:, :], in0=HN[b][:, :], scalar=TG[:, 1:2], in1=XO[b][:, :],
                                       op0=ALU.mult, op1=ALU.add).then_inc(xo_ready[b], 1)

            for b in range(B):
                centre(b, 3, XO[b])
            for b in range(B):
                normed(b, 3, HN[b], ln_out[b])
            for b in range(B):
                rt = RT[b]
                n = [0]

                def rstep(ins):
                    ins.then_inc(rt_step[b], 1)
                    n[0] += 1
                    dve.wait_ge(rt_step[b], n[0])

                u = ("router", b)
                dve.wait_ge(G.full(u), G.count(u))
                logits = rt[:, 0, :, :]
                v.tensor_copy(logits, G.at(u)[:, 0:NT * NE].rearrange("p (t e) -> p t e", e=NE))\
                    .then_inc(G.free(u), 1)
                dve.wait_ge(G.free(u), G.read(u))
                top = rt[:, 1, :, 0:1]
                rstep(v.tensor_reduce(top, logits, AX.X, ALU.max))
                eq = rt[:, 2, :, :]
                rstep(v.tensor_tensor(eq, logits, top.broadcast_to([P, NT, NE]), ALU.is_ge))
                left, pick = rt[:, 3, :, :], rt[:, 4, :, :]
                rstep(v.tensor_scalar(left[:, :, 0:1], eq[:, :, 0:1], -1.0, 1.0, ALU.mult, ALU.add))
                for e in range(1, NE):
                    rstep(v.tensor_tensor(pick[:, :, e:e + 1], eq[:, :, e:e + 1], left[:, :, e - 1:e], ALU.mult))
                    if e < NE - 1:
                        rstep(v.tensor_tensor(left[:, :, e:e + 1], left[:, :, e - 1:e], pick[:, :, e:e + 1],
                                              ALU.subtract))
                v.tensor_copy(OH[b][:, :, 0:1], eq[:, :, 0:1])
                rstep(v.tensor_copy(OH[b][:, :, 1:NE], pick[:, :, 1:NE]))
                for c in range(FC):
                    dve.wait_ge(es_ready[b], c + 1)
                    u = ("moe", b, c)
                    v.tensor_tensor(SG[b][:, c, :], SG[b][:, c, :], T.at(u)[:, 512:1024], ALU.mult)\
                        .then_inc(T.free(u), 1)
                acc, tmp = ON[b], OD[b]
                for e in range(NE):
                    u = ("edown", b, e)
                    dve.wait_ge(G.full(u), G.count(u))
                    v.tensor_tensor((tmp if e else acc)[:, :], ME[b][:, e, :], G.at(u)[:, :], ALU.mult)\
                        .then_inc(G.free(u), 1)
                    if e:
                        dve.wait_ge(G.free(u), G.read(u))
                        v.tensor_tensor(acc[:, :], acc[:, :], tmp[:, :], ALU.add).then_inc(ey_step[b], 1)
                        dve.wait_ge(ey_step[b], e)
                v.scalar_tensor_tensor(out=XO[b][:, :], in0=acc[:, :], scalar=TG[:, 3:4], in1=XO[b][:, :],
                                       op0=ALU.mult, op1=ALU.add).then_inc(xo_ready[b], 1)


def constants(BF):
    inv = (1.0 / 10000.0 ** (np.arange(0, HD, 2, dtype=np.float32) / np.float32(HD))).astype(np.float32)
    angle = np.arange(L, dtype=np.float32)[:, None] * inv[None, :]
    cos = np.cos(np.concatenate([angle, angle], 1)).astype(np.float32)
    sin = np.sin(np.concatenate([-angle, angle], 1)).astype(np.float32)
    bf = BF
    q = np.arange(P)
    pos = np.clip((np.arange(L, dtype=np.float32) + np.float32(0.5)) * np.float32(S / L) - np.float32(0.5),
                  0.0, S - 1).astype(np.float32)
    lo = np.floor(pos).astype(np.int32)
    hi = np.minimum(lo + 1, S - 1)
    w = (pos - lo.astype(np.float32)).astype(np.float32)
    interp = np.zeros((S, L), np.float32)
    np.add.at(interp, (lo, np.arange(L)), np.float32(1) - w)
    np.add.at(interp, (hi, np.arange(L)), w)
    return dict(
        cos=np.ascontiguousarray(np.repeat(cos.T, H, 0)),
        sin=np.ascontiguousarray(np.repeat(sin.T, H, 0)),
        idb=np.eye(P, dtype=bf), idf=np.eye(P, dtype=np.float32),
        onesd=np.full((P, P), 1.0 / P, np.float32),
        triq=np.where(q[None, :] <= q[:, None], 0.0, NEG).astype(bf),
        trik=np.where(q[:, None] <= q[None, :], 0.0, NEG).astype(bf),
        iota=np.broadcast_to(np.arange(S, dtype=np.float32), (P, S)).copy(),
        kidx=np.stack([q, q + LOOKBACK], 1).astype(np.float32),
        interp=interp,
    )


def kernel(**inputs):
    import numpy as _np
    import concourse.bacc as _bacc
    from concourse import mybir as _mybir
    from concourse.bass_utils import run_bass_kernel_spmd as _run

    a = {k: _np.asarray(x) for k, x in inputs.items()}
    d_h = _np.arange(P).reshape(H, HD).T.reshape(-1)
    rot = (_np.arange(HD) + HD // 2) % HD
    d_h_rot = _np.arange(P).reshape(H, HD)[:, rot].T.reshape(-1)
    out_rows = _np.arange(P).reshape(NG, HG, HD).transpose(1, 2, 0).reshape(-1)

    def cat(blocks):
        return _np.ascontiguousarray(_np.concatenate(blocks, 1))

    wqkv, bqkv = a["L0_xattn_Wqkv"], a["L0_xattn_bqkv"]
    w1, w2, w3, bv, vec = [], [], [], [], []
    for l in range(LAYERS):
        wq, wk, wv = wqkv[l, :P], wqkv[l, P:2 * P], wqkv[l, 2 * P:]
        bq, bk = bqkv[l, :P], bqkv[l, P:2 * P]
        w1.append(cat([wq[d_h].T, wq[d_h_rot].T, wk[d_h].T, wk[d_h_rot].T, wv.T]))
        bv.append(_np.broadcast_to(bqkv[l, 2 * P:], (P, P)).copy())
        wkv = a["L0_xattn_Wkv_c"][l]
        w2.append(cat([a["L0_xattn_Wo"][l][:, out_rows].T, a["L0_xattn_Wq_c"][l][d_h].T,
                       wkv[:P][d_h].T, wkv[P:].T]))
        w3.append(cat([a["L0_xattn_Wo_c"][l][:, out_rows].T, a["L0_xattn_Wg"][l].T, a["L0_xattn_Wu"][l].T]
                      + [a["L0_xattn_Wd"][l][:, c * P:(c + 1) * P].T for c in range(FC)]))
        vec += [a["L0_xattn_n1"][l], a["L0_xattn_n2"][l], a["L0_xattn_n3"][l], a["L0_xattn_bo"][l],
                bq[d_h], bq[d_h_rot], bk[d_h], bk[d_h_rot]]
    w1.append(w1[0])
    bv.append(bv[0])
    seg = a["itok_BxS_0_255"].reshape(-1)
    wg = a["L1_xattn_Wg"]
    wvx, wp = a["L1_ffn_w_v"], a["L1_ffn_w_proj"]
    arrays = dict(
        x=_np.ascontiguousarray(a["x"].transpose(0, 2, 1)),
        ctx=_np.ascontiguousarray(a["ctx_1024"].reshape(B * S, P).T),
        segr=_np.ascontiguousarray(_np.broadcast_to(seg, (S, B * L))),
        segc=_np.ascontiguousarray(seg.reshape(B * NT, P).T),
        gates=_np.broadcast_to(_np.concatenate([a["g_xattn"], a["g_ffn"]]), (P, 4)).copy(),
        w1=_np.stack(w1), w2=_np.stack(w2), w3=_np.stack(w3), bv=_np.stack(bv),
        vec=_np.ascontiguousarray(_np.stack(vec, 1)),
        uv=_np.stack([a["L0_xattn_nf"], a["L1_xattn_bq_c"], a["L1_xattn_bk_s"],
                      a["L1_xattn_bq_s"], a["L1_xattn_bk_c"], a["L1_xattn_bg"]], 1),
        qbias=_np.ascontiguousarray(a["L0_ffn_bias"].reshape(P, 1)),
        kw=_np.ascontiguousarray(a["L0_ffn_kernel"]),
        xsc=_np.broadcast_to(_np.concatenate([a["L0_ffn_input_scale"], a["L0_ffn_kernel_scale"]]), (P, 2)).copy(),
        wx=cat([a["L1_xattn_" + n].T for n in ("Wq_c", "Wk_s", "Wv_s", "Wq_s", "Wk_c", "Wv_c")]
               + [wg[:, :P].T, wg[:, P:].T]),
        bvs=_np.broadcast_to(a["L1_xattn_bv_s"], (P, P)).copy(),
        bvc=_np.broadcast_to(a["L1_xattn_bv_c"], (P, P)).copy(),
        wr=_np.ascontiguousarray(a["L1_ffn_w_router"]),
        wv=_np.ascontiguousarray(wvx.transpose(1, 0, 2).reshape(P, -1)),
        wp=_np.ascontiguousarray(wp.reshape(NE, FC, P, P).transpose(2, 0, 1, 3).reshape(P, -1)),
        **constants(a["L0_ffn_kernel"].dtype))
    nc = _bacc.Bacc("TRN2", target_bir_lowering=False, num_devices=1)
    d = {}
    for name, arr in arrays.items():
        d[name] = nc.dram_tensor(f"in_{name}", arr.shape, _mybir.dt.from_np(arr.dtype), kind="ExternalInput").ap()
    out = nc.dram_tensor("out_t", (B, P, L), _mybir.dt.float32, kind="ExternalOutput").ap()
    build(nc, d, out)
    r = _run(nc, [{f"in_{k}": x for k, x in arrays.items()}], core_ids=[0])
    return _np.ascontiguousarray(r.results[0]["out_t"].transpose(0, 2, 1))
```

```python
from contextlib import ExitStack

import numpy as np
import concourse.bass as bass
from concourse import mybir

F32 = mybir.dt.float32
BF16 = mybir.dt.bfloat16
FP8 = mybir.dt.float8e4
I32 = mybir.dt.int32
ALU = mybir.AluOpType
ACT = mybir.ActivationFunctionType
AX = mybir.AxisListType

P = 128
B = 2
L = 512
NT = L // P
S = 77
H = 16
HD = P // H
HG = 4
NG = H // HG
LAYERS = 4
FC = 4
NE = 4
PARTS = 3
PRODUCTS = [(0, 0), (0, 1), (0, 2), (1, 0), (1, 1), (2, 0)]
PP = len(PRODUCTS)
KZ = 96
KM = KZ + PARTS
VW = 2 * HD
NEG = -1e30
LOOKBACK = 128
RMS_EPS = 1e-6
LN_EPS = 1e-5
SCALE = float(HD) ** -0.5
SCALE1 = float(P) ** -0.5
FP8_MAX = 240.0

V_N1, V_N2, V_N3, V_BO, V_BQ, V_BQR, V_BK, V_BKR = range(8)
NV = 8
W_Q, W_QR, W_K, W_KR, W_V = range(5)
W_O, W_QC, W_KC, W_VC = range(4)
W_OC, W_G, W_U, W_D = 0, 1, 1 + FC, 1 + 2 * FC
NW1, NW2, NW3 = 5, 4, 1 + 3 * FC
X_QC, X_KS, X_VS, X_QS, X_KC, X_VC, X_G1, X_G2 = range(8)
U_NF, U_BQC, U_BKS, U_BQS, U_BKC, U_BG = range(6)

S_UNITS = [(t, h, n) for t, n in ((0, 4), (1, 2), (2, 1), (3, 1)) for h in range(0, H, n)]
C_UNITS = [(t, h, n) for t in range(NT) for h, n in ((0, 6), (6, 5), (11, 5))]
A_SLOTS, C_SLOTS = 5, 2

PERIOD = 148.0
BEHIND = 37.0


def chain(b):
    c = [(0.0, "norm", 1), (3.5, "rope", 0), (4.5, "rope", 1), (5.5, "vals"),
         (6.0, "high", 0), (7.0, "high", 1), (8.0, "low", 0), (9.0, "low", 1)]
    c += [(19.0 + 0.6 * i, "smax", i) for i in range(len(S_UNITS))]
    c += [(46.5, "mrow", 1)]
    for g in range(NG):
        c += [(51.0 + 1.15 * (A_SLOTS * g + v), "scores", g, v) for v in range(A_SLOTS)]
        c += [(51.0 + 1.15 * (A_SLOTS * (g + 1) + (2 if g < NG - 1 else 0)) + 0.3, "values", g)]
    c += [(84.0, "heads", 1), (86.5, "oproj"), (88.0, "norm", 2), (91.5, "qc"), (92.5, "high", 2), (93.5, "low", 2)]
    c += [(101.0 + 0.6 * i, "csmax", i) for i in range(len(C_UNITS))]
    c += [(109.0, "mrow", 2)]
    for g in range(NG):
        c += [(113.0 + 1.2 * (C_SLOTS * g + v), "cscores", g, v) for v in range(C_SLOTS)]
        c += [(113.0 + 1.2 * (C_SLOTS * (g + 1) + (1 if g < NG - 1 else 0)) + 0.3, "cvalues", g)]
    c += [(131.0, "heads", 2), (133.0, "ocproj"), (134.5, "norm", 3)]
    c += [(138.0 + 1.8 * i, "ffn", i) for i in range(FC)] + [(145.6, "down")]
    if b == 0:
        c += [(70.0, "kvc"), (71.5, "kchigh"), (72.5, "kclow")]
    else:
        c += [(6.5, "w1"), (92.5, "w2"), (146.5, "w3")]
    return [(t, (n[0], b) + tuple(n[1:])) for t, *n in c]


LATER = {("pe", "norm"): 1.3, ("act", "norm"): 1.8, ("dve", "norm"): 2.5, ("dve", "rope"): 0.3,
         ("pool", "rope"): 1.5, ("dve", "vals"): 0.3, ("pe", "mrow"): 1.0, ("act", "mrow"): 1.5,
         ("sp", "mrow"): 1.5, ("act", "scores"): 0.5, ("act", "cscores"): 0.5, ("dve", "values"): 0.8,
         ("sp", "values"): 1.0, ("dve", "cvalues"): 0.8, ("sp", "cvalues"): 1.0, ("dve", "heads"): 1.2,
         ("dve", "oproj"): 0.8, ("dve", "ocproj"): 0.8, ("dve", "smax"): 0.3, ("dve", "csmax"): 0.3,
         ("act", "qc"): 0.5, ("pool", "high"): 0.3, ("pool", "low"): 0.3, ("sp", "high"): 0.5,
         ("sp", "low"): 0.5, ("act", "ffn"): 0.5, ("dve", "ffn"): 1.0, ("dve", "down"): 0.8}


def order(engine):
    at = []
    for b in range(B):
        for t, piece in chain(b):
            t += BEHIND * b + LATER.get((engine, piece[0]), 0.0)
            laps = int(t // PERIOD)
            assert laps in (0, 1)
            at.append((t - laps * PERIOD, laps, piece))
    return [(piece, laps) for _, laps, piece in sorted(at, key=lambda x: x[0])]


def uses_of(piece):
    n, b = piece[:2]
    if n in ("norm", "mrow"):
        return [("G", piece, "act")]
    if n in ("oproj", "ocproj", "down", "vals"):
        return [("G", piece, "dve")]
    if n == "qc":
        return [("G", piece, "act")]
    if n == "kvc":
        return [("G", ("kc", 0), "act"), ("G", ("vc", 0), "act")]
    if n in ("rope", "ffn"):
        return [("T", piece, "dve")]
    if n in ("scores", "cscores"):
        return [("T", piece, "act")]
    if n in ("smax", "csmax"):
        return [("Q", piece, "dve")]
    if n in ("values", "cvalues"):
        return [("O", piece, "dve")]
    return []


class Ring:

    def __init__(self, name, slots, filled, freed, before=(), after=()):
        self.slots, self.filled, self.freed = slots, filled, freed
        turn = [(u, laps) for piece, laps in order("pe") for k, u, _ in uses_of(piece) if k == name]
        self.before = {u: i for i, u in enumerate(before)}
        self.turn = {u: (i, laps) for i, (u, laps) in enumerate(turn)}
        self.size = len(turn)
        last = [u for u, laps in turn if laps]
        self.last = {u: i for i, u in enumerate(last)}
        self.after = {u: i for i, u in enumerate(after)}
        assert len(before) % len(slots) == 0 and self.size % len(slots) == 0

    def number(self, u, layer=0):
        n = len(self.before)
        if u in self.before:
            return self.before[u]
        if u in self.after:
            return n + LAYERS * self.size + len(self.last) + self.after[u]
        i, laps = self.turn[u]
        if isinstance(layer, int) and layer + laps == LAYERS:
            return n + LAYERS * self.size + self.last[u]
        return layer, n + laps * self.size + i

    def slot(self, u, layer=0):
        n = self.number(u, layer)
        return (n if isinstance(n, int) else n[1]) % len(self.slots)

    def at(self, u, layer=0):
        return self.slots[self.slot(u, layer)]

    def full(self, u, layer=0):
        return self.filled[self.slot(u, layer)]

    def free(self, u, layer=0):
        return self.freed[self.slot(u, layer)]

    def count(self, u, layer=0, more=1):
        n = self.number(u, layer)
        if isinstance(n, int):
            return n // len(self.slots) + more
        return n[0] * (self.size // len(self.slots)) + (n[1] // len(self.slots) + more)

    def read(self, u, layer=0):
        return self.count(u, layer, 2)


def general_after():
    after = [("nf", b) for b in range(B)]
    after += [(w, b, 1) for w in ("mean", "var") for b in range(B)] + [("dense", b) for b in range(B)]
    after += [(w, b, 2) for w in ("mean", "var") for b in range(B)]
    for b in range(B):
        after += [(w, b) for w in XATTN]
    after += [(w, b, 3) for w in ("mean", "var") for b in range(B)]
    for b in range(B):
        after += [("router", b)] + [("spread", b, e) for e in range(NE)] + [("edown", b, e) for e in range(NE)]
    return after


class Exponentials:

    def __init__(self, n):
        self.n = n
        self.turn = [(piece, laps) for piece, laps in order("pe") if piece[0] in ("scores", "cscores")]
        self.where = {piece: i for i, (piece, _) in enumerate(self.turn)}
        self.last = [piece for piece, laps in self.turn if laps]
        assert len(self.turn) % n == 0

    def position(self, piece, layer):
        i = self.where[piece]
        if isinstance(layer, int) and layer + self.turn[i][1] == LAYERS:
            return self.last.index(piece)
        return i

    def buffer(self, piece, layer):
        return self.position(piece, layer) % self.n

    def before(self, piece, layer):
        i = self.position(piece, layer) - self.n
        turn = layer + self.turn[self.where[piece]][1]
        if i < 0:
            i, turn = i + len(self.turn), turn - 1
        elif isinstance(turn, int) and turn == LAYERS:
            i = self.where[self.last[i]]
        if isinstance(turn, int) and turn < 0:
            return None
        former, laps = self.turn[i]
        return (former[0].replace("scores", "values"), former[1], former[2]), turn - laps


XATTN = ("xqc", "xks", "xvs", "xqs", "xkc", "xvc", "s1", "s2", "p1t", "p2t", "c2s", "s2c0", "s2c", "gate")


def build(nc, d, out):
    with ExitStack() as ctx:
        def sb(name, shape, dt=F32):
            return ctx.enter_context(nc.sbuf_tensor(name, shape, dt))

        def sem(name):
            return ctx.enter_context(nc.semaphore(name))

        def sems(name, n=B):
            return [sem(f"{name}{i}") for i in range(n)]

        def ring(key, name, n, width, before=(), after=()):
            slots = [ctx.enter_context(nc.psum_tensor(f"{name}{i}", [P, width], F32)) for i in range(n)]
            return Ring(key, slots, sems(f"{name}_filled", n), sems(f"{name}_freed", n), before, after)

        G = ring("G", "general", 1, 512, [(w, b, 0) for w in ("mean", "var") for b in range(B)], general_after())
        Q = ring("Q", "maxscores", 2, 512)
        T = ring("T", "wide", 2, 1024, (), [("moe", b, c) for b in range(B) for c in range(FC)])
        O = ring("O", "headout", 1, 512)
        RINGS = dict(G=G, Q=Q, T=T, O=O)
        E = Exponentials(8)

        X = [sb(f"x{b}", [P, L]) for b in range(B)]
        HN = [sb(f"hn{b}", [P, L]) for b in range(B)]
        RA = [[sb(f"ra{b}{i}", [P, L]) for i in range(2)] for b in range(B)]
        RB = [[sb(f"rb{b}{i}", [P, L]) for i in range(2)] for b in range(B)]
        RS = [RA[b][0] for b in range(B)]
        PART = [[sb(f"part{b}{i}", [P, PARTS, L], BF16) for i in range(2)] for b in range(B)]
        QST = [sb(f"qstack{b}", [P, H, L], BF16) for b in range(B)]
        KST = [sb(f"kstack{b}", [P, H, L], BF16) for b in range(B)]
        KC32 = sb("kc32", [P, B * S])
        KCREST = sb("kcrest", [P, B * S])
        KCPART = sb("kcpart", [P, PARTS, B * S], BF16)
        KCST = sb("kcstack", [KM, H, B * S], BF16)
        VA = [sb(f"va{b}", [P, NT, H + 1, VW]) for b in range(B)]
        VCA = sb("vca", [S, B, H + 1, VW])
        MX = [sb(f"mx{b}", [P, NT, H]) for b in range(B)]
        MREST = [sb(f"mrest{b}", [P, NT, H]) for b in range(B)]
        MPART = [sb(f"mpart{b}", [P, NT, PARTS, H], BF16) for b in range(B)]
        MT = [sb(f"mt{b}", [PARTS * H, L], BF16) for b in range(B)]
        PR = sb("prob", [P, E.n, 1024])
        OA = [sb(f"oa{b}", [P, NG, L]) for b in range(B)]
        ON = [sb(f"on{b}", [P, L]) for b in range(B)]
        OD = [sb(f"od{b}", [P, L]) for b in range(B)]
        SQR = ON
        SG = OA
        W1 = sb("w1", [P, NW1 * P])
        W2 = sb("w2", [P, NW2 * P])
        W3 = sb("w3", [P, NW3 * P])
        BV = sb("bv", [P, P])
        VEC = sb("vec", [P, LAYERS * NV])
        COS = sb("cos_t", [P, L])
        SIN = sb("sin_t", [P, L])
        IDB = sb("ident_bf", [P, P], BF16)
        IDF = sb("ident_f", [P, P])
        ONESD = sb("ones_d", [P, P])
        TRIQ = sb("tri_q", [P, P], BF16)
        TRIK = sb("tri_k", [P, P], BF16)
        CBQ = sb("cross_bias_q", [P, B * NT, S], BF16)
        CBK = sb("cross_bias_k", [S, B * L], BF16)
        SEGR = PR[0:S, 2, :].bitcast(I32)
        SEGC = sb("seg_cols", [P, B * NT], I32)
        SEGF = sb("seg_f", [P, 2, B * NT])
        IOTA = sb("iota", [P, S])
        KIDX = sb("kidx", [P, 2])
        CTX = sb("ctx", [P, B * S])
        EPS = sb("eps", [P, 2])
        GATES = sb("gates", [P, 4])
        TG = sb("tanh_gates", [P, 4])
        UV = sb("uvec", [P, 6])
        TILES = dict(cos=COS, sin=SIN, idb=IDB, idf=IDF, onesd=ONESD, triq=TRIQ, trik=TRIK, iota=IOTA,
                     kidx=KIDX, ctx=CTX, segc=SEGC, segr=SEGR, gates=GATES, uv=UV, vec=VEC)

        def carve(tile):
            flat = tile[:, :, :].rearrange("p h t -> p (h t)").bitcast(F32)
            at = [0]

            def take(rows, *shape, dt=F32):
                n = int(np.prod(shape)) * (4 if dt == F32 else 2 if dt == BF16 else 1) // 4
                v = flat[0:rows, at[0]:at[0] + n]
                v = v if dt == F32 else v.bitcast(dt)
                at[0] += n
                assert at[0] <= H * L // 2
                return v.rearrange("p (a c) -> p a c", a=shape[0]) if len(shape) == 2 else v
            return take
        in_q = [carve(QST[b]) for b in range(B)]
        in_k = [carve(KST[b]) for b in range(B)]
        in_x = [carve(QST[b]) for b in range(B)]
        XM = [in_q[b](P, NE, L) for b in range(B)]
        KW = in_x[1](P, P, dt=BF16)
        QBIAS = sb("qbias", [P, 1], BF16)
        XO = [in_k[1](P, L) for b in range(B)]
        XSC = sb("xscales", [P, 2])
        SC = sb("scales", [P, 3])
        QT = [in_x[0](P, L) for i in range(2)]
        Q8 = [in_x[0](P, L, dt=FP8) for i in range(2)]
        QK8 = [in_x[1](P, P, dt=FP8) for i in range(2)]
        XQ = [in_x[b](P, L, dt=BF16) for b in range(B)]
        KQ = in_x[1](P, P, dt=BF16)
        YB = [in_x[b](P, L, dt=BF16) for b in range(B)]
        HB = [in_x[b](P, L, dt=BF16) for b in range(B)]
        WX = in_k[1](P, 8 * P)
        in_x2 = [carve(QST[b]) for b in range(B)]
        INTERP = in_x2[1](S, L)
        BVS, BVC = in_x2[0](P, P), in_x2[0](P, P)
        KS1 = [in_q[b](P, S) for b in range(B)]
        QS1 = [in_q[b](P, S) for b in range(B)]
        VS1 = [in_x2[b](S, P) for b in range(B)]
        VC1 = [in_x2[b](P, NT, P) for b in range(B)]
        P1 = [in_q[b](P, NT, S) for b in range(B)]
        P1T = [in_q[b](S, L) for b in range(B)]
        P2 = [in_q[b](S, L) for b in range(B)]
        P2T = [in_q[b](P, NT, S) for b in range(B)]
        S2C0 = [in_q[b](S, P) for b in range(B)]
        ST1 = [sb(f"st1{b}", [P, 4, NT]) for b in range(B)]
        ST2 = [sb(f"st2{b}", [P, 4]) for b in range(B)]
        WR = sb("wr", [P, NE])
        WV = in_k[0](P, NE * 2 * FC * P)
        WP = in_k[1](P, NE * FC * P)
        RT = [in_q[b](P, 5 * NT * NE).rearrange("p (w t e) -> p w t e", t=NT, e=NE) for b in range(B)]
        OH = [sb(f"oh{b}", [P, NT, NE], BF16) for b in range(B)]
        ME = [PR[:, 2 * b:2 * b + 2, :].rearrange("p a (c t) -> p (a c) t", c=2) for b in range(B)]
        

        s_const, s_init, s_mask = sem("const_loaded"), sem("buffers_set"), sem("mask_steps")
        s_w1, s_w2, s_w3, s_late = sem("w1_loaded"), sem("w2_loaded"), sem("w3_loaded"), sem("late_loaded")
        s_interp = sem("interp_loaded")
        x_ready, xo_ready = sems("x_ready"), sems("xo_ready")
        sq_ready, rs_ready, h_ready = sems("squares_ready"), sems("rstd_ready"), sems("h_ready")
        rope_ready = sems("rope_ready")
        part1, rest1, part2, part3 = (sems(n) for n in ("part1_ready", "rest1_ready", "part2_ready", "part3_ready"))
        kc_part1, kc_rest1, kc_part2, kc_part3 = (sem(n) for n in ("kcpart1", "kcrest1", "kcpart2", "kcpart3"))
        q_landed, k_landed, kc_landed = sems("q_landed"), sems("k_landed"), sem("kc_landed")
        m_split, m_landed = sems("maximum_split"), sems("maximum_landed")
        o_landed, den_step, o_ready = sems("heads_landed"), sems("denominator_step"), sems("heads_ready")
        silu_ready, hid_ready = sems("silu_ready"), sems("hidden_ready")
        ln_sq, ln_rs, ln_out = sems("ln_squares"), sems("ln_rstd"), sems("ln_out")
        tg_ready, nf_ready = sem("tanh_ready"), sems("nf_ready")
        q_step, y_step, s_kq = sem("quantise_step"), sems("dense_step"), sem("kq_ready")
        x_q = sems("xq_ready")
        st_step, p1_ready, p2_ready = sems("softmax_step"), sems("p1_ready"), sems("p2_ready")
        exp1_ready, exp2_ready = sems("exp1_ready"), sems("exp2_ready")
        gate_ready, mix_step = sems("gate_ready"), sems("mix_step")
        rt_step, xm_ready, es_ready = sems("router_step"), sems("masked_ready"), sems("expert_silu_ready")
        eh_ready, ey_step = sems("expert_hidden_ready"), sems("expert_out_step")
        s_out = sem("out_stored")

        block = ctx.enter_context(nc.Block())

        def w1(i):
            return W1[:, i * P:(i + 1) * P]

        def w2(i):
            return W2[:, i * P:(i + 1) * P]

        def w3(i):
            return W3[:, i * P:(i + 1) * P]

        def wx(i):
            return WX[:, i * P:(i + 1) * P]

        def uv(i):
            return UV[:, i:i + 1]

        def vec(l, i):
            return VEC[:, bass.ds(l * NV + i, 1)]

        def ctx_b(b):
            return CTX[:, b * S:(b + 1) * S]

        late = [(KW, "kw"), (QBIAS, "qbias"), (XSC, "xsc"), (WX, "wx"), 
                (WR, "wr"), (WV, "wv"), (WP, "wp")]
        N_INIT = 6 + 3 * B
        N_CONST = 16 * (B + len(TILES))
        N_LATE = 16 * (B + len(late))

        def turns(eng, name, do):
            pieces = order(name)

            def skip(piece):
                for k, u, reader in uses_of(piece):
                    ring = RINGS[k]
                    if not ring.turn[u][1]:
                        continue
                    if name == "pe":
                        eng.wait_ge(ring.free(u, -1), ring.count(u, -1))
                        eng.sem_inc(ring.full(u, -1), 1)
                    elif name == reader:
                        eng.wait_ge(ring.full(u, -1), ring.count(u, -1))
                        eng.sem_inc(ring.free(u, -1), 1)

            for piece, laps in pieces:
                if laps:
                    skip(piece)
                else:
                    do(piece, 0)
            with eng.Fori(1, LAYERS) as turn:
                for piece, laps in pieces:
                    do(piece, turn - laps if laps else turn)
            for piece, laps in pieces:
                if laps:
                    do(piece, LAYERS - 1)

        @block.sync
        def _(sp):
            for b in range(B):
                sp.dma_start(RB[b][0][:, :], d["x"][b]).then_inc(s_const, 16)
            for name, tile in TILES.items():
                sp.dma_start(tile[:, :], d[name]).then_inc(s_const, 16)
            sp.dma_start(W1[:, :], d["w1"][0]).then_inc(s_w1, 16)
            sp.dma_start(BV[:, :], d["bv"][0]).then_inc(s_w1, 16)
            sp.dma_start(W2[:, :], d["w2"][0]).then_inc(s_w2, 16)
            sp.dma_start(W3[:, :], d["w3"][0]).then_inc(s_w3, 16)
            sp.wait_ge(s_init, N_INIT)

            def restack(part, stack, side, i, landed):
                for r, pair in enumerate(PRODUCTS):
                    if pair[side] == i:
                        sp.dma_start(stack[r * HD:(r + 1) * HD, :, :], part[:, i, :]).then_inc(landed, 16)

            def do(piece, l):
                s, b, *at = piece
                if s in ("high", "low"):
                    i = at[0]
                    ready = 3 * l + i + 1
                    part, stack = PART[b][i % 2], (QST, KST)[i == 1][b]
                    landed = (q_landed, k_landed)[i == 1][b]
                    if s == "high":
                        sp.wait_ge(part1[b], ready)
                        restack(part, stack, i == 1, 0, landed)
                    else:
                        sp.wait_ge(part2[b], ready)
                        restack(part, stack, i == 1, 1, landed)
                        sp.wait_ge(part3[b], ready)
                        restack(part, stack, i == 1, 2, landed)
                elif s == "kchigh":
                    sp.wait_ge(kc_part1, l + 1)
                    restack(KCPART, KCST, 1, 0, kc_landed)
                elif s == "kclow":
                    for i, ready in ((1, kc_part2), (2, kc_part3)):
                        sp.wait_ge(ready, l + 1)
                        restack(KCPART, KCST, 1, i, kc_landed)
                elif s == "mrow":
                    sp.wait_ge(G.free(piece, l), G.read(piece, l))
                    sp.dma_start(QST[b][KZ:KM, :, :], MT[b][:, :]).then_inc(m_landed[b], 16)
                elif s in ("values", "cvalues") and at[0] == NG - 1:
                    sp.wait_ge(O.free(piece, l), O.read(piece, l))
                    for j in range(HG):
                        for tile, r in ((ON, 32 * j), (OD, 32 * j + HD)):
                            sp.dma_start(tile[b][32 * j:32 * j + 32, :],
                                         OA[b][r:r + HD, :, :]).then_inc(o_landed[b], 16)
                elif s == "w1":
                    sp.wait_ge(G.free(("vals", b), l), G.read(("vals", b), l))
                    sp.dma_start(W1[:, :], d["w1"][bass.ds(l + 1, 1)]).then_inc(s_w1, 16)
                    sp.dma_start(BV[:, :], d["bv"][bass.ds(l + 1, 1)]).then_inc(s_w1, 16)
                elif s == "w2":
                    sp.wait_ge(G.free(("qc", b), l), G.read(("qc", b), l))
                    sp.dma_start(W2[:, :], d["w2"][bass.ds(l + 1, 1)]).then_inc(s_w2, 16)
                elif s == "w3" and not isinstance(l, int):
                    sp.wait_ge(G.free(("down", b), l), G.read(("down", b), l))
                    sp.dma_start(W3[:, :], d["w3"][bass.ds(l + 1, 1)]).then_inc(s_w3, 16)

            turns(sp, "sp", do)
            for b in range(B):
                sp.wait_ge(x_ready[b], 3 * LAYERS + 1)
            for b in range(B):
                sp.dma_start(XO[b], d["x"][b]).then_inc(s_late, 16)
            for tile, name in late:
                sp.dma_start(tile[:, :], d[name]).then_inc(s_late, 16)
            for b in range(B):
                sp.wait_ge(xo_ready[b], 2)
            for tile, name in ((BVS, "bvs"), (BVC, "bvc"), (INTERP, "interp")):
                sp.dma_start(tile, d[name]).then_inc(s_interp, 16)
            for b in range(B):
                sp.wait_ge(xo_ready[b], 4)
                sp.dma_start(out[b], XO[b][:, :]).then_inc(s_out, 16)
            sp.wait_ge(s_out, 16 * B)
            sp.wait_ge(s_w1, 32 * (LAYERS + 1))
            sp.wait_ge(s_w2, 16 * (LAYERS + 1))

        @block.tensor
        def _(pe):
            for r in RINGS.values():
                for k in r.freed:
                    pe.sem_inc(k, 1)
            pe.wait_ge(s_const, N_CONST)

            def general(u, l, lhsT, rhs, width=512):
                pe.wait_ge(G.free(u, l), G.count(u, l))
                pe.matmul(G.at(u, l)[0:lhsT.shape[1], 0:width], lhsT, rhs, start=True, stop=True)\
                  .then_inc(G.full(u, l), 1)

            def layer_norm(b, n, src, ready, value):
                pe.wait_ge(ready, value)
                general(("mean", b, n), 0, ONESD[:, :], src[:, :])

            def layer_var(b, n):
                pe.wait_ge(ln_sq[b], n + 1)
                general(("var", b, n), 0, ONESD[:, :], SQR[b][:, :])

            for b in range(B):
                layer_norm(b, 0, RB[b][0], s_const, N_CONST)
            for b in range(B):
                layer_var(b, 0)
            pe.wait_ge(s_init, N_INIT)
            pe.wait_ge(s_mask, 7)

            def do(piece, l):
                s, b, *at = piece
                if s == "norm":
                    pe.wait_ge(sq_ready[b], 3 * l + at[0])
                    general(piece, l, ONESD[:, :], SQR[b][:, :])
                elif s == "rope":
                    if at[0] == 0:
                        pe.wait_ge(h_ready[b], 3 * l + 1)
                        pe.wait_ge(s_w1, 32 * (l + 1))
                    w = (W_Q, W_K)[at[0]]
                    pe.wait_ge(T.free(piece, l), T.count(piece, l))
                    pe.matmul(T.at(piece, l)[:, 0:512], w1(w), HN[b][:, :], start=True, stop=True)
                    pe.matmul(T.at(piece, l)[:, 512:1024], w1(w + 1), HN[b][:, :], start=True, stop=True)\
                      .then_inc(T.full(piece, l), 1)
                elif s == "vals":
                    pe.wait_ge(G.free(piece, l), G.count(piece, l))
                    for t in range(NT):
                        mm = pe.matmul(G.at(piece, l)[:, t * P:(t + 1) * P], HN[b][:, t * P:(t + 1) * P], w1(W_V),
                                       start=True, stop=True)
                    mm.then_inc(G.full(piece, l), 1)
                elif s == "kvc":
                    pe.wait_ge(s_w2, 16 * (l + 1))
                    general(("kc", 0), l, w2(W_KC), CTX[:, :], B * S)
                    u = ("vc", 0)
                    pe.wait_ge(G.free(u, l), G.count(u, l))
                    for c in range(B):
                        mm = pe.matmul(G.at(u, l)[0:S, c * P:(c + 1) * P], ctx_b(c), w2(W_VC), start=True, stop=True)
                    mm.then_inc(G.full(u, l), 1)
                elif s == "smax":
                    max_scores(piece, l)
                elif s == "csmax":
                    max_cross_scores(piece, l)
                elif s == "mrow":
                    minus_maxima(piece, l)
                elif s == "scores":
                    self_scores(piece, l)
                elif s == "cscores":
                    cross_scores(piece, l)
                elif s in ("values", "cvalues"):
                    value_products(piece, l)
                elif s in ("oproj", "ocproj"):
                    n = 1 if s == "oproj" else 2
                    if s == "ocproj":
                        pe.wait_ge(s_w3, 16 * (l + 1))
                    elif b == 0:
                        pe.wait_ge(s_w2, 16 * (l + 1))
                    pe.wait_ge(o_ready[b], 2 * l + n)
                    general(piece, l, w2(W_O) if n == 1 else w3(W_OC), ON[b][:, :])
                elif s == "qc":
                    pe.wait_ge(h_ready[b], 3 * l + 2)
                    general(piece, l, w2(W_QC), HN[b][:, :])
                elif s == "ffn":
                    if at[0] == 0:
                        pe.wait_ge(h_ready[b], 3 * l + 3)
                    pe.wait_ge(T.free(piece, l), T.count(piece, l))
                    pe.matmul(T.at(piece, l)[:, 0:512], w3(W_G + at[0]), HN[b][:, :], start=True, stop=True)
                    pe.matmul(T.at(piece, l)[:, 512:1024], w3(W_U + at[0]), HN[b][:, :], start=True, stop=True)\
                      .then_inc(T.full(piece, l), 1)
                elif s == "down":
                    pe.wait_ge(G.free(piece, l), G.count(piece, l))
                    for c in range(FC):
                        u = ("ffn", b, c)
                        pe.wait_ge(T.free(u, l), T.read(u, l))
                        mm = pe.matmul(G.at(piece, l)[:, :], w3(W_D + c), SG[b][:, c, :],
                                       start=(c == 0), stop=(c == FC - 1))
                    mm.then_inc(G.full(piece, l), 1)

            def max_scores(u, l):
                _, b, i = u
                if i == 0:
                    pe.wait_ge(q_landed[b], 16 * PP * (2 * l + 1))
                    pe.wait_ge(k_landed[b], 16 * PP * (l + 1))
                t, h0, n = S_UNITS[i]
                keys = (t + 1) * P
                pe.wait_ge(Q.free(u, l), Q.count(u, l))
                for k in range(n):
                    o = k * keys
                    pe.matmul(Q.at(u, l)[:, o:o + keys], QST[b][0:KZ, h0 + k, t * P:(t + 1) * P],
                              KST[b][0:KZ, h0 + k, 0:keys], start=True, stop=False)
                    mm = pe.matmul(Q.at(u, l)[:, o + keys - P:o + keys], IDB[:, :], TRIQ[:, :],
                                   start=False, stop=True)
                mm.then_inc(Q.full(u, l), 1)

            def max_cross_scores(u, l):
                _, b, i = u
                if i == 0:
                    pe.wait_ge(q_landed[b], 16 * PP * (2 * l + 2))
                    pe.wait_ge(kc_landed, 16 * PP * (l + 1))
                t, h0, n = C_UNITS[i]
                pe.wait_ge(Q.free(u, l), Q.count(u, l))
                for k in range(n):
                    pe.matmul(Q.at(u, l)[:, k * S:(k + 1) * S], QST[b][0:KZ, h0 + k, t * P:(t + 1) * P],
                              KCST[0:KZ, h0 + k, b * S:(b + 1) * S], start=(k == 0), stop=False,
                              skip_group_check=True)
                pe.matmul(Q.at(u, l)[:, 0:n * S].rearrange("p (h k) -> p h k", k=S), IDB[:, :],
                          CBQ[:, b * NT + t:b * NT + t + 1, :].broadcast_to([P, n, S]),
                          start=False, stop=True, skip_group_check=True).then_inc(Q.full(u, l), 1)

            def minus_maxima(u, l):
                _, b, n = u
                pe.wait_ge(m_split[b], 8 * l + 4 * n)
                pe.wait_ge(G.free(u, l), G.count(u, l))
                for t in range(NT):
                    mm = pe.matmul(G.at(u, l)[0:PARTS * H, t * P:(t + 1) * P],
                                   MPART[b][:, t, :, :].rearrange("p a h -> p (a h)"), IDB[:, :],
                                   start=True, stop=True)
                mm.then_inc(G.full(u, l), 1)

            def self_scores(u, l):
                _, b, g, v = u

                def product(bank, h, kt):
                    pe.matmul(bank[:, 0:L - kt * P], KST[b][0:KM, h, kt * P:(kt + 1) * P],
                              QST[b][0:KM, h, kt * P:L], start=True, stop=False)
                    return pe.matmul(bank[:, 0:P], IDB[:, :], TRIK[:, :], start=False, stop=True)

                if g == 0 and v == 0:
                    pe.wait_ge(m_landed[b], 16 * (2 * l + 1))
                slot = T.at(u, l)
                pe.wait_ge(T.free(u, l), T.count(u, l))
                for j in range(2) if v < 4 else range(4):
                    h = HG * g + (2 * (v % 2) + j if v < 4 else j)
                    if v < 2:
                        mm = product(slot[:, j * 512:(j + 1) * 512], h, 0)
                    elif v < 4:
                        product(slot[:, j * 512:j * 512 + 384], h, 1)
                        mm = product(slot[:, j * 512 + 384:(j + 1) * 512], h, 3)
                    else:
                        mm = product(slot[:, j * 256:(j + 1) * 256], h, 2)
                mm.then_inc(T.full(u, l), 1)

            def cross_scores(u, l):
                _, b, g, v = u
                if g == 0 and v == 0:
                    pe.wait_ge(m_landed[b], 16 * (2 * l + 2))
                pe.wait_ge(T.free(u, l), T.count(u, l))
                for j in range(2):
                    bank = T.at(u, l)[0:S, j * 512:(j + 1) * 512]
                    h = HG * g + 2 * v + j
                    pe.matmul(bank, KCST[0:KM, h, b * S:(b + 1) * S], QST[b][0:KM, h, :],
                              start=True, stop=False)
                    mm = pe.matmul(bank, IDB[0:S, 0:S], CBK[:, b * L:(b + 1) * L], start=False, stop=True)
                mm.then_inc(T.full(u, l), 1)

            def where(j, kt):
                if kt == 0:
                    return j // 2, (j % 2) * 512
                if kt == 2:
                    return 4, j * 256
                return 2 + j // 2, (j % 2) * 512 + (0 if kt == 1 else 384)

            def value_products(u, l):
                s, b, g = u
                name = "scores" if s == "values" else "cscores"
                slots = A_SLOTS if s == "values" else C_SLOTS
                if g == 0:
                    own = ("vals", b) if s == "values" else ("vc", 0)
                    pe.wait_ge(G.free(own, l), G.read(own, l))
                for v in range(slots - 2, slots):
                    w = (name, b, g, v)
                    pe.wait_ge(T.free(w, l), T.read(w, l))
                pe.wait_ge(O.free(u, l), O.count(u, l))
                for kt in range(NT if s == "values" else 1):
                    for j in range(HG):
                        h = HG * g + j
                        if s == "values":
                            v, c = where(j, kt)
                            probs = PR[:, E.buffer((name, b, g, v), l), c:c + L - kt * P]
                            operand = VA[b][:, kt, h:h + 2, :]
                        else:
                            probs = PR[0:S, E.buffer((name, b, g, j // 2), l), (j % 2) * 512:(j % 2 + 1) * 512]
                            operand = VCA[:, b, h:h + 2, :]
                        mm = pe.matmul(O.at(u, l)[32 * j:32 * j + 32, kt * P:L],
                                       operand.rearrange("p h c -> p (h c)"), probs,
                                       start=(kt == 0), stop=(kt == NT - 1 or s == "cvalues"))
                mm.then_inc(O.full(u, l), 1)

            turns(pe, "pe", do)

            for b in range(B):
                pe.wait_ge(sq_ready[b], 3 * LAYERS + 1)
                general(("nf", b), 0, ONESD[:, :], SQR[b][:, :])
            for b in range(B):
                layer_norm(b, 1, XO[b], xo_ready[b], 1)
            for b in range(B):
                layer_var(b, 1)
            pe.wait_ge(s_kq, 1)
            for b in range(B):
                pe.wait_ge(x_q[b], 1)
                general(("dense", b), 0, KQ[:, :], XQ[b][:, :])
            for b in range(B):
                layer_norm(b, 2, XO[b], xo_ready[b], 2)
            for b in range(B):
                layer_var(b, 2)
            for b in range(B):
                qct, kct = RA[b][1], RB[b][1]
                pe.wait_ge(ln_out[b], 2)
                general(("xqc", b), 0, wx(X_QC), HN[b][:, :])
                general(("xks", b), 0, wx(X_KS), ctx_b(b), S)
                general(("xvs", b), 0, ctx_b(b), wx(X_VS), P)
                general(("xqs", b), 0, wx(X_QS), ctx_b(b), S)
                general(("xkc", b), 0, wx(X_KC), HN[b][:, :])
                u = ("xvc", b)
                pe.wait_ge(G.free(u), G.count(u))
                for t in range(NT):
                    mm = pe.matmul(G.at(u)[:, t * P:(t + 1) * P], HN[b][:, t * P:(t + 1) * P], wx(X_VC),
                                   start=True, stop=True)
                mm.then_inc(G.full(u), 1)
                u = ("s1", b)
                pe.wait_ge(G.free(u), G.count(u))
                for t in range(NT):
                    mm = pe.matmul(G.at(u)[:, t * S:(t + 1) * S], qct[:, t * P:(t + 1) * P], KS1[b][:, :],
                                   start=True, stop=True)
                mm.then_inc(G.full(u), 1)
                general(("s2", b), 0, QS1[b][:, :], kct[:, :])
                u = ("p1t", b)
                pe.wait_ge(p1_ready[b], 1)
                pe.wait_ge(G.free(u), G.count(u))
                for t in range(NT):
                    mm = pe.transpose(G.at(u)[0:S, t * P:(t + 1) * P], P1[b][:, t, :], IDF[:, :])
                mm.then_inc(G.full(u), 1)
                u = ("p2t", b)
                pe.wait_ge(p2_ready[b], 1)
                pe.wait_ge(G.free(u), G.count(u))
                for t in range(NT):
                    mm = pe.transpose(G.at(u)[:, t * S:(t + 1) * S], P2[b][:, t * P:(t + 1) * P], IDF[0:S, 0:S])
                mm.then_inc(G.full(u), 1)
                general(("c2s", b), 0, VS1[b][:, :], P1T[b][:, :])
                u = ("s2c0", b)
                pe.wait_ge(G.free(u), G.count(u))
                for t in range(NT):
                    mm = pe.matmul(G.at(u)[0:S, 0:P], P2T[b][:, t, :], VC1[b][:, t, :],
                                   start=(t == 0), stop=(t == NT - 1))
                mm.then_inc(G.full(u), 1)
                pe.wait_ge(G.free(u), G.read(u))
                pe.wait_ge(s_interp, 48)
                general(("s2c", b), 0, S2C0[b][:, :], INTERP[:, :])
                u = ("gate", b)
                pe.wait_ge(G.free(u), G.count(u))
                pe.matmul(G.at(u)[:, :], wx(X_G1), RA[b][0][:, :], start=True, stop=False)
                pe.matmul(G.at(u)[:, :], wx(X_G2), RB[b][0][:, :], start=False, stop=True).then_inc(G.full(u), 1)
            for b in range(B):
                layer_norm(b, 3, XO[b], xo_ready[b], 3)
            for b in range(B):
                layer_var(b, 3)
            for b in range(B):
                u = ("router", b)
                pe.wait_ge(ln_out[b], 3)
                pe.wait_ge(G.free(u), G.count(u))
                for t in range(NT):
                    mm = pe.matmul(G.at(u)[:, t * NE:(t + 1) * NE], HN[b][:, t * P:(t + 1) * P], WR[:, :],
                                   start=True, stop=True)
                mm.then_inc(G.full(u), 1)
                pe.wait_ge(rt_step[b], 9)
                for e in range(NE):
                    u = ("spread", b, e)
                    pe.wait_ge(G.free(u), G.count(u))
                    for t in range(NT):
                        mm = pe.matmul(G.at(u)[:, t * P:(t + 1) * P],
                                       OH[b][:, t, e:e + 1].broadcast_to([P, P]), IDB[:, :], start=True, stop=True)
                    mm.then_inc(G.full(u), 1)
                pe.wait_ge(xm_ready[b], NE)
                for c in range(FC):
                    u = ("moe", b, c)
                    pe.wait_ge(T.free(u), T.count(u))
                    for half in range(2):
                        for e in range(NE):
                            o = (e * 2 * FC + half * FC + c) * P
                            mm = pe.matmul(T.at(u)[:, half * 512:(half + 1) * 512], WV[:, o:o + P],
                                           XM[b][:, e, :], start=(e == 0), stop=(e == NE - 1))
                    mm.then_inc(T.full(u), 1)
                for c in range(FC):
                    pe.wait_ge(T.free(("moe", b, c)), T.read(("moe", b, c)))
                for e in range(NE):
                    u = ("edown", b, e)
                    pe.wait_ge(G.free(u), G.count(u))
                    for c in range(FC):
                        o = (e * FC + c) * P
                        mm = pe.matmul(G.at(u)[:, :], WP[:, o:o + P], SG[b][:, c, :],
                                       start=(c == 0), stop=(c == FC - 1))
                    mm.then_inc(G.full(u), 1)

        @block.scalar
        def _(act):
            act.wait_ge(s_const, N_CONST)
            act.wait_ge(s_init, N_INIT)
            nc.scalar.activation(TG[:, :], GATES[:, :], ACT.Tanh).then_inc(tg_ready, 1)
            loaded = [None]

            def logexp():
                if loaded[0] != "logexp":
                    nc.scalar.preload_act_table_set("natural_log_exp_and_others")
                    loaded[0] = "logexp"

            def root(u, b, l, eps, ready):
                logexp()
                act.wait_ge(G.full(u, l), G.count(u, l))
                nc.scalar.activation(RS[b][:, :], G.at(u, l)[:, :], ACT.Ln, bias=EPS[:, eps:eps + 1])\
                    .then_inc(G.free(u, l), 1)
                act.wait_ge(G.free(u, l), G.read(u, l))
                nc.scalar.activation(RS[b][:, :], RS[b][:, :], ACT.Exp, scale=-0.5).then_inc(ready, 1)

            def copy(u, l, dst, rows=P, width=512, view=None):
                act.wait_ge(G.full(u, l), G.count(u, l))
                src = view(G.at(u, l)) if view else G.at(u, l)[0:rows, 0:width]
                nc.scalar.activation(dst, src, ACT.Copy).then_inc(G.free(u, l), 1)

            def do(piece, l):
                s, b, *at = piece
                if s == "norm":
                    root(piece, b, l, 0, rs_ready[b])
                elif s == "kvc":
                    copy(("kc", 0), l, KC32[:, :], P, B * S)
                    copy(("vc", 0), l, VCA[:, :, 0:H, 0:HD],
                         view=lambda bank: bank[0:S, 0:B * P].rearrange("p (b h d) -> p b h d", b=B, h=H))
                elif s == "mrow":
                    copy(piece, l, MT[b][:, :], PARTS * H, L)
                elif s in ("scores", "cscores"):
                    logexp()
                    rows = P if s == "scores" else S
                    former = E.before(piece, l)
                    if former:
                        act.wait_ge(O.full(*former), O.count(*former))
                    act.wait_ge(T.full(piece, l), T.count(piece, l))
                    nc.scalar.activation(PR[0:rows, E.buffer(piece, l), :], T.at(piece, l)[0:rows, :], ACT.Exp,
                                         scale=SCALE).then_inc(T.free(piece, l), 1)
                elif s == "heads":
                    n = at[0]
                    logexp()
                    act.wait_ge(o_landed[b], 16 * 2 * HG * (2 * l + n))
                    nc.scalar.activation(OD[b][:, :], OD[b][:, :], ACT.Ln).then_inc(den_step[b], 1)
                    act.wait_ge(den_step[b], 4 * l + 2 * n - 1)
                    nc.scalar.activation(OD[b][:, :], OD[b][:, :], ACT.Exp, scale=-1.0).then_inc(den_step[b], 1)
                elif s == "qc":
                    copy(piece, l, RA[b][0][:, :])
                elif s == "ffn":
                    loaded[0] = "silu"
                    act.wait_ge(T.full(piece, l), T.count(piece, l))
                    nc.scalar.activation(SG[b][:, at[0], :], T.at(piece, l)[:, 0:512], ACT.Silu)\
                        .then_inc(silu_ready[b], 1)

            for b in range(B):
                root(("var", b, 0), b, 0, 1, ln_rs[b])
            turns(act, "act", do)
            for b in range(B):
                root(("nf", b), b, 0, 0, rs_ready[b])
            for b in range(B):
                root(("var", b, 1), b, 0, 1, ln_rs[b])
            for b in range(B):
                root(("var", b, 2), b, 0, 1, ln_rs[b])
            for b in range(B):
                def biased(u, dst, bias, width):
                    act.wait_ge(G.full(u), G.count(u))
                    nc.scalar.activation(dst, G.at(u)[:, 0:width], ACT.Identity, bias=uv(bias))\
                        .then_inc(G.free(u), 1)

                biased(("xqc", b), RA[b][1][:, :], U_BQC, L)
                biased(("xks", b), KS1[b][:, :], U_BKS, S)
                biased(("xqs", b), QS1[b][:, :], U_BQS, S)
                biased(("xkc", b), RB[b][1][:, :], U_BKC, L)
                act.wait_ge(st_step[b], 1)
                for t in range(NT):
                    ins = nc.scalar.activation(P1[b][:, t, :], G.at(("s1", b))[:, t * S:(t + 1) * S], ACT.Exp,
                                               scale=SCALE1, bias=ST1[b][:, 1, t:t + 1],
                                               accum_out=ST1[b][:, 2, t:t + 1])
                    ins.then_inc(exp1_ready[b], 1)
                act.wait_ge(st_step[b], 3)
                nc.scalar.activation(P2[b][:, :], G.at(("s2", b))[0:S, :], ACT.Exp, scale=SCALE1,
                                     bias=ST2[b][0:S, 1:2], accum_out=ST2[b][0:S, 2:3]).then_inc(exp2_ready[b], 1)
                loaded[0] = "other"
                copy(("p1t", b), 0, P1T[b][:, :], S, L)
                copy(("p2t", b), 0, P2T[b][:, :, :],
                     view=lambda bank: bank[:, 0:NT * S].rearrange("p (t k) -> p t k", t=NT))
                copy(("c2s", b), 0, RA[b][0][:, :])
                copy(("s2c0", b), 0, S2C0[b][:, :], S, P)
                copy(("s2c", b), 0, RB[b][0][:, :])
                u = ("gate", b)
                act.wait_ge(G.full(u), G.count(u))
                nc.scalar.activation(ON[b][:, :], G.at(u)[:, :], ACT.Sigmoid, bias=uv(U_BG))\
                    .then_inc(G.free(u), 1)
            for b in range(B):
                root(("var", b, 3), b, 0, 1, ln_rs[b])
            for b in range(B):
                for e in range(NE):
                    copy(("spread", b, e), 0, ME[b][:, e, :])
                for c in range(FC):
                    u = ("moe", b, c)
                    act.wait_ge(T.full(u), T.count(u))
                    nc.scalar.activation(SG[b][:, c, :], T.at(u)[:, 0:512], ACT.Silu).then_inc(es_ready[b], 1)

        @block.gpsimd
        def _(pool):
            for b in range(B):
                pool.memset(QST[b][32:64, :, :], 0.0).then_inc(s_init, 1)
                pool.memset(QST[b][64:KZ, :, :], 0.0).then_inc(s_init, 1)
                pool.memset(KST[b][64:KZ, :, :], 0.0).then_inc(s_init, 1)
            pool.memset(KCST[32:64, :, :], 0.0).then_inc(s_init, 1)
            pool.memset(KCST[64:KZ, :, :], 0.0).then_inc(s_init, 1)
            pool.wait_ge(s_init, N_INIT)

            def tt(out_, a, b_, op, done):
                nc.gpsimd.tensor_tensor(out_, a, b_, op).then_inc(done, 1)

            def centred(b, n):
                u = ("mean", b, n)
                pool.wait_ge(G.free(u), G.read(u))
                tt(SQR[b][:, :], OD[b][:, :], OD[b][:, :], ALU.mult, ln_sq[b])

            for b in range(B):
                centred(b, 0)

            def do(piece, l):
                s, b, *at = piece
                if s == "norm":
                    pool.wait_ge(x_ready[b], 3 * l + at[0])
                    tt(SQR[b][:, :], X[b][:, :], X[b][:, :], ALU.mult, sq_ready[b])
                elif s == "rope":
                    i = at[0]
                    pool.wait_ge(T.free(piece, l), T.read(piece, l))
                    tt(RA[b][i][:, :], RA[b][i][:, :], RB[b][i][:, :], ALU.add, rope_ready[b])
                elif s == "high":
                    i, n = at[0] % 2, at[0] + 1
                    pool.wait_ge(part1[b], 3 * l + n)
                    tt(RB[b][i][:, :], RA[b][i][:, :], PART[b][i][:, 0, :], ALU.subtract, rest1[b])
                elif s == "low":
                    i, n = at[0] % 2, at[0] + 1
                    pool.wait_ge(part2[b], 3 * l + n)
                    pool.wait_ge(rest1[b], 3 * l + n)
                    tt(PART[b][i][:, 2, :], RB[b][i][:, :], PART[b][i][:, 1, :], ALU.subtract, part3[b])
                elif s == "kchigh":
                    pool.wait_ge(kc_part1, l + 1)
                    tt(KCREST[:, :], KC32[:, :], KCPART[:, 0, :], ALU.subtract, kc_rest1)
                elif s == "kclow":
                    pool.wait_ge(kc_part2, l + 1)
                    pool.wait_ge(kc_rest1, l + 1)
                    tt(KCPART[:, 2, :], KCREST[:, :], KCPART[:, 1, :], ALU.subtract, kc_part3)

            turns(pool, "pool", do)
            for b in range(B):
                pool.wait_ge(x_ready[b], 3 * LAYERS + 1)
                tt(SQR[b][:, :], X[b][:, :], X[b][:, :], ALU.mult, sq_ready[b])
            for n in (1, 2):
                for b in range(B):
                    centred(b, n)
            for b in range(B):
                pool.wait_ge(mix_step[b], 1)
                tt(OD[b][:, :], OD[b][:, :], ON[b][:, :], ALU.mult, gate_ready[b])
            for b in range(B):
                centred(b, 3)
            for b in range(B):
                for e in range(NE):
                    u = ("spread", b, e)
                    pool.wait_ge(G.free(u), G.read(u))
                    tt(XM[b][:, e, :], HN[b][:, :], ME[b][:, e, :], ALU.mult, xm_ready[b])

        @block.vector
        def _(dve):
            v = nc.vector
            for b in range(B):
                v.memset(KST[b][KZ:KM, :, :], 1.0)
                v.memset(VA[b][:, :, 0:H, HD:VW], 1.0)
                v.memset(VA[b][:, :, H, :], 0.0)
            v.memset(KCST[KZ:KM, :, :], 1.0)
            v.memset(VCA[:, :, 0:H, HD:VW], 1.0)
            v.memset(VCA[:, :, H, :], 0.0)
            for b in range(B):
                v.memset(KST[b][32:64, :, :], 0.0)
            v.memset(EPS[:, 0:1], RMS_EPS).then_inc(s_init, 1)
            v.memset(EPS[:, 1:2], LN_EPS).then_inc(s_init, 1)
            v.memset(ST2[0][:, :], 0.0).then_inc(s_init, 1)
            v.memset(ST2[1][:, :], 0.0).then_inc(s_init, 1)
            dve.wait_ge(s_const, N_CONST)

            def centre(b, n, src):
                u = ("mean", b, n)
                dve.wait_ge(G.full(u), G.count(u))
                v.tensor_tensor(OD[b][:, :], src[:, :], G.at(u)[:, :], ALU.subtract).then_inc(G.free(u), 1)

            def normed(b, n, dst, done):
                dve.wait_ge(ln_rs[b], n + 1)
                v.tensor_tensor(dst[:, :], OD[b][:, :], RS[b][:, :], ALU.mult).then_inc(done, 1)

            for b in range(B):
                centre(b, 0, RB[b][0])
            allow = PR[0:S, 0, :]
            allow2 = PR[0:S, 1, :]
            v.tensor_scalar(allow, SEGR[:, :], KIDX[0:S, 0:1], None, ALU.is_ge).then_inc(s_mask, 1)
            v.tensor_scalar(SEGF[:, 0, :], SEGC[:, :], 1.0, None, ALU.mult).then_inc(s_mask, 1)
            dve.wait_ge(s_mask, 1)
            v.scalar_tensor_tensor(out=allow2, in0=SEGR[:, :], scalar=KIDX[0:S, 1:2], in1=allow,
                                   op0=ALU.is_lt, op1=ALU.mult).then_inc(s_mask, 1)
            dve.wait_ge(s_mask, 3)
            v.tensor_scalar(CBK[:, :], allow2, -1.0, -NEG, ALU.add, ALU.mult).then_inc(s_mask, 1)
            tiles = B * NT
            qa = PR[:, 3, 0:tiles * S].rearrange("p (t k) -> p t k", t=tiles)
            qb = PR[:, 4, 0:tiles * S].rearrange("p (t k) -> p t k", t=tiles)
            seg = SEGF[:, 0, :].rearrange("p (t o) -> p t o", o=1).broadcast_to([P, tiles, S])
            idx = IOTA[:, :].rearrange("p (o k) -> p o k", o=1).broadcast_to([P, tiles, S])
            v.tensor_tensor(qa, idx, seg, ALU.is_le).then_inc(s_mask, 1)
            dve.wait_ge(s_mask, 5)
            v.tensor_tensor(qb, seg, idx, ALU.subtract).then_inc(s_mask, 1)
            dve.wait_ge(s_mask, 6)
            v.scalar_tensor_tensor(out=qb, in0=qb, scalar=float(LOOKBACK), in1=qa,
                                   op0=ALU.is_lt, op1=ALU.mult).then_inc(s_mask, 1)
            dve.wait_ge(s_mask, 7)
            v.tensor_scalar(CBQ[:, :, :], qb, -1.0, -NEG, ALU.add, ALU.mult).then_inc(s_mask, 1)
            for b in range(B):
                normed(b, 0, X[b], x_ready[b])

            def normed_rms(b, l, n, col):
                dve.wait_ge(rs_ready[b], 3 * l + n)
                v.scalar_tensor_tensor(out=HN[b][:, :], in0=X[b][:, :], scalar=col, in1=RS[b][:, :],
                                       op0=ALU.mult, op1=ALU.mult).then_inc(h_ready[b], 1)

            def split_maxima(piece, l):
                _, b, n = piece
                name, units = ("smax", S_UNITS) if n == 1 else ("csmax", C_UNITS)
                for i in (len(units) - 2, len(units) - 1):
                    dve.wait_ge(Q.free((name, b, i), l), Q.read((name, b, i), l))
                base = 8 * l + 4 * n - 4
                v.tensor_scalar(MPART[b][:, :, 0, :], MX[b][:, :, :], -1.0, None, ALU.mult).then_inc(m_split[b], 1)
                dve.wait_ge(m_split[b], base + 1)
                v.scalar_tensor_tensor(out=MREST[b][:, :, :], in0=MX[b][:, :, :], scalar=-1.0,
                                       in1=MPART[b][:, :, 0, :], op0=ALU.mult, op1=ALU.subtract)\
                    .then_inc(m_split[b], 1)
                dve.wait_ge(m_split[b], base + 2)
                v.tensor_copy(MPART[b][:, :, 1, :], MREST[b][:, :, :]).then_inc(m_split[b], 1)
                dve.wait_ge(m_split[b], base + 3)
                v.tensor_tensor(MPART[b][:, :, 2, :], MREST[b][:, :, :], MPART[b][:, :, 1, :], ALU.subtract)\
                    .then_inc(m_split[b], 1)

            def do(piece, l):
                s, b, *at = piece
                if s == "norm":
                    normed_rms(b, l, at[0], vec(l, (V_N1, V_N2, V_N3)[at[0] - 1]))
                elif s == "rope":
                    i = at[0]
                    c0, c1 = ((V_BQ, V_BQR), (V_BK, V_BKR))[i]
                    dve.wait_ge(T.full(piece, l), T.count(piece, l))
                    v.scalar_tensor_tensor(out=RA[b][i][:, :], in0=T.at(piece, l)[:, 0:512], scalar=vec(l, c0),
                                           in1=COS[:, :], op0=ALU.add, op1=ALU.mult)
                    v.scalar_tensor_tensor(out=RB[b][i][:, :], in0=T.at(piece, l)[:, 512:1024], scalar=vec(l, c1),
                                           in1=SIN[:, :], op0=ALU.add, op1=ALU.mult).then_inc(T.free(piece, l), 1)
                elif s == "vals":
                    dve.wait_ge(G.full(piece, l), G.count(piece, l))
                    for t in range(NT):
                        ins = v.tensor_tensor(VA[b][:, t, 0:H, 0:HD],
                                              G.at(piece, l)[:, t * P:(t + 1) * P]
                                              .rearrange("p (h d) -> p h d", h=H),
                                              BV[:, :].rearrange("p (h d) -> p h d", h=H), ALU.add)
                    ins.then_inc(G.free(piece, l), 1)
                elif s == "high":
                    i = at[0] % 2
                    if at[0] < 2:
                        dve.wait_ge(rope_ready[b], 2 * l + i + 1)
                    else:
                        dve.wait_ge(G.free(("qc", b), l), G.read(("qc", b), l))
                    v.tensor_copy(PART[b][i][:, 0, :], RA[b][i][:, :]).then_inc(part1[b], 1)
                elif s == "low":
                    i = at[0] % 2
                    dve.wait_ge(rest1[b], 3 * l + at[0] + 1)
                    v.tensor_copy(PART[b][i][:, 1, :], RB[b][i][:, :]).then_inc(part2[b], 1)
                elif s == "kchigh":
                    dve.wait_ge(G.free(("kc", 0), l), G.read(("kc", 0), l))
                    v.tensor_copy(KCPART[:, 0, :], KC32[:, :]).then_inc(kc_part1, 1)
                elif s == "kclow":
                    dve.wait_ge(kc_rest1, l + 1)
                    v.tensor_copy(KCPART[:, 1, :], KCREST[:, :]).then_inc(kc_part2, 1)
                elif s in ("smax", "csmax"):
                    t, h0, n = (S_UNITS if s == "smax" else C_UNITS)[at[0]]
                    k = (t + 1) * P if s == "smax" else S
                    dve.wait_ge(Q.full(piece, l), Q.count(piece, l))
                    v.tensor_reduce(MX[b][:, t, h0:h0 + n],
                                    Q.at(piece, l)[:, 0:n * k].rearrange("p (h k) -> p h k", k=k),
                                    AX.X, ALU.max).then_inc(Q.free(piece, l), 1)
                elif s == "mrow":
                    split_maxima(piece, l)
                elif s in ("values", "cvalues"):
                    dve.wait_ge(O.full(piece, l), O.count(piece, l))
                    v.tensor_copy(OA[b][:, at[0], :], O.at(piece, l)[:, :]).then_inc(O.free(piece, l), 1)
                elif s == "heads":
                    dve.wait_ge(den_step[b], 4 * l + 2 * at[0])
                    v.tensor_tensor(ON[b][:, :], ON[b][:, :], OD[b][:, :], ALU.mult).then_inc(o_ready[b], 1)
                elif s in ("oproj", "ocproj", "down"):
                    dve.wait_ge(G.full(piece, l), G.count(piece, l))
                    if s == "oproj":
                        ins = v.scalar_tensor_tensor(out=X[b][:, :], in0=G.at(piece, l)[:, :], scalar=vec(l, V_BO),
                                                     in1=X[b][:, :], op0=ALU.add, op1=ALU.add)
                    else:
                        ins = v.tensor_tensor(X[b][:, :], X[b][:, :], G.at(piece, l)[:, :], ALU.add)
                    ins.then_inc(G.free(piece, l), 1)
                    dve.wait_ge(G.free(piece, l), G.read(piece, l))
                    dve.sem_inc(x_ready[b], 1)
                elif s == "ffn":
                    c = at[0]
                    dve.wait_ge(silu_ready[b], FC * l + c + 1)
                    v.tensor_tensor(SG[b][:, c, :], SG[b][:, c, :], T.at(piece, l)[:, 512:1024], ALU.mult)\
                        .then_inc(T.free(piece, l), 1)

            turns(dve, "dve", do)

            dve.wait_ge(tg_ready, 1)
            dve.wait_ge(s_late, N_LATE)
            for b in range(B):
                normed_rms(b, LAYERS, 1, uv(U_NF))
                dve.wait_ge(h_ready[b], 3 * LAYERS + 1)
                v.scalar_tensor_tensor(out=XO[b][:, :], in0=HN[b][:, :], scalar=TG[:, 0:1], in1=XO[b][:, :],
                                       op0=ALU.mult, op1=ALU.add).then_inc(xo_ready[b], 1)

            dve.wait_ge(s_late, N_LATE)
            qs = [0]

            def step(ins):
                ins.then_inc(q_step, 1)
                qs[0] += 1
                dve.wait_ge(q_step, qs[0])

            step(v.reciprocal(SC[:, 0:2], XSC[:, :]))
            step(v.tensor_tensor(SC[:, 2:3], XSC[:, 0:1], XSC[:, 1:2], ALU.mult))

            def quantise(dst, src, scale, width, q8, done):
                a, m = QT[0][:, 0:width], QT[1][:, 0:width]
                lo, hi = q8[0][:, 0:width], q8[1][:, 0:width]
                step(v.tensor_scalar(a, src, scale, None, ALU.mult))
                step(v.tensor_scalar(hi, a, 0.5, None, ALU.mult, saturate=False))
                step(v.tensor_scalar(m, a, -1.0, None, ALU.mult))
                step(v.tensor_tensor(m, a, m, ALU.max))
                step(v.tensor_scalar(m, m, FP8_MAX, None, ALU.is_gt))
                step(v.tensor_scalar(a, a, FP8_MAX, -FP8_MAX, ALU.min, ALU.max))
                step(v.tensor_copy(lo, a, saturate=False))
                step(v.scalar_tensor_tensor(out=a, in0=hi, scalar=2.0, in1=lo, op0=ALU.mult, op1=ALU.subtract))
                step(v.tensor_tensor(a, a, m, ALU.mult))
                ins = v.tensor_tensor(dst, a, lo, ALU.add)
                ins.then_inc(done, 1)
                dve.wait_ge(done, 1)

            quantise(KQ[:, :], KW[:, :], SC[:, 1:2], P, QK8, s_kq)
            for b in range(B):
                centre(b, 1, XO[b])
            for b in range(B):
                normed(b, 1, HB[b], ln_out[b])
                dve.wait_ge(ln_out[b], 1)
                quantise(XQ[b][:, :], HB[b][:, :], SC[:, 0:1], L, Q8, x_q[b])
            for b in range(B):
                u = ("dense", b)
                dve.wait_ge(G.full(u), G.count(u))
                v.tensor_scalar(YB[b][:, :], G.at(u)[:, :], SC[:, 2:3], None, ALU.mult).then_inc(G.free(u), 1)
                dve.wait_ge(G.free(u), G.read(u))
                v.tensor_scalar(YB[b][:, :], YB[b][:, :], QBIAS[:, 0:1], None, ALU.add).then_inc(y_step[b], 1)
                dve.wait_ge(y_step[b], 1)
                v.scalar_tensor_tensor(out=XO[b][:, :], in0=YB[b][:, :], scalar=TG[:, 2:3], in1=XO[b][:, :],
                                       op0=ALU.mult, op1=ALU.add).then_inc(xo_ready[b], 1)

            dve.wait_ge(s_interp, 48)
            for b in range(B):
                centre(b, 2, XO[b])
            for b in range(B):
                normed(b, 2, HN[b], ln_out[b])
            for b in range(B):
                u = ("xvs", b)
                dve.wait_ge(G.full(u), G.count(u))
                v.tensor_tensor(VS1[b][:, :], G.at(u)[0:S, 0:P], BVS[0:S, :], ALU.add).then_inc(G.free(u), 1)
                u = ("xvc", b)
                dve.wait_ge(G.full(u), G.count(u))
                for t in range(NT):
                    ins = v.tensor_tensor(VC1[b][:, t, :], G.at(u)[:, t * P:(t + 1) * P], BVC[:, :], ALU.add)
                ins.then_inc(G.free(u), 1)
                u = ("s1", b)
                dve.wait_ge(G.full(u), G.count(u))
                v.tensor_reduce(ST1[b][:, 0, :], G.at(u)[:, 0:NT * S].rearrange("p (t k) -> p t k", t=NT),
                                AX.X, ALU.max).then_inc(y_step[b], 1)
                dve.wait_ge(y_step[b], 2)
                v.tensor_scalar(ST1[b][:, 1, :], ST1[b][:, 0, :], -SCALE1, None, ALU.mult).then_inc(st_step[b], 1)
                dve.wait_ge(exp1_ready[b], NT)
                v.reciprocal(ST1[b][:, 3, :], ST1[b][:, 2, :]).then_inc(G.free(u), 1)
                dve.wait_ge(G.free(u), G.read(u))
                v.tensor_tensor(P1[b][:, :, :], P1[b][:, :, :],
                                ST1[b][:, 3, :].rearrange("p (t o) -> p t o", o=1).broadcast_to([P, NT, S]),
                                ALU.mult).then_inc(p1_ready[b], 1)
                u = ("s2", b)
                dve.wait_ge(G.full(u), G.count(u))
                v.tensor_reduce(ST2[b][0:S, 0:1], G.at(u)[0:S, :], AX.X, ALU.max).then_inc(st_step[b], 1)
                dve.wait_ge(st_step[b], 2)
                v.tensor_scalar(ST2[b][0:S, 1:2], ST2[b][0:S, 0:1], -SCALE1, None, ALU.mult).then_inc(st_step[b], 1)
                dve.wait_ge(exp2_ready[b], 1)
                v.reciprocal(ST2[b][0:S, 3:4], ST2[b][0:S, 2:3]).then_inc(G.free(u), 1)
                dve.wait_ge(G.free(u), G.read(u))
                v.tensor_scalar(P2[b][:, :], P2[b][:, :], ST2[b][0:S, 3:4], None, ALU.mult).then_inc(p2_ready[b], 1)
                u = ("s2c", b)
                dve.wait_ge(G.free(u), G.read(u))
                v.tensor_tensor(OD[b][:, :], RA[b][0][:, :], RB[b][0][:, :], ALU.subtract)\
                    .then_inc(y_step[b], 1)
                u = ("gate", b)
                dve.wait_ge(G.free(u), G.read(u))
                dve.wait_ge(y_step[b], 3)
                dve.sem_inc(mix_step[b], 1)
                dve.wait_ge(gate_ready[b], 1)
                v.tensor_tensor(HN[b][:, :], OD[b][:, :], RB[b][0][:, :], ALU.add).then_inc(y_step[b], 1)
                dve.wait_ge(y_step[b], 4)
                v.scalar_tensor_tensor(out=XO[b][:, :], in0=HN[b][:, :], scalar=TG[:, 1:2], in1=XO[b][:, :],
                                       op0=ALU.mult, op1=ALU.add).then_inc(xo_ready[b], 1)

            for b in range(B):
                centre(b, 3, XO[b])
            for b in range(B):
                normed(b, 3, HN[b], ln_out[b])
            for b in range(B):
                rt = RT[b]
                n = [0]

                def rstep(ins):
                    ins.then_inc(rt_step[b], 1)
                    n[0] += 1
                    dve.wait_ge(rt_step[b], n[0])

                u = ("router", b)
                dve.wait_ge(G.full(u), G.count(u))
                logits = rt[:, 0, :, :]
                v.tensor_copy(logits, G.at(u)[:, 0:NT * NE].rearrange("p (t e) -> p t e", e=NE))\
                    .then_inc(G.free(u), 1)
                dve.wait_ge(G.free(u), G.read(u))
                top = rt[:, 1, :, 0:1]
                rstep(v.tensor_reduce(top, logits, AX.X, ALU.max))
                eq = rt[:, 2, :, :]
                rstep(v.tensor_tensor(eq, logits, top.broadcast_to([P, NT, NE]), ALU.is_ge))
                left, pick = rt[:, 3, :, :], rt[:, 4, :, :]
                rstep(v.tensor_scalar(left[:, :, 0:1], eq[:, :, 0:1], -1.0, 1.0, ALU.mult, ALU.add))
                for e in range(1, NE):
                    rstep(v.tensor_tensor(pick[:, :, e:e + 1], eq[:, :, e:e + 1], left[:, :, e - 1:e], ALU.mult))
                    if e < NE - 1:
                        rstep(v.tensor_tensor(left[:, :, e:e + 1], left[:, :, e - 1:e], pick[:, :, e:e + 1],
                                              ALU.subtract))
                v.tensor_copy(OH[b][:, :, 0:1], eq[:, :, 0:1])
                rstep(v.tensor_copy(OH[b][:, :, 1:NE], pick[:, :, 1:NE]))
                for c in range(FC):
                    dve.wait_ge(es_ready[b], c + 1)
                    u = ("moe", b, c)
                    v.tensor_tensor(SG[b][:, c, :], SG[b][:, c, :], T.at(u)[:, 512:1024], ALU.mult)\
                        .then_inc(T.free(u), 1)
                acc, tmp = ON[b], OD[b]
                for e in range(NE):
                    u = ("edown", b, e)
                    dve.wait_ge(G.full(u), G.count(u))
                    v.tensor_tensor((tmp if e else acc)[:, :], ME[b][:, e, :], G.at(u)[:, :], ALU.mult)\
                        .then_inc(G.free(u), 1)
                    if e:
                        dve.wait_ge(G.free(u), G.read(u))
                        v.tensor_tensor(acc[:, :], acc[:, :], tmp[:, :], ALU.add).then_inc(ey_step[b], 1)
                        dve.wait_ge(ey_step[b], e)
                v.scalar_tensor_tensor(out=XO[b][:, :], in0=acc[:, :], scalar=TG[:, 3:4], in1=XO[b][:, :],
                                       op0=ALU.mult, op1=ALU.add).then_inc(xo_ready[b], 1)


def constants(BF):
    inv = (1.0 / 10000.0 ** (np.arange(0, HD, 2, dtype=np.float32) / np.float32(HD))).astype(np.float32)
    angle = np.arange(L, dtype=np.float32)[:, None] * inv[None, :]
    cos = np.cos(np.concatenate([angle, angle], 1)).astype(np.float32)
    sin = np.sin(np.concatenate([-angle, angle], 1)).astype(np.float32)
    bf = BF
    q = np.arange(P)
    pos = np.clip((np.arange(L, dtype=np.float32) + np.float32(0.5)) * np.float32(S / L) - np.float32(0.5),
                  0.0, S - 1).astype(np.float32)
    lo = np.floor(pos).astype(np.int32)
    hi = np.minimum(lo + 1, S - 1)
    w = (pos - lo.astype(np.float32)).astype(np.float32)
    interp = np.zeros((S, L), np.float32)
    np.add.at(interp, (lo, np.arange(L)), np.float32(1) - w)
    np.add.at(interp, (hi, np.arange(L)), w)
    return dict(
        cos=np.ascontiguousarray(np.repeat(cos.T, H, 0)),
        sin=np.ascontiguousarray(np.repeat(sin.T, H, 0)),
        idb=np.eye(P, dtype=bf), idf=np.eye(P, dtype=np.float32),
        onesd=np.full((P, P), 1.0 / P, np.float32),
        triq=np.where(q[None, :] <= q[:, None], 0.0, NEG).astype(bf),
        trik=np.where(q[:, None] <= q[None, :], 0.0, NEG).astype(bf),
        iota=np.broadcast_to(np.arange(S, dtype=np.float32), (P, S)).copy(),
        kidx=np.stack([q, q + LOOKBACK], 1).astype(np.float32),
        interp=interp,
    )


def kernel(**inputs):
    import numpy as _np
    import concourse.bacc as _bacc
    from concourse import mybir as _mybir
    from concourse.bass_utils import run_bass_kernel_spmd as _run

    a = {k: _np.asarray(x) for k, x in inputs.items()}
    d_h = _np.arange(P).reshape(H, HD).T.reshape(-1)
    rot = (_np.arange(HD) + HD // 2) % HD
    d_h_rot = _np.arange(P).reshape(H, HD)[:, rot].T.reshape(-1)
    out_rows = _np.arange(P).reshape(NG, HG, HD).transpose(1, 2, 0).reshape(-1)

    def cat(blocks):
        return _np.ascontiguousarray(_np.concatenate(blocks, 1))

    wqkv, bqkv = a["L0_xattn_Wqkv"], a["L0_xattn_bqkv"]
    w1, w2, w3, bv, vec = [], [], [], [], []
    for l in range(LAYERS):
        wq, wk, wv = wqkv[l, :P], wqkv[l, P:2 * P], wqkv[l, 2 * P:]
        bq, bk = bqkv[l, :P], bqkv[l, P:2 * P]
        w1.append(cat([wq[d_h].T, wq[d_h_rot].T, wk[d_h].T, wk[d_h_rot].T, wv.T]))
        bv.append(_np.broadcast_to(bqkv[l, 2 * P:], (P, P)).copy())
        wkv = a["L0_xattn_Wkv_c"][l]
        w2.append(cat([a["L0_xattn_Wo"][l][:, out_rows].T, a["L0_xattn_Wq_c"][l][d_h].T,
                       wkv[:P][d_h].T, wkv[P:].T]))
        w3.append(cat([a["L0_xattn_Wo_c"][l][:, out_rows].T, a["L0_xattn_Wg"][l].T, a["L0_xattn_Wu"][l].T]
                      + [a["L0_xattn_Wd"][l][:, c * P:(c + 1) * P].T for c in range(FC)]))
        vec += [a["L0_xattn_n1"][l], a["L0_xattn_n2"][l], a["L0_xattn_n3"][l], a["L0_xattn_bo"][l],
                bq[d_h], bq[d_h_rot], bk[d_h], bk[d_h_rot]]
    w1.append(w1[0])
    w2.append(w2[0])
    bv.append(bv[0])
    seg = a["itok_BxS_0_255"].reshape(-1)
    wg = a["L1_xattn_Wg"]
    wvx, wp = a["L1_ffn_w_v"], a["L1_ffn_w_proj"]
    arrays = dict(
        x=_np.ascontiguousarray(a["x"].transpose(0, 2, 1)),
        ctx=_np.ascontiguousarray(a["ctx_1024"].reshape(B * S, P).T),
        segr=_np.ascontiguousarray(_np.broadcast_to(seg, (S, B * L))),
        segc=_np.ascontiguousarray(seg.reshape(B * NT, P).T),
        gates=_np.broadcast_to(_np.concatenate([a["g_xattn"], a["g_ffn"]]), (P, 4)).copy(),
        w1=_np.stack(w1), w2=_np.stack(w2), w3=_np.stack(w3), bv=_np.stack(bv),
        vec=_np.ascontiguousarray(_np.stack(vec, 1)),
        uv=_np.stack([a["L0_xattn_nf"], a["L1_xattn_bq_c"], a["L1_xattn_bk_s"],
                      a["L1_xattn_bq_s"], a["L1_xattn_bk_c"], a["L1_xattn_bg"]], 1),
        qbias=_np.ascontiguousarray(a["L0_ffn_bias"].reshape(P, 1)),
        kw=_np.ascontiguousarray(a["L0_ffn_kernel"]),
        xsc=_np.broadcast_to(_np.concatenate([a["L0_ffn_input_scale"], a["L0_ffn_kernel_scale"]]), (P, 2)).copy(),
        wx=cat([a["L1_xattn_" + n].T for n in ("Wq_c", "Wk_s", "Wv_s", "Wq_s", "Wk_c", "Wv_c")]
               + [wg[:, :P].T, wg[:, P:].T]),
        bvs=_np.broadcast_to(a["L1_xattn_bv_s"], (P, P)).copy(),
        bvc=_np.broadcast_to(a["L1_xattn_bv_c"], (P, P)).copy(),
        wr=_np.ascontiguousarray(a["L1_ffn_w_router"]),
        wv=_np.ascontiguousarray(wvx.transpose(1, 0, 2).reshape(P, -1)),
        wp=_np.ascontiguousarray(wp.reshape(NE, FC, P, P).transpose(2, 0, 1, 3).reshape(P, -1)),
        **constants(a["L0_ffn_kernel"].dtype))
    nc = _bacc.Bacc("TRN2", target_bir_lowering=False, num_devices=1)
    d = {}
    for name, arr in arrays.items():
        d[name] = nc.dram_tensor(f"in_{name}", arr.shape, _mybir.dt.from_np(arr.dtype), kind="ExternalInput").ap()
    out = nc.dram_tensor("out_t", (B, P, L), _mybir.dt.float32, kind="ExternalOutput").ap()
    build(nc, d, out)
    r = _run(nc, [{f"in_{k}": x for k, x in arrays.items()}], core_ids=[0])
    return _np.ascontiguousarray(r.results[0]["out_t"].transpose(0, 2, 1))
```

```python
from contextlib import ExitStack

import numpy as np
import concourse.bass as bass
from concourse import mybir

F32 = mybir.dt.float32
BF16 = mybir.dt.bfloat16
FP8 = mybir.dt.float8e4
I32 = mybir.dt.int32
ALU = mybir.AluOpType
ACT = mybir.ActivationFunctionType
AX = mybir.AxisListType

P = 128
B = 2
L = 512
NT = L // P
S = 77
H = 16
HD = P // H
HG = 4
NG = H // HG
LAYERS = 4
FC = 4
NE = 4
PARTS = 3
PRODUCTS = [(0, 0), (0, 1), (0, 2), (1, 0), (1, 1), (2, 0)]
PP = len(PRODUCTS)
KZ = 96
KM = KZ + PARTS
VW = 2 * HD
NEG = -1e30
LOOKBACK = 128
RMS_EPS = 1e-6
LN_EPS = 1e-5
SCALE = float(HD) ** -0.5
SCALE1 = float(P) ** -0.5
TWO_ONES = float(np.uint32(0x3F803F80).view(np.float32))
FP8_MAX = 240.0

V_N1, V_N2, V_N3, V_BO, V_BQ, V_BQR, V_BK, V_BKR = range(8)
NV = 8
W_Q, W_QR, W_K, W_KR, W_V = range(5)
W_O, W_QC, W_KC, W_VC = range(4)
W_OC, W_G, W_U, W_D = 0, 1, 1 + FC, 1 + 2 * FC
NW1, NW2, NW3 = 5, 4, 1 + 3 * FC
X_QC, X_KS, X_VS, X_QS, X_KC, X_VC, X_G1, X_G2 = range(8)
U_NF, U_BQC, U_BKS, U_BQS, U_BKC, U_BG = range(6)

PORTIONS = 2
PH = H // PORTIONS
S_UNITS = [(t, h, n) for p in range(PORTIONS) for t, n in ((0, 4), (1, 2), (2, 1), (3, 1))
           for h in range(p * PH, (p + 1) * PH, n)]
C_UNITS = [(t, h, 4) for p in range(PORTIONS) for t in range(NT) for h in range(p * PH, (p + 1) * PH, 4)]
SPLIT = (1, 0, 2)
A_SLOTS, C_SLOTS = 5, 2

AT = dict(lag=2.0, clag=1.0, norm1=0.0, rope=3.0, split=5.5, smax=16.73, smax_step=0.75, mrow_after=1.5,
          scores=38.18, scores_step=1.7, heads1=81.18, oproj=84.3, norm2=84.29, qc=87.79, kvc=65.07,
          csmax=95.79, csmax_step=0.73, cscores=108.79, cscores_step=1.2, heads2=124.87, ocproj=128.79,
          norm3=130.29, ffn=133.79, down=144.29)
PERIOD = 147.49
BEHIND = 32.8
TAIL = dict(nf=-2.7, ln1=4.5, dense=17.0, ln2=20.5, x=27.0, s1=33.3, s2=34.0, p1t=38.0, p2t=41.0, c2s=42.5,
            gate=48.0, ln3=55.33, router=60.04, spread=65.04, moe0=69.04, moe1=71.45, moe_step=7.0,
            edown0=101.45, edown1=105.32, edown_step=9.27)


def chain(b):
    at = AT
    c = [(at["norm1"], "norm", 1), (at["rope"], "rope", 1), (at["rope"] + 1.0, "rope", 0), (at["rope"] + 2.0, "vals")]
    c += [(at["split"] + k, n, i) for k, (n, i) in enumerate((("high", 1), ("high", 0), ("low", 1), ("low", 0)))]
    c += [(at["smax"] + at["smax_step"] * i, "smax", i) for i in range(len(S_UNITS))]
    half = len(S_UNITS) // PORTIONS
    c += [(at["smax"] + at["smax_step"] * half * (p + 1) + at["mrow_after"], "mrow", 1, p) for p in range(PORTIONS)]
    t0, dt = at["scores"], at["scores_step"]
    for g in range(NG):
        c += [(t0 + dt * (A_SLOTS * g + v), "scores", g, v) for v in range(A_SLOTS)]
        c += [(t0 + dt * (A_SLOTS * (g + 1) + (at["lag"] if g < NG - 1 else 0)) + 0.3, "values", g)]
    c += [(at["heads1"], "heads", 1), (at["oproj"], "oproj"), (at["norm2"], "norm", 2), (at["qc"], "qc"),
          (at["qc"] + 1.0, "high", 2), (at["qc"] + 2.0, "low", 2)]
    c += [(at["csmax"] + at["csmax_step"] * i, "csmax", i) for i in range(len(C_UNITS))]
    half = len(C_UNITS) // PORTIONS
    c += [(at["csmax"] + at["csmax_step"] * half * (p + 1) + at["mrow_after"], "mrow", 2, p) for p in range(PORTIONS)]
    t0, dt = at["cscores"], at["cscores_step"]
    for g in range(NG):
        c += [(t0 + dt * (C_SLOTS * g + v), "cscores", g, v) for v in range(C_SLOTS)]
        c += [(t0 + dt * (C_SLOTS * (g + 1) + (at["clag"] if g < NG - 1 else 0)) + 0.3, "cvalues", g)]
    c += [(at["heads2"], "heads", 2), (at["ocproj"], "ocproj"), (at["norm3"], "norm", 3)]
    c += [(at["ffn"] + 2.4 * i, "ffn", i) for i in range(FC)] + [(at["down"], "down")]
    if b == 0:
        c += [(at["kvc"], "kvc"), (at["kvc"] + 1.5, "kchigh"), (at["kvc"] + 2.5, "kclow")]
    else:
        c += [(at["rope"] + 3.5, "w1"), (at["qc"] + 0.5, "w2"), (at["down"] + 1.0, "w3")]
    return [(t, (n[0], b) + tuple(n[1:])) for t, *n in c]


def tail(b):
    at = TAIL
    c = [(at["nf"], "nf"), (at["ln1"], "mean", 1), (at["ln1"] + 2.5, "var", 1), (at["dense"], "dense"),
         (at["ln2"], "mean", 2), (at["ln2"] + 2.5, "var", 2)]
    c += [(at["x"] + k, n) for k, n in ((0.0, "xqc"), (1.0, "xks"), (1.5, "xkc"), (2.5, "xqs"), (3.0, "xvs"),
                                        (3.5, "xvc"))]
    c += [(at["s1"], "s1"), (at["s2"], "s2"), (at["p1t"], "p1t"), (at["p2t"], "p2t"), (at["c2s"], "c2s"),
          (at["c2s"] + 1.5, "s2c0"), (at["c2s"] + 3.0, "s2c"), (at["gate"], "gate"),
          (at["ln3"], "mean", 3), (at["ln3"] + 2.5, "var", 3), (at["router"], "router")]
    c += [(at["spread"] + 0.8 * e, "spread", e) for e in range(NE)]
    moe, down = (at["moe0"], at["edown0"]) if b == 0 else (at["moe1"], at["edown1"])
    c += [(moe + at["moe_step"] * i, "moe", i) for i in range(FC)]
    c += [(down + at["edown_step"] * e, "edown", e) for e in range(NE)] + [(down + 4 * at["edown_step"] + 1.0, "out")]
    c += [(-2.0, "late")] if b == 0 else [(-10.0, "late")]
    return [(t, (n[0], b) + tuple(n[1:])) for t, *n in c]


LATER = {("act", "heads"): 0.0, ("act", "kvc"): 0.0, ("dve", "mrow"): 0.0, ("act", "s1"): 2.26,
         ("act", "s2"): 1.8, ("dve", "p1t"): -1.0, ("dve", "p2t"): -1.0, ("dve", "spread"): 1.2,
         ("pe", "norm"): 1.3, ("act", "norm"): 1.8, ("dve", "norm"): 2.5, ("dve", "rope"): 0.3,
         ("dve", "vals"): 0.3, ("pe", "mrow"): 1.0, ("act", "mrow"): 1.5, ("sp", "mrow"): 1.5,
         ("act", "scores"): 0.5, ("act", "cscores"): 0.5, ("act", "values"): 0.8, ("sp", "values"): 1.0,
         ("act", "cvalues"): 0.8, ("sp", "cvalues"): 1.0, ("dve", "heads"): 1.2, ("dve", "oproj"): 0.8,
         ("dve", "ocproj"): 0.8, ("dve", "smax"): 0.3, ("dve", "csmax"): 0.3, ("dve", "qc"): 0.5,
         ("dve", "high"): 0.7, ("dve", "low"): 0.7, ("pool", "high"): 0.5, ("pool", "low"): 0.5,
         ("pool", "values"): 1.0, ("pool", "cvalues"): 1.0, ("pool", "kchigh"): 0.5, ("pool", "kclow"): 0.5,
         ("sp", "high"): 0.5, ("sp", "low"): 0.5, ("act", "ffn"): 0.5, ("dve", "ffn"): 1.0,
         ("dve", "down"): 0.8}
TAIL_LATER = {"pe": 0.0, "act": 0.6, "dve": 1.2, "pool": 0.0, "sp": 0.0}


def order(engine):
    at = []
    for b in range(B):
        for t, piece in chain(b):
            t += BEHIND * b + LATER.get((engine, piece[0]), 0.0)
            laps = int(t // PERIOD)
            assert laps in (0, 1)
            at.append((t - laps * PERIOD, laps, piece))
    return [(piece, laps) for _, laps, piece in sorted(at, key=lambda x: x[0])]


def final(engine):
    at = []
    for b in range(B):
        for t, piece in chain(b):
            t += BEHIND * b + LATER.get((engine, piece[0]), 0.0) - PERIOD
            if t >= 0:
                at.append((t, piece, LAYERS - 1))
        for t, piece in tail(b):
            t += BEHIND * b + LATER.get((engine, piece[0]), TAIL_LATER[engine])
            at.append((t, piece, None))
    return [(piece, layer) for _, piece, layer in sorted(at, key=lambda x: x[0])]


TAIL_RING = {"s1": "G", "s2": "O", "edown": "GO", "moe": "T"}
AFTER = {piece for b in range(B) for _, piece in tail(b)}


def tail_ring(piece):
    r = TAIL_RING.get(piece[0], "Q")
    return r[piece[2] % len(r)] if len(r) > 1 else r


def uses_of(piece):
    n, b = piece[:2]
    if piece in AFTER:
        return [] if n in ("late", "out") else [(tail_ring(piece), piece, "")]
    if n in ("norm", "mrow"):
        return [("G", piece, "act")]
    if n in ("oproj", "ocproj", "down", "vals", "qc"):
        return [("G", piece, "dve")]
    if n == "kvc":
        return [("G", ("kc", 0), "act"), ("G", ("vc", 0), "act")]
    if n in ("rope", "ffn"):
        return [("T", piece, "dve")]
    if n in ("scores", "cscores"):
        return [("T", piece, "act")]
    if n in ("smax", "csmax"):
        return [("Q", piece, "dve")]
    if n in ("values", "cvalues"):
        return [("O", piece, "act")]
    return []


class Ring:

    def __init__(self, name, slots, filled, freed, before=()):
        self.slots, self.filled, self.freed = slots, filled, freed
        turn = [(u, laps) for piece, laps in order("pe") for k, u, _ in uses_of(piece) if k == name]
        self.before = {u: i for i, u in enumerate(before)}
        self.turn = {u: (i, laps) for i, (u, laps) in enumerate(turn)}
        self.size = len(turn)
        last = [u for piece, _ in final("pe") for k, u, _ in uses_of(piece) if k == name]
        self.last = {u: i for i, u in enumerate(last)}
        assert len(before) % len(slots) == 0 and self.size % len(slots) == 0

    def number(self, u, layer=0):
        n = len(self.before)
        if u in self.before:
            return self.before[u]
        if u in AFTER:
            return n + LAYERS * self.size + self.last[u]
        i, laps = self.turn[u]
        if isinstance(layer, int) and layer + laps == LAYERS:
            return n + LAYERS * self.size + self.last[u]
        return layer, n + laps * self.size + i

    def slot(self, u, layer=0):
        n = self.number(u, layer)
        return (n if isinstance(n, int) else n[1]) % len(self.slots)

    def at(self, u, layer=0):
        return self.slots[self.slot(u, layer)]

    def full(self, u, layer=0):
        return self.filled[self.slot(u, layer)]

    def free(self, u, layer=0):
        return self.freed[self.slot(u, layer)]

    def count(self, u, layer=0, more=1):
        n = self.number(u, layer)
        if isinstance(n, int):
            return n // len(self.slots) + more
        return n[0] * (self.size // len(self.slots)) + (n[1] // len(self.slots) + more)

    def read(self, u, layer=0):
        return self.count(u, layer, 2)


class Exponentials:

    def __init__(self, n):
        self.n = n
        self.turn = [(piece, laps) for piece, laps in order("pe") if piece[0] in ("scores", "cscores")]
        self.where = {piece: i for i, (piece, _) in enumerate(self.turn)}
        self.last = [piece for piece, laps in self.turn if laps]
        assert len(self.turn) % n == 0

    def position(self, piece, layer):
        i = self.where[piece]
        if isinstance(layer, int) and layer + self.turn[i][1] == LAYERS:
            return self.last.index(piece)
        return i

    def buffer(self, piece, layer):
        return self.position(piece, layer) % self.n

    def before(self, piece, layer):
        i = self.position(piece, layer) - self.n
        turn = layer + self.turn[self.where[piece]][1]
        if i < 0:
            i, turn = i + len(self.turn), turn - 1
        elif isinstance(turn, int) and turn == LAYERS:
            i = self.where[self.last[i]]
        if isinstance(turn, int) and turn < 0:
            return None
        former, laps = self.turn[i]
        return (former[0].replace("scores", "values"), former[1], former[2]), turn - laps


def build(nc, d, out):
    with ExitStack() as ctx:
        def sb(name, shape, dt=F32):
            return ctx.enter_context(nc.sbuf_tensor(name, shape, dt))

        def sem(name):
            return ctx.enter_context(nc.semaphore(name))

        def sems(name, n=B):
            return [sem(f"{name}{i}") for i in range(n)]

        def ring(key, name, n, width, before=()):
            slots = [ctx.enter_context(nc.psum_tensor(f"{name}{i}", [P, width], F32)) for i in range(n)]
            return Ring(key, slots, sems(f"{name}_filled", n), sems(f"{name}_freed", n), before)

        G = ring("G", "general", 1, 512, [(w, b, 0) for w in ("mean", "var") for b in range(B)])
        Q = ring("Q", "maxscores", 2, 512)
        T = ring("T", "wide", 2, 1024)
        O = ring("O", "headout", 1, 512)
        RINGS = dict(G=G, Q=Q, T=T, O=O)
        E = Exponentials(8)

        def after(piece):
            return RINGS[tail_ring(piece)]

        X = [sb(f"x{b}", [P, L]) for b in range(B)]
        HN = [sb(f"hn{b}", [P, L]) for b in range(B)]
        RA = [[sb(f"ra{b}{i}", [P, L]) for i in range(2)] for b in range(B)]
        RB = [[sb(f"rb{b}{i}", [P, L]) for i in range(2)] for b in range(B)]
        RS = [RA[b][0] for b in range(B)]
        PART = [[sb(f"part{b}{i}", [P, PARTS, L], BF16) for i in range(2)] for b in range(B)]
        QST = [sb(f"qstack{b}", [P, H, L], BF16) for b in range(B)]
        KST = [sb(f"kstack{b}", [P, H, L], BF16) for b in range(B)]
        KC32 = sb("kc32", [P, B * S])
        KCREST = sb("kcrest", [P, B * S])
        KCPART = sb("kcpart", [P, PARTS, B * S], BF16)
        KCST = sb("kcstack", [KM, H, B * S], BF16)
        VA = [sb(f"va{b}", [P, NT, H + 1, VW]) for b in range(B)]
        VCA = sb("vca", [S, B, H + 1, VW])
        MX = [sb(f"mx{b}", [P, PORTIONS, NT, PH]) for b in range(B)]
        MREST = [sb(f"mrest{b}", [P, PORTIONS, NT, PH]) for b in range(B)]
        MPART = [sb(f"mpart{b}", [P, PORTIONS, NT, PARTS, PH], BF16) for b in range(B)]
        MT = [sb(f"mt{b}", [PARTS * PH, PORTIONS, L], BF16) for b in range(B)]
        PR = sb("prob", [P, E.n, 1024])
        OA = [sb(f"oa{b}", [P, NG, L]) for b in range(B)]
        ON = [sb(f"on{b}", [P, L]) for b in range(B)]
        OD = [sb(f"od{b}", [P, L]) for b in range(B)]
        SQR = ON
        SG = OA
        W1 = sb("w1", [P, NW1 * P])
        W2 = sb("w2", [P, NW2 * P])
        W3 = sb("w3", [P, NW3 * P])
        BV = sb("bv", [P, P])
        VEC = sb("vec", [P, LAYERS * NV])
        COS = sb("cos_t", [P, L])
        SIN = sb("sin_t", [P, L])
        IDB = sb("ident_bf", [P, P], BF16)
        IDF = sb("ident_f", [P, P])
        ONESD = sb("ones_d", [P, P])
        TRIQ = sb("tri_q", [P, P], BF16)
        TRIK = sb("tri_k", [P, P], BF16)
        CBQ = sb("cross_bias_q", [P, B * NT, S], BF16)
        CBK = sb("cross_bias_k", [S, B * L], BF16)
        SEGR = PR[0:S, 2, :].bitcast(I32)
        SEGC = sb("seg_cols", [P, B * NT], I32)
        SEGF = sb("seg_f", [P, 2, B * NT])
        IOTA = sb("iota", [P, S])
        KIDX = sb("kidx", [P, 2])
        CTX = sb("ctx", [P, B * S])
        EPS = sb("eps", [P, 2])
        GATES = sb("gates", [P, 4])
        TG = sb("tanh_gates", [P, 4])
        UV = sb("uvec", [P, 6])
        XSC = sb("xscales", [P, 2])
        QBIAS = sb("qbias", [P, 1], BF16)
        WR = sb("wr", [P, NE])
        MASKS = dict(segr=SEGR, segc=SEGC, kidx=KIDX, iota=IOTA)
        TILES = dict(vec=VEC, cos=COS, sin=SIN, idb=IDB, triq=TRIQ, trik=TRIK, ctx=CTX, gates=GATES,
                     uv=UV, idf=IDF, xsc=XSC, qbias=QBIAS, wr=WR)

        def carve(tile):
            flat = tile[:, :, :].rearrange("p h t -> p (h t)").bitcast(F32)
            at = [0]

            def take(rows, *shape, dt=F32):
                n = int(np.prod(shape)) * (4 if dt == F32 else 2 if dt == BF16 else 1) // 4
                v = flat[0:rows, at[0]:at[0] + n]
                v = v if dt == F32 else v.bitcast(dt)
                at[0] += n
                assert at[0] <= H * L // 2
                return v.rearrange("p (a c) -> p a c", a=shape[0]) if len(shape) == 2 else v
            return take
        in_q = [carve(QST[b]) for b in range(B)]
        in_k = [carve(KST[b]) for b in range(B)]
        XO = [in_q[b](P, L) for b in range(B)]
        in_x = [carve(QST[b]) for b in range(B)]
        for b in range(B):
            in_x[b](P, L)
        XM = [in_q[b](P, NE, L) for b in range(B)]
        QT = [[in_x[b](P, L) for i in range(2)] for b in range(B)]
        Q8 = [[in_x[b](P, L, dt=FP8) for i in range(2)] for b in range(B)]
        XQ = [in_x[b](P, L, dt=BF16) for b in range(B)]
        HB = [in_x[b](P, L, dt=BF16) for b in range(B)]
        YB = [in_x[b](P, L, dt=BF16) for b in range(B)]
        KS1 = [in_q[b](P, S) for b in range(B)]
        QS1 = [in_q[b](P, S) for b in range(B)]
        VS1 = [in_q[b](S, P) for b in range(B)]
        P1 = [in_q[b](P, NT, S) for b in range(B)]
        P2T = [in_q[b](P, NT, S) for b in range(B)]
        S2C0 = [in_q[b](S, P) for b in range(B)]
        RT = [in_q[b](P, 5 * NT * NE).rearrange("p (w t e) -> p w t e", t=NT, e=NE)
              for b in range(B)]
        VC1 = [OA[b][:, 0, :].rearrange("p (t d) -> p t d", t=NT) for b in range(B)]
        P1T = [OA[b][0:S, 1, :] for b in range(B)]
        P2 = [OA[b][0:S, 2, :] for b in range(B)]
        WX = in_k[0](P, 8 * P)
        WP = in_k[0](P, NE * FC * P)
        INTERP = in_k[0](S, L)
        BVS, BVC = in_k[0](P, P), in_k[0](P, P)
        KW = in_k[0](P, P, dt=BF16)
        KQ = in_k[0](P, P, dt=BF16)
        QK8 = [in_k[0](P, P, dt=FP8) for i in range(2)]
        WV = in_k[1](P, NE * 2 * FC * P)
        SC = sb("scales", [P, 3])
        ST1 = [sb(f"st1{b}", [P, 4, NT]) for b in range(B)]
        ST2 = [sb(f"st2{b}", [P, 4]) for b in range(B)]
        OH = [sb(f"oh{b}", [P, NT, NE], BF16) for b in range(B)]

        def me(b, e):
            return PART[b][e // PARTS][:, e % PARTS, :]

        s_first, s_segs, s_eps = sem("x_loaded"), sem("segments_loaded"), sem("eps_set")
        s_const, s_mask = sem("const_loaded"), sem("mask_steps")
        s_zeros, s_ones = sem("zeros_set"), sem("ones_set")
        s_w1, s_w2, s_w3, s_late = sem("w1_loaded"), sem("w2_loaded"), sem("w3_loaded"), sem("late_loaded")
        s_kw, s_wv, x_again = sem("kw_loaded"), sem("wv_loaded"), sems("x_again_loaded")
        x_ready, xo_ready = sems("x_ready"), sems("xo_ready")
        sq_ready, rs_ready, h_ready = sems("squares_ready"), sems("rstd_ready"), sems("h_ready")
        rope_ready = sems("rope_ready")
        part1, rest1, part2, part3 = (sems(n) for n in ("part1_ready", "rest1_ready", "part2_ready", "part3_ready"))
        kc_part1, kc_rest1, kc_part2, kc_part3 = (sem(n) for n in ("kcpart1", "kcrest1", "kcpart2", "kcpart3"))
        q_landed, k_landed, kc_landed = sems("q_landed"), sems("k_landed"), sem("kc_landed")
        m_split = sems("maximum_split")
        m_landed = [sems(f"maximum_landed{p}_") for p in range(PORTIONS)]
        num_landed, den_landed = sems("numerators_landed"), sems("denominators_landed")
        den_step, o_ready = sems("denominator_step"), sems("heads_ready")
        silu_ready = sems("silu_ready")
        ln_sq, ln_rs, ln_out = sems("ln_squares"), sems("ln_rstd"), sems("ln_out")
        tg_ready = sem("tanh_ready")
        q_step, y_step, s_kq = sem("quantise_step"), sems("dense_step"), sem("kq_ready")
        x_q = sems("xq_ready")
        st_step, p1_ready, p2_ready = sems("softmax_step"), sems("p1_ready"), sems("p2_ready")
        exp1_ready, exp2_ready = sems("exp1_ready"), sems("exp2_ready")
        gate_ready = sems("gate_ready")
        rt_step, xm_ready, es_ready = sems("router_step"), sems("masked_ready"), sems("expert_silu_ready")
        ey_step = sems("expert_out_step")
        s_out = sem("out_stored")
        copy_turn = sem("copy_turn")

        block = ctx.enter_context(nc.Block())

        def words(stack, lo, hi):
            return stack[lo:hi, :, :].rearrange("p h t -> p (h t)").bitcast(F32)

        def w1(i):
            return W1[:, i * P:(i + 1) * P]

        def w2(i):
            return W2[:, i * P:(i + 1) * P]

        def w3(i):
            return W3[:, i * P:(i + 1) * P]

        def wx(i):
            return WX[:, i * P:(i + 1) * P]

        def uv(i):
            return UV[:, i:i + 1]

        def vec(l, i):
            return VEC[:, bass.ds(l * NV + i, 1)]

        def ctx_b(b):
            return CTX[:, b * S:(b + 1) * S]

        late = [(WX, "wx"), (BVS, "bvs"), (BVC, "bvc"), (INTERP, "interp"), (WP, "wp")]
        N_ZEROS = 4 * B + 2
        N_FIRST, N_SEGS, N_CONST = 16 * (B + 1), 16 * len(MASKS), 16 * len(TILES)
        N_LATE = 16 * len(late)

        def m_count(l, n, p):
            return 8 * PORTIONS * l + (4 * PORTIONS * (n - 1) + 4 * p)

        def turns(eng, name, do, rest):
            pieces = order(name)

            def skip(piece):
                for k, u, reader in uses_of(piece):
                    ring = RINGS[k]
                    if not ring.turn[u][1]:
                        continue
                    if name == "pe":
                        eng.wait_ge(ring.free(u, -1), ring.count(u, -1))
                        eng.sem_inc(ring.full(u, -1), 1)
                    elif name == reader:
                        eng.wait_ge(ring.full(u, -1), ring.count(u, -1))
                        eng.sem_inc(ring.free(u, -1), 1)

            for piece, laps in pieces:
                if laps:
                    skip(piece)
                else:
                    do(piece, 0)
            with eng.Fori(1, LAYERS) as turn:
                for piece, laps in pieces:
                    do(piece, turn - laps if laps else turn)
            for piece, l in final(name):
                if l is None:
                    rest(piece)
                else:
                    do(piece, l)

        def restack(eng, part, stack, side, i, landed):
            for r, pair in enumerate(PRODUCTS):
                if pair[side] == i:
                    eng.dma_start(stack[r * HD:(r + 1) * HD, :, :], part[:, i, :]).then_inc(landed, 16)

        def wait(eng, semaphore, value):
            eng.wait_ge(semaphore, value)
            if eng is nc.gpsimd:
                eng.sem_inc(copy_turn, 1)

        def restack_parts(eng, s, b, i, l, parts):
            ready = 3 * l + (SPLIT[i] + 1)
            part, stack = PART[b][i % 2], (QST, KST)[i == 1][b]
            landed = (k_landed if eng is nc.gpsimd else q_landed)[b]
            for n in parts:
                wait(eng, (part1, part2, part3)[n][b], ready)
                restack(eng, part, stack, i == 1, n, landed)

        def regroup(eng, b, tile, j, row, landed):
            r = 32 * j + row
            eng.dma_start(tile[b][32 * j:32 * j + 32, :], OA[b][r:r + HD, :, :]).then_inc(landed, 16)

        @block.sync
        def _(sp):
            for b in range(B):
                sp.dma_start(RB[b][0][:, :], d["x"][b]).then_inc(s_first, 16)
            sp.dma_start(ONESD[:, :], d["onesd"]).then_inc(s_first, 16)
            for name, tile in MASKS.items():
                sp.dma_start(tile[:, :], d[name]).then_inc(s_segs, 16)
            for name, tile in TILES.items():
                sp.dma_start(tile[:, :], d[name]).then_inc(s_const, 16)
            sp.dma_start(W1[:, :], d["w1"][0]).then_inc(s_w1, 16)
            sp.dma_start(BV[:, :], d["bv"][0]).then_inc(s_w1, 16)
            sp.dma_start(W2[:, :], d["w2"][0]).then_inc(s_w2, 16)
            sp.dma_start(W3[:, :], d["w3"][0]).then_inc(s_w3, 16)
            sp.wait_ge(s_zeros, N_ZEROS)

            def do(piece, l):
                s, b, *at = piece
                if s == "high" and at[0] != 1:
                    restack_parts(sp, s, b, at[0], l, (0,))
                elif s == "low":
                    restack_parts(sp, s, b, at[0], l, (2,) if at[0] == 1 else (1, 2))
                elif s == "mrow":
                    n, p = at
                    sp.wait_ge(G.free(piece, l), G.read(piece, l))
                    sp.dma_start(QST[b][KZ:KM, p * PH:(p + 1) * PH, :], MT[b][:, p, :]).then_inc(m_landed[p][b], 16)
                elif s in ("values", "cvalues") and at[0] == NG - 1:
                    sp.wait_ge(O.free(piece, l), O.read(piece, l))
                    for j in range(HG):
                        regroup(sp, b, OD, j, HD, den_landed[b])
                    regroup(sp, b, ON, 0, 0, den_landed[b])
                elif s == "w1":
                    sp.wait_ge(G.free(("vals", b), l), G.read(("vals", b), l))
                    sp.dma_start(W1[:, :], d["w1"][bass.ds(l + 1, 1)]).then_inc(s_w1, 16)
                    sp.dma_start(BV[:, :], d["bv"][bass.ds(l + 1, 1)]).then_inc(s_w1, 16)
                elif s == "w2":
                    sp.wait_ge(G.free(("qc", b), l), G.read(("qc", b), l))
                    sp.dma_start(W2[:, :], d["w2"][bass.ds(l + 1, 1)]).then_inc(s_w2, 16)
                elif s == "w3" and not isinstance(l, int):
                    sp.wait_ge(G.free(("down", b), l), G.read(("down", b), l))
                    sp.dma_start(W3[:, :], d["w3"][bass.ds(l + 1, 1)]).then_inc(s_w3, 16)

            def rest(piece):
                s, b = piece[:2]
                if s == "late":
                    u = ("cscores", b, NG - 1, C_SLOTS - 1)
                    sp.wait_ge(T.free(u, LAYERS - 1), T.read(u, LAYERS - 1))
                    sp.dma_start(XO[b], d["x"][b]).then_inc(x_again[b], 16)
                    if b == 0:
                        sp.dma_start(KW, d["kw"]).then_inc(s_kw, 16)
                        for tile, name in late:
                            sp.dma_start(tile, d[name]).then_inc(s_late, 16)
                    else:
                        sp.dma_start(WV, d["wv"]).then_inc(s_wv, 16)
                elif s == "out":
                    sp.wait_ge(xo_ready[b], 4)
                    sp.dma_start(out[b], XO[b]).then_inc(s_out, 16)

            turns(sp, "sp", do, rest)
            sp.wait_ge(s_out, 16 * B)
            sp.wait_ge(s_w1, 32 * (LAYERS + 1))
            sp.wait_ge(s_w2, 16 * (LAYERS + 1))

        @block.tensor
        def _(pe):
            for r in RINGS.values():
                for k in r.freed:
                    pe.sem_inc(k, 1)
            pe.wait_ge(s_first, N_FIRST)

            def general(u, l, lhsT, rhs, width=512):
                pe.wait_ge(G.free(u, l), G.count(u, l))
                pe.matmul(G.at(u, l)[0:lhsT.shape[1], 0:width], lhsT, rhs, start=True, stop=True)\
                  .then_inc(G.full(u, l), 1)

            for b in range(B):
                general(("mean", b, 0), 0, ONESD[:, :], RB[b][0][:, :])
            for b in range(B):
                pe.wait_ge(ln_sq[b], 1)
                general(("var", b, 0), 0, ONESD[:, :], SQR[b][:, :])
            pe.wait_ge(s_const, N_CONST)

            def do(piece, l):
                s, b, *at = piece
                if s == "norm":
                    pe.wait_ge(sq_ready[b], 3 * l + at[0])
                    general(piece, l, ONESD[:, :], SQR[b][:, :])
                elif s == "rope":
                    if at[0] == 1:
                        pe.wait_ge(h_ready[b], 3 * l + 1)
                        pe.wait_ge(s_w1, 32 * (l + 1))
                    w = (W_Q, W_K)[at[0]]
                    pe.wait_ge(T.free(piece, l), T.count(piece, l))
                    pe.matmul(T.at(piece, l)[:, 0:512], w1(w), HN[b][:, :], start=True, stop=True)
                    pe.matmul(T.at(piece, l)[:, 512:1024], w1(w + 1), HN[b][:, :], start=True, stop=True)\
                      .then_inc(T.full(piece, l), 1)
                elif s == "vals":
                    pe.wait_ge(G.free(piece, l), G.count(piece, l))
                    for t in range(NT):
                        mm = pe.matmul(G.at(piece, l)[:, t * P:(t + 1) * P], HN[b][:, t * P:(t + 1) * P], w1(W_V),
                                       start=True, stop=True)
                    mm.then_inc(G.full(piece, l), 1)
                elif s == "kvc":
                    pe.wait_ge(s_w2, 16 * (l + 1))
                    general(("kc", 0), l, w2(W_KC), CTX[:, :], B * S)
                    u = ("vc", 0)
                    pe.wait_ge(G.free(u, l), G.count(u, l))
                    for c in range(B):
                        mm = pe.matmul(G.at(u, l)[0:S, c * P:(c + 1) * P], ctx_b(c), w2(W_VC), start=True, stop=True)
                    mm.then_inc(G.full(u, l), 1)
                elif s == "smax":
                    max_scores(piece, l)
                elif s == "csmax":
                    max_cross_scores(piece, l)
                elif s == "mrow":
                    minus_maxima(piece, l)
                elif s == "scores":
                    self_scores(piece, l)
                elif s == "cscores":
                    cross_scores(piece, l)
                elif s in ("values", "cvalues"):
                    value_products(piece, l)
                elif s in ("oproj", "ocproj"):
                    n = 1 if s == "oproj" else 2
                    if s == "ocproj":
                        pe.wait_ge(s_w3, 16 * (l + 1))
                    elif b == 0:
                        pe.wait_ge(s_w2, 16 * (l + 1))
                    pe.wait_ge(o_ready[b], 2 * l + n)
                    general(piece, l, w2(W_O) if n == 1 else w3(W_OC), ON[b][:, :])
                elif s == "qc":
                    pe.wait_ge(h_ready[b], 3 * l + 2)
                    general(piece, l, w2(W_QC), HN[b][:, :])
                elif s == "ffn":
                    if at[0] == 0:
                        pe.wait_ge(h_ready[b], 3 * l + 3)
                    pe.wait_ge(T.free(piece, l), T.count(piece, l))
                    pe.matmul(T.at(piece, l)[:, 0:512], w3(W_G + at[0]), HN[b][:, :], start=True, stop=True)
                    pe.matmul(T.at(piece, l)[:, 512:1024], w3(W_U + at[0]), HN[b][:, :], start=True, stop=True)\
                      .then_inc(T.full(piece, l), 1)
                elif s == "down":
                    pe.wait_ge(G.free(piece, l), G.count(piece, l))
                    for c in range(FC):
                        u = ("ffn", b, c)
                        pe.wait_ge(T.free(u, l), T.read(u, l))
                        mm = pe.matmul(G.at(piece, l)[:, :], w3(W_D + c), SG[b][:, c, :],
                                       start=(c == 0), stop=(c == FC - 1))
                    mm.then_inc(G.full(piece, l), 1)

            def max_scores(u, l):
                _, b, i = u
                if i == 0:
                    pe.wait_ge(q_landed[b], 16 * (2 * PP + 1) * l + 16 * (PP + 1))
                    pe.wait_ge(k_landed[b], 16 * (PP - 1) * (l + 1))
                t, h0, n = S_UNITS[i]
                keys = (t + 1) * P
                pe.wait_ge(Q.free(u, l), Q.count(u, l))
                for k in range(n):
                    o = k * keys
                    pe.matmul(Q.at(u, l)[:, o:o + keys], QST[b][0:KZ, h0 + k, t * P:(t + 1) * P],
                              KST[b][0:KZ, h0 + k, 0:keys], start=True, stop=False)
                    mm = pe.matmul(Q.at(u, l)[:, o + keys - P:o + keys], IDB[:, :], TRIQ[:, :],
                                   start=False, stop=True)
                mm.then_inc(Q.full(u, l), 1)

            def max_cross_scores(u, l):
                _, b, i = u
                if i == 0:
                    pe.wait_ge(q_landed[b], 16 * (2 * PP + 1) * (l + 1))
                    pe.wait_ge(kc_landed, 16 * PP * (l + 1))
                t, h0, n = C_UNITS[i]
                pe.wait_ge(Q.free(u, l), Q.count(u, l))
                for k in range(n):
                    pe.matmul(Q.at(u, l)[:, k * S:(k + 1) * S], QST[b][0:KZ, h0 + k, t * P:(t + 1) * P],
                              KCST[0:KZ, h0 + k, b * S:(b + 1) * S], start=(k == 0), stop=False,
                              skip_group_check=True)
                pe.matmul(Q.at(u, l)[:, 0:n * S].rearrange("p (h k) -> p h k", k=S), IDB[:, :],
                          CBQ[:, b * NT + t:b * NT + t + 1, :].broadcast_to([P, n, S]),
                          start=False, stop=True, skip_group_check=True).then_inc(Q.full(u, l), 1)

            def minus_maxima(u, l):
                _, b, n, p = u
                pe.wait_ge(m_split[b], m_count(l, n, p) + 4)
                pe.wait_ge(G.free(u, l), G.count(u, l))
                for t in range(NT):
                    mm = pe.matmul(G.at(u, l)[0:PARTS * PH, t * P:(t + 1) * P],
                                   MPART[b][:, p, t, :, :].rearrange("p a h -> p (a h)"), IDB[:, :],
                                   start=True, stop=True)
                mm.then_inc(G.full(u, l), 1)

            def self_scores(u, l):
                _, b, g, v = u

                def product(bank, h, kt):
                    pe.matmul(bank[:, 0:L - kt * P], KST[b][0:KM, h, kt * P:(kt + 1) * P],
                              QST[b][0:KM, h, kt * P:L], start=True, stop=False)
                    return pe.matmul(bank[:, 0:P], IDB[:, :], TRIK[:, :], start=False, stop=True)

                if isinstance(l, int) and g == 0 and v == 0:
                    pe.wait_ge(s_mask, 8)
                    pe.wait_ge(s_ones, B + 1)
                if g % (NG // PORTIONS) == 0 and v == 0:
                    pe.wait_ge(m_landed[g // (NG // PORTIONS)][b], 16 * (2 * l + 1))
                slot = T.at(u, l)
                pe.wait_ge(T.free(u, l), T.count(u, l))
                for j in range(2) if v < 4 else range(4):
                    h = HG * g + (2 * (v % 2) + j if v < 4 else j)
                    if v < 2:
                        mm = product(slot[:, j * 512:(j + 1) * 512], h, 0)
                    elif v < 4:
                        product(slot[:, j * 512:j * 512 + 384], h, 1)
                        mm = product(slot[:, j * 512 + 384:(j + 1) * 512], h, 3)
                    else:
                        mm = product(slot[:, j * 256:(j + 1) * 256], h, 2)
                mm.then_inc(T.full(u, l), 1)

            def cross_scores(u, l):
                _, b, g, v = u
                if g % (NG // PORTIONS) == 0 and v == 0:
                    pe.wait_ge(m_landed[g // (NG // PORTIONS)][b], 16 * (2 * l + 2))
                pe.wait_ge(T.free(u, l), T.count(u, l))
                for j in range(2):
                    bank = T.at(u, l)[0:S, j * 512:(j + 1) * 512]
                    h = HG * g + 2 * v + j
                    pe.matmul(bank, KCST[0:KM, h, b * S:(b + 1) * S], QST[b][0:KM, h, :],
                              start=True, stop=False)
                    mm = pe.matmul(bank, IDB[0:S, 0:S], CBK[:, b * L:(b + 1) * L], start=False, stop=True)
                mm.then_inc(T.full(u, l), 1)

            def where(j, kt):
                if kt == 0:
                    return j // 2, (j % 2) * 512
                if kt == 2:
                    return 4, j * 256
                return 2 + j // 2, (j % 2) * 512 + (0 if kt == 1 else 384)

            def value_products(u, l):
                s, b, g = u
                name = "scores" if s == "values" else "cscores"
                slots = A_SLOTS if s == "values" else C_SLOTS
                if g == 0:
                    own = ("vals", b) if s == "values" else ("vc", 0)
                    pe.wait_ge(G.free(own, l), G.read(own, l))
                w = (name, b, g, slots - 1)
                pe.wait_ge(T.free(w, l), T.read(w, l))
                pe.wait_ge(O.free(u, l), O.count(u, l))
                for kt in range(NT if s == "values" else 1):
                    for j in range(HG):
                        h = HG * g + j
                        if s == "values":
                            v, c = where(j, kt)
                            probs = PR[:, E.buffer((name, b, g, v), l), c:c + L - kt * P]
                            operand = VA[b][:, kt, h:h + 2, :]
                        else:
                            probs = PR[0:S, E.buffer((name, b, g, j // 2), l), (j % 2) * 512:(j % 2 + 1) * 512]
                            operand = VCA[:, b, h:h + 2, :]
                        mm = pe.matmul(O.at(u, l)[32 * j:32 * j + 32, kt * P:L],
                                       operand.rearrange("p h c -> p (h c)"), probs,
                                       start=(kt == 0), stop=(kt == NT - 1 or s == "cvalues"))
                mm.then_inc(O.full(u, l), 1)

            def landed(*uses):
                for u in uses:
                    pe.wait_ge(after(u).free(u), after(u).read(u))

            def rest(u):
                s, b = u[:2]
                if s in ("late", "out"):
                    return
                R = after(u)
                qct, kct, k = RA[b][1], RB[b][1], (RA[b][0], RB[b][0])

                def product(lhsT, rhs, width=512, rows=P):
                    pe.wait_ge(R.free(u), R.count(u))
                    pe.matmul(R.at(u)[0:rows, 0:width], lhsT, rhs, start=True, stop=True).then_inc(R.full(u), 1)

                def tiles(each):
                    pe.wait_ge(R.free(u), R.count(u))
                    for t in range(NT):
                        mm = each(R.at(u), t, slice(t * P, (t + 1) * P))
                    mm.then_inc(R.full(u), 1)

                if s == "nf":
                    pe.wait_ge(sq_ready[b], 3 * LAYERS + 1)
                    product(ONESD[:, :], SQR[b][:, :])
                elif s == "mean":
                    pe.wait_ge(xo_ready[b], u[2])
                    product(ONESD[:, :], XO[b])
                elif s == "var":
                    pe.wait_ge(ln_sq[b], u[2] + 1)
                    product(ONESD[:, :], SQR[b][:, :])
                elif s == "dense":
                    pe.wait_ge(s_kq, 1)
                    pe.wait_ge(x_q[b], 1)
                    product(KQ, XQ[b])
                elif s == "xqc":
                    pe.wait_ge(ln_out[b], 2)
                    pe.wait_ge(s_late, N_LATE)
                    product(wx(X_QC), HN[b][:, :])
                elif s == "xks":
                    product(wx(X_KS), ctx_b(b), S)
                elif s == "xvs":
                    product(ctx_b(b), wx(X_VS), P, S)
                elif s == "xqs":
                    product(wx(X_QS), ctx_b(b), S)
                elif s == "xkc":
                    product(wx(X_KC), HN[b][:, :])
                elif s == "xvc":
                    tiles(lambda o, t, c: pe.matmul(o[:, c], HN[b][:, c], wx(X_VC), start=True, stop=True))
                elif s == "s1":
                    landed(("xqc", b), ("xks", b))
                    tiles(lambda o, t, c: pe.matmul(o[:, t * S:(t + 1) * S], qct[:, c], KS1[b],
                                                    start=True, stop=True))
                elif s == "s2":
                    landed(("xkc", b), ("xqs", b))
                    product(QS1[b], kct[:, :], rows=S)
                elif s == "p1t":
                    pe.wait_ge(p1_ready[b], 1)
                    tiles(lambda o, t, c: pe.transpose(o[0:S, c], P1[b][:, t, :], IDF[:, :]))
                elif s == "p2t":
                    pe.wait_ge(p2_ready[b], 1)
                    tiles(lambda o, t, c: pe.transpose(o[:, t * S:(t + 1) * S], P2[b][:, c], IDF[0:S, 0:S]))
                elif s == "c2s":
                    landed(("xvs", b), ("p1t", b))
                    product(VS1[b], P1T[b])
                elif s == "s2c0":
                    landed(("xvc", b), ("p2t", b))
                    tiles(lambda o, t, c: pe.matmul(o[0:S, 0:P], P2T[b][:, t, :], VC1[b][:, t, :],
                                                    start=(t == 0), stop=(t == NT - 1)))
                elif s == "s2c":
                    landed(("s2c0", b))
                    product(S2C0[b], INTERP)
                elif s == "gate":
                    landed(("c2s", b), ("s2c", b))
                    pe.wait_ge(R.free(u), R.count(u))
                    pe.matmul(R.at(u)[:, :], wx(X_G1), k[0][:, :], start=True, stop=False)
                    pe.matmul(R.at(u)[:, :], wx(X_G2), k[1][:, :], start=False, stop=True).then_inc(R.full(u), 1)
                elif s == "router":
                    pe.wait_ge(ln_out[b], 3)
                    tiles(lambda o, t, c: pe.matmul(o[:, t * NE:(t + 1) * NE], HN[b][:, c], WR[:, :],
                                                    start=True, stop=True))
                elif s == "spread":
                    pe.wait_ge(rt_step[b], 9)
                    tiles(lambda o, t, c: pe.matmul(o[:, c], OH[b][:, t, u[2]:u[2] + 1].broadcast_to([P, P]),
                                                    IDB[:, :], start=True, stop=True))
                elif s == "moe":
                    pe.wait_ge(xm_ready[b], NE)
                    pe.wait_ge(s_wv, 16)
                    pe.wait_ge(R.free(u), R.count(u))
                    for half in range(2):
                        for e in range(NE):
                            o = (e * 2 * FC + half * FC + u[2]) * P
                            mm = pe.matmul(R.at(u)[:, half * 512:(half + 1) * 512], WV[:, o:o + P],
                                           XM[b][:, e, :], start=(e == 0), stop=(e == NE - 1))
                    mm.then_inc(R.full(u), 1)
                elif s == "edown":
                    landed(*[("moe", b, c) for c in range(FC)])
                    pe.wait_ge(R.free(u), R.count(u))
                    for c in range(FC):
                        o = (u[2] * FC + c) * P
                        mm = pe.matmul(R.at(u)[:, :], WP[:, o:o + P], SG[b][:, c, :],
                                       start=(c == 0), stop=(c == FC - 1))
                    mm.then_inc(R.full(u), 1)

            turns(pe, "pe", do, rest)

        @block.scalar
        def _(act):
            act.wait_ge(s_eps, 2)
            loaded = [None]

            def logexp():
                if loaded[0] != "logexp":
                    nc.scalar.preload_act_table_set("natural_log_exp_and_others")
                    loaded[0] = "logexp"

            def root(u, b, l, eps, ready, R=G):
                logexp()
                act.wait_ge(R.full(u, l), R.count(u, l))
                nc.scalar.activation(RS[b][:, :], R.at(u, l)[:, :], ACT.Ln, bias=EPS[:, eps:eps + 1])\
                    .then_inc(R.free(u, l), 1)
                act.wait_ge(R.free(u, l), R.read(u, l))
                nc.scalar.activation(RS[b][:, :], RS[b][:, :], ACT.Exp, scale=-0.5).then_inc(ready, 1)

            def copy(u, l, dst, rows=P, width=512, view=None, R=G):
                act.wait_ge(R.full(u, l), R.count(u, l))
                src = view(R.at(u, l)) if view else R.at(u, l)[0:rows, 0:width]
                nc.scalar.activation(dst, src, ACT.Copy).then_inc(R.free(u, l), 1)

            def do(piece, l):
                s, b, *at = piece
                if s == "norm":
                    root(piece, b, l, 0, rs_ready[b])
                elif s == "kvc":
                    copy(("kc", 0), l, KC32[:, :], P, B * S)
                    copy(("vc", 0), l, VCA[:, :, 0:H, 0:HD],
                         view=lambda bank: bank[0:S, 0:B * P].rearrange("p (b h d) -> p b h d", b=B, h=H))
                elif s == "mrow":
                    if isinstance(l, int) and l == 0 and piece == ("mrow", 0, 1, 0):
                        nc.scalar.activation(TG[:, :], GATES[:, :], ACT.Tanh).then_inc(tg_ready, 1)
                        loaded[0] = "tanh"
                    copy(piece, l, MT[b][:, at[1], :], PARTS * PH, L)
                elif s in ("scores", "cscores"):
                    logexp()
                    rows = P if s == "scores" else S
                    former = E.before(piece, l)
                    if former:
                        act.wait_ge(O.full(*former), O.count(*former))
                    act.wait_ge(T.full(piece, l), T.count(piece, l))
                    nc.scalar.activation(PR[0:rows, E.buffer(piece, l), :], T.at(piece, l)[0:rows, :], ACT.Exp,
                                         scale=SCALE).then_inc(T.free(piece, l), 1)
                elif s in ("values", "cvalues"):
                    act.wait_ge(O.full(piece, l), O.count(piece, l))
                    nc.scalar.activation(OA[b][:, at[0], :], O.at(piece, l)[:, :], ACT.Copy)\
                        .then_inc(O.free(piece, l), 1)
                elif s == "heads":
                    n = at[0]
                    logexp()
                    act.wait_ge(den_landed[b], 16 * (HG + 1) * (2 * l + n))
                    nc.scalar.activation(OD[b][:, :], OD[b][:, :], ACT.Ln).then_inc(den_step[b], 1)
                    act.wait_ge(den_step[b], 4 * l + 2 * n - 1)
                    nc.scalar.activation(OD[b][:, :], OD[b][:, :], ACT.Exp, scale=-1.0).then_inc(den_step[b], 1)
                elif s == "ffn":
                    loaded[0] = "silu"
                    act.wait_ge(T.full(piece, l), T.count(piece, l))
                    nc.scalar.activation(SG[b][:, at[0], :], T.at(piece, l)[:, 0:512], ACT.Silu)\
                        .then_inc(silu_ready[b], 1)

            for b in range(B):
                root(("var", b, 0), b, 0, 1, ln_rs[b])
            act.wait_ge(s_const, N_CONST)
            def rest(u):
                s, b = u[:2]
                if s in ("late", "out"):
                    return
                R = after(u)

                def biased(dst, bias, width):
                    act.wait_ge(R.full(u), R.count(u))
                    nc.scalar.activation(dst, R.at(u)[:, 0:width], ACT.Identity, bias=uv(bias))\
                        .then_inc(R.free(u), 1)

                if s == "nf":
                    root(u, b, 0, 0, rs_ready[b], R)
                elif s == "var":
                    root(u, b, 0, 1, ln_rs[b], R)
                elif s == "xqc":
                    biased(RA[b][1][:, :], U_BQC, L)
                elif s == "xks":
                    biased(KS1[b], U_BKS, S)
                elif s == "xqs":
                    biased(QS1[b], U_BQS, S)
                elif s == "xkc":
                    biased(RB[b][1][:, :], U_BKC, L)
                elif s == "s1":
                    logexp()
                    act.wait_ge(st_step[b], 1)
                    for t in range(NT):
                        nc.scalar.activation(P1[b][:, t, :], R.at(u)[:, t * S:(t + 1) * S], ACT.Exp,
                                             scale=SCALE1, bias=ST1[b][:, 1, t:t + 1],
                                             accum_out=ST1[b][:, 2, t:t + 1]).then_inc(exp1_ready[b], 1)
                elif s == "s2":
                    logexp()
                    act.wait_ge(st_step[b], 3)
                    nc.scalar.activation(P2[b], R.at(u)[0:S, :], ACT.Exp, scale=SCALE1,
                                         bias=ST2[b][0:S, 1:2], accum_out=ST2[b][0:S, 2:3])\
                        .then_inc(exp2_ready[b], 1)
                elif s == "p1t":
                    copy(u, 0, P1T[b], S, L, R=R)
                elif s == "p2t":
                    copy(u, 0, P2T[b], view=lambda bank: bank[:, 0:NT * S].rearrange("p (t k) -> p t k", t=NT), R=R)
                elif s == "c2s":
                    copy(u, 0, RA[b][0][:, :], R=R)
                elif s == "s2c0":
                    copy(u, 0, S2C0[b], S, P, R=R)
                elif s == "s2c":
                    copy(u, 0, RB[b][0][:, :], R=R)
                elif s == "gate":
                    loaded[0] = "sigmoid"
                    act.wait_ge(R.full(u), R.count(u))
                    nc.scalar.activation(ON[b][:, :], R.at(u)[:, :], ACT.Sigmoid, bias=uv(U_BG))\
                        .then_inc(R.free(u), 1)
                elif s == "spread":
                    copy(u, 0, me(b, u[2]), R=R)
                elif s == "moe":
                    loaded[0] = "silu"
                    act.wait_ge(R.full(u), R.count(u))
                    nc.scalar.activation(SG[b][:, u[2], :], R.at(u)[:, 0:512], ACT.Silu).then_inc(es_ready[b], 1)

            turns(act, "act", do, rest)

        @block.gpsimd
        def _(pool):
            for b in range(B):
                for stack in (QST[b], KST[b]):
                    pool.memset(words(stack, 32, 64), 0.0).then_inc(s_zeros, 1)
                    pool.memset(words(stack, 64, KZ), 0.0).then_inc(s_zeros, 1)
            pool.memset(words(KCST, 32, 64), 0.0).then_inc(s_zeros, 1)
            pool.memset(words(KCST, 64, KZ), 0.0).then_inc(s_zeros, 1)
            pool.wait_ge(s_zeros, N_ZEROS)

            def do(piece, l):
                s, b, *at = piece
                if s in ("high", "low") and at[0] == 1:
                    restack_parts(pool, s, b, 1, l, (0,) if s == "high" else (1,))
                    if isinstance(l, int) and l == 0 and (s, b) == ("low", 0):
                        for stack in (*KST, KCST):
                            pool.memset(words(stack, KZ, KM), TWO_ONES).then_inc(s_ones, 1)
                elif s == "kchigh":
                    wait(pool, kc_part1, l + 1)
                    restack(pool, KCPART, KCST, 1, 0, kc_landed)
                elif s == "kclow":
                    for i, ready in ((1, kc_part2), (2, kc_part3)):
                        wait(pool, ready, l + 1)
                        restack(pool, KCPART, KCST, 1, i, kc_landed)
                elif s in ("values", "cvalues") and at[0] == NG - 1:
                    wait(pool, O.free(piece, l), O.read(piece, l))
                    for j in range(1, HG):
                        regroup(pool, b, ON, j, 0, num_landed[b])

            turns(pool, "pool", do, lambda piece: None)

        @block.vector
        def _(dve):
            v = nc.vector
            v.memset(EPS[:, 0:1], RMS_EPS).then_inc(s_eps, 1)
            v.memset(EPS[:, 1:2], LN_EPS).then_inc(s_eps, 1)
            dve.wait_ge(s_first, N_FIRST)

            def centre(b, n, src, R=G):
                u = ("mean", b, n)
                dve.wait_ge(R.full(u), R.count(u))
                v.tensor_tensor(OD[b][:, :], src[:, :], R.at(u)[:, :], ALU.subtract).then_inc(R.free(u), 1)
                dve.wait_ge(R.free(u), R.read(u))
                v.tensor_tensor(SQR[b][:, :], OD[b][:, :], OD[b][:, :], ALU.mult).then_inc(ln_sq[b], 1)

            def normed(b, n, dst, done):
                dve.wait_ge(ln_rs[b], n + 1)
                v.tensor_tensor(dst[:, :], OD[b][:, :], RS[b][:, :], ALU.mult).then_inc(done, 1)

            def squares(b):
                v.tensor_tensor(SQR[b][:, :], X[b][:, :], X[b][:, :], ALU.mult).then_inc(sq_ready[b], 1)

            for b in range(B):
                centre(b, 0, RB[b][0])
            for b in range(B):
                normed(b, 0, X[b], x_ready[b])
                dve.wait_ge(x_ready[b], 1)
                squares(b)
            dve.wait_ge(s_const, N_CONST)

            def set_up():
                for b in range(B):
                    v.memset(VA[b][:, :, 0:H, HD:VW], 1.0)
                    v.memset(VA[b][:, :, H, :], 0.0)
                v.memset(VCA[:, :, 0:H, HD:VW], 1.0)
                v.memset(VCA[:, :, H, :], 0.0)
                dve.wait_ge(s_segs, N_SEGS)
                allow = PR[0:S, 0, :]
                allow2 = PR[0:S, 1, :]
                v.tensor_scalar(allow, SEGR[:, :], KIDX[0:S, 0:1], None, ALU.is_ge).then_inc(s_mask, 1)
                v.tensor_scalar(SEGF[:, 0, :], SEGC[:, :], 1.0, None, ALU.mult).then_inc(s_mask, 1)
                dve.wait_ge(s_mask, 1)
                v.scalar_tensor_tensor(out=allow2, in0=SEGR[:, :], scalar=KIDX[0:S, 1:2], in1=allow,
                                       op0=ALU.is_lt, op1=ALU.mult).then_inc(s_mask, 1)
                dve.wait_ge(s_mask, 3)
                v.tensor_scalar(CBK[:, :], allow2, -1.0, -NEG, ALU.add, ALU.mult).then_inc(s_mask, 1)
                tiles = B * NT
                qa = PR[:, 3, 0:tiles * S].rearrange("p (t k) -> p t k", t=tiles)
                qb = PR[:, 4, 0:tiles * S].rearrange("p (t k) -> p t k", t=tiles)
                seg = SEGF[:, 0, :].rearrange("p (t o) -> p t o", o=1).broadcast_to([P, tiles, S])
                idx = IOTA[:, :].rearrange("p (o k) -> p o k", o=1).broadcast_to([P, tiles, S])
                v.tensor_tensor(qa, idx, seg, ALU.is_le).then_inc(s_mask, 1)
                dve.wait_ge(s_mask, 5)
                v.tensor_tensor(qb, seg, idx, ALU.subtract).then_inc(s_mask, 1)
                dve.wait_ge(s_mask, 6)
                v.scalar_tensor_tensor(out=qb, in0=qb, scalar=float(LOOKBACK), in1=qa,
                                       op0=ALU.is_lt, op1=ALU.mult).then_inc(s_mask, 1)
                dve.wait_ge(s_mask, 7)
                v.tensor_scalar(CBQ[:, :, :], qb, -1.0, -NEG, ALU.add, ALU.mult).then_inc(s_mask, 1)

            def normed_rms(b, l, n, col):
                dve.wait_ge(rs_ready[b], 3 * l + n)
                v.scalar_tensor_tensor(out=HN[b][:, :], in0=X[b][:, :], scalar=col, in1=RS[b][:, :],
                                       op0=ALU.mult, op1=ALU.mult).then_inc(h_ready[b], 1)

            def split_maxima(piece, l):
                _, b, n, p = piece
                name, units = ("smax", S_UNITS) if n == 1 else ("csmax", C_UNITS)
                last = (name, b, len(units) // PORTIONS * (p + 1) - 1)
                dve.wait_ge(Q.free(last, l), Q.read(last, l))
                mx, rest, part = MX[b][:, p], MREST[b][:, p], MPART[b][:, p]
                v.tensor_scalar(part[:, :, 0, :], mx, -1.0, None, ALU.mult).then_inc(m_split[b], 1)
                dve.wait_ge(m_split[b], m_count(l, n, p) + 1)
                v.scalar_tensor_tensor(out=rest, in0=mx, scalar=-1.0, in1=part[:, :, 0, :],
                                       op0=ALU.mult, op1=ALU.subtract).then_inc(m_split[b], 1)
                dve.wait_ge(m_split[b], m_count(l, n, p) + 2)
                v.tensor_copy(part[:, :, 1, :], rest).then_inc(m_split[b], 1)
                dve.wait_ge(m_split[b], m_count(l, n, p) + 3)
                v.tensor_tensor(part[:, :, 2, :], rest, part[:, :, 1, :], ALU.subtract).then_inc(m_split[b], 1)

            def do(piece, l):
                s, b, *at = piece
                if s == "norm":
                    normed_rms(b, l, at[0], vec(l, (V_N1, V_N2, V_N3)[at[0] - 1]))
                elif s == "rope":
                    i = at[0]
                    c0, c1 = ((V_BQ, V_BQR), (V_BK, V_BKR))[i]
                    dve.wait_ge(T.full(piece, l), T.count(piece, l))
                    v.scalar_tensor_tensor(out=RA[b][i][:, :], in0=T.at(piece, l)[:, 0:512], scalar=vec(l, c0),
                                           in1=COS[:, :], op0=ALU.add, op1=ALU.mult)
                    v.scalar_tensor_tensor(out=RB[b][i][:, :], in0=T.at(piece, l)[:, 512:1024], scalar=vec(l, c1),
                                           in1=SIN[:, :], op0=ALU.add, op1=ALU.mult).then_inc(T.free(piece, l), 1)
                    dve.wait_ge(T.free(piece, l), T.read(piece, l))
                    v.tensor_tensor(RA[b][i][:, :], RA[b][i][:, :], RB[b][i][:, :], ALU.add)\
                        .then_inc(rope_ready[b], 1)
                elif s == "vals":
                    dve.wait_ge(G.full(piece, l), G.count(piece, l))
                    for t in range(NT):
                        ins = v.tensor_tensor(VA[b][:, t, 0:H, 0:HD],
                                              G.at(piece, l)[:, t * P:(t + 1) * P]
                                              .rearrange("p (h d) -> p h d", h=H),
                                              BV[:, :].rearrange("p (h d) -> p h d", h=H), ALU.add)
                    ins.then_inc(G.free(piece, l), 1)
                elif s == "qc":
                    dve.wait_ge(G.full(piece, l), G.count(piece, l))
                    v.tensor_copy(PART[b][0][:, 0, :], G.at(piece, l)[:, :]).then_inc(part1[b], 1)
                    dve.wait_ge(part1[b], 3 * l + SPLIT[2] + 1)
                    v.tensor_tensor(RB[b][0][:, :], G.at(piece, l)[:, :], PART[b][0][:, 0, :], ALU.subtract)\
                        .then_inc(G.free(piece, l), 1)
                elif s == "high" and at[0] < 2:
                    i = at[0]
                    dve.wait_ge(rope_ready[b], 2 * l + SPLIT[i] + 1)
                    v.tensor_copy(PART[b][i][:, 0, :], RA[b][i][:, :]).then_inc(part1[b], 1)
                    dve.wait_ge(part1[b], 3 * l + SPLIT[i] + 1)
                    v.tensor_tensor(RB[b][i][:, :], RA[b][i][:, :], PART[b][i][:, 0, :], ALU.subtract)\
                        .then_inc(rest1[b], 1)
                elif s == "low":
                    i = at[0] % 2
                    if at[0] < 2:
                        dve.wait_ge(rest1[b], 2 * l + SPLIT[i] + 1)
                    else:
                        dve.wait_ge(G.free(("qc", b), l), G.read(("qc", b), l))
                    v.tensor_copy(PART[b][i][:, 1, :], RB[b][i][:, :]).then_inc(part2[b], 1)
                    dve.wait_ge(part2[b], 3 * l + SPLIT[at[0]] + 1)
                    v.tensor_tensor(PART[b][i][:, 2, :], RB[b][i][:, :], PART[b][i][:, 1, :], ALU.subtract)\
                        .then_inc(part3[b], 1)
                    if isinstance(l, int) and l == 0 and (b, at[0]) == (0, 0):
                        set_up()
                elif s == "kchigh":
                    dve.wait_ge(G.free(("kc", 0), l), G.read(("kc", 0), l))
                    v.tensor_copy(KCPART[:, 0, :], KC32[:, :]).then_inc(kc_part1, 1)
                    dve.wait_ge(kc_part1, l + 1)
                    v.tensor_tensor(KCREST[:, :], KC32[:, :], KCPART[:, 0, :], ALU.subtract).then_inc(kc_rest1, 1)
                elif s == "kclow":
                    dve.wait_ge(kc_rest1, l + 1)
                    v.tensor_copy(KCPART[:, 1, :], KCREST[:, :]).then_inc(kc_part2, 1)
                    dve.wait_ge(kc_part2, l + 1)
                    v.tensor_tensor(KCPART[:, 2, :], KCREST[:, :], KCPART[:, 1, :], ALU.subtract)\
                        .then_inc(kc_part3, 1)
                elif s in ("smax", "csmax"):
                    t, h0, n = (S_UNITS if s == "smax" else C_UNITS)[at[0]]
                    k = (t + 1) * P if s == "smax" else S
                    dve.wait_ge(Q.full(piece, l), Q.count(piece, l))
                    v.tensor_reduce(MX[b][:, h0 // PH, t, h0 % PH:h0 % PH + n],
                                    Q.at(piece, l)[:, 0:n * k].rearrange("p (h k) -> p h k", k=k),
                                    AX.X, ALU.max).then_inc(Q.free(piece, l), 1)
                elif s == "mrow":
                    split_maxima(piece, l)
                elif s == "heads":
                    dve.wait_ge(num_landed[b], 16 * (HG - 1) * (2 * l + at[0]))
                    dve.wait_ge(den_step[b], 4 * l + 2 * at[0])
                    v.tensor_tensor(ON[b][:, :], ON[b][:, :], OD[b][:, :], ALU.mult).then_inc(o_ready[b], 1)
                elif s in ("oproj", "ocproj", "down"):
                    dve.wait_ge(G.full(piece, l), G.count(piece, l))
                    if s == "oproj":
                        ins = v.scalar_tensor_tensor(out=X[b][:, :], in0=G.at(piece, l)[:, :], scalar=vec(l, V_BO),
                                                     in1=X[b][:, :], op0=ALU.add, op1=ALU.add)
                    else:
                        ins = v.tensor_tensor(X[b][:, :], X[b][:, :], G.at(piece, l)[:, :], ALU.add)
                    ins.then_inc(G.free(piece, l), 1)
                    dve.wait_ge(G.free(piece, l), G.read(piece, l))
                    squares(b)
                elif s == "ffn":
                    c = at[0]
                    dve.wait_ge(silu_ready[b], FC * l + c + 1)
                    v.tensor_tensor(SG[b][:, c, :], SG[b][:, c, :], T.at(piece, l)[:, 512:1024], ALU.mult)\
                        .then_inc(T.free(piece, l), 1)

            qs = [0]

            def step(ins):
                ins.then_inc(q_step, 1)
                qs[0] += 1
                dve.wait_ge(q_step, qs[0])

            def quantise(dst, src, scale, b, q8, done, width):
                a, m = QT[b][0][:, 0:width], QT[b][1][:, 0:width]
                lo, hi = q8
                step(v.tensor_scalar(a, src, scale, None, ALU.mult))
                step(v.tensor_scalar(hi, a, 0.5, None, ALU.mult, saturate=False))
                step(v.tensor_scalar(m, a, -1.0, None, ALU.mult))
                step(v.tensor_tensor(m, a, m, ALU.max))
                step(v.tensor_scalar(m, m, FP8_MAX, None, ALU.is_gt))
                step(v.tensor_scalar(a, a, FP8_MAX, -FP8_MAX, ALU.min, ALU.max))
                step(v.tensor_copy(lo, a, saturate=False))
                step(v.scalar_tensor_tensor(out=a, in0=hi, scalar=2.0, in1=lo, op0=ALU.mult, op1=ALU.subtract))
                step(v.tensor_tensor(a, a, m, ALU.mult))
                v.tensor_tensor(dst, a, lo, ALU.add).then_inc(done, 1)
                dve.wait_ge(done, 1)

            def rest(u):
                s, b = u[:2]
                if s in ("late", "out"):
                    return
                R = after(u)
                if s == "nf":
                    normed_rms(b, LAYERS, 1, uv(U_NF))
                    dve.wait_ge(h_ready[b], 3 * LAYERS + 1)
                    dve.wait_ge(tg_ready, 1)
                    dve.wait_ge(x_again[b], 16)
                    v.scalar_tensor_tensor(out=XO[b], in0=HN[b][:, :], scalar=TG[:, 0:1], in1=XO[b],
                                           op0=ALU.mult, op1=ALU.add).then_inc(xo_ready[b], 1)
                    if b == 0:
                        step(v.reciprocal(SC[:, 0:2], XSC[:, :]))
                        step(v.tensor_tensor(SC[:, 2:3], XSC[:, 0:1], XSC[:, 1:2], ALU.mult))
                        dve.wait_ge(s_kw, 16)
                        quantise(KQ, KW, SC[:, 1:2], 0, QK8, s_kq, P)
                elif s == "mean":
                    dve.wait_ge(xo_ready[b], u[2])
                    centre(b, u[2], XO[b], R)
                elif s == "var" and u[2] == 1:
                    normed(b, 1, HB[b], ln_out[b])
                    dve.wait_ge(ln_out[b], 1)
                    quantise(XQ[b], HB[b], SC[:, 0:1], b, Q8[b], x_q[b], L)
                elif s == "var":
                    normed(b, u[2], HN[b], ln_out[b])
                elif s == "dense":
                    dve.wait_ge(R.full(u), R.count(u))
                    v.tensor_scalar(YB[b], R.at(u)[:, :], SC[:, 2:3], None, ALU.mult).then_inc(R.free(u), 1)
                    dve.wait_ge(R.free(u), R.read(u))
                    v.tensor_scalar(YB[b], YB[b], QBIAS[:, 0:1], None, ALU.add).then_inc(y_step[b], 1)
                    dve.wait_ge(y_step[b], 1)
                    v.scalar_tensor_tensor(out=XO[b], in0=YB[b], scalar=TG[:, 2:3], in1=XO[b],
                                           op0=ALU.mult, op1=ALU.add).then_inc(xo_ready[b], 1)
                elif s == "xvs":
                    dve.wait_ge(s_late, N_LATE)
                    dve.wait_ge(R.full(u), R.count(u))
                    v.tensor_tensor(VS1[b], R.at(u)[0:S, 0:P], BVS[0:S, :], ALU.add).then_inc(R.free(u), 1)
                elif s == "xvc":
                    dve.wait_ge(R.full(u), R.count(u))
                    for t in range(NT):
                        ins = v.tensor_tensor(VC1[b][:, t, :], R.at(u)[:, t * P:(t + 1) * P], BVC[:, :], ALU.add)
                    ins.then_inc(R.free(u), 1)
                elif s == "s1":
                    dve.wait_ge(R.full(u), R.count(u))
                    v.tensor_reduce(ST1[b][:, 0, :], R.at(u)[:, 0:NT * S].rearrange("p (t k) -> p t k", t=NT),
                                    AX.X, ALU.max).then_inc(y_step[b], 1)
                    dve.wait_ge(y_step[b], 2)
                    v.tensor_scalar(ST1[b][:, 1, :], ST1[b][:, 0, :], -SCALE1, None, ALU.mult)\
                        .then_inc(st_step[b], 1)
                elif s == "p1t":
                    w = ("s1", b)
                    dve.wait_ge(exp1_ready[b], NT)
                    v.reciprocal(ST1[b][:, 3, :], ST1[b][:, 2, :]).then_inc(after(w).free(w), 1)
                    dve.wait_ge(after(w).free(w), after(w).read(w))
                    v.tensor_tensor(P1[b], P1[b],
                                    ST1[b][:, 3, :].rearrange("p (t o) -> p t o", o=1).broadcast_to([P, NT, S]),
                                    ALU.mult).then_inc(p1_ready[b], 1)
                elif s == "s2":
                    dve.wait_ge(R.full(u), R.count(u))
                    v.tensor_reduce(ST2[b][0:S, 0:1], R.at(u)[0:S, :], AX.X, ALU.max).then_inc(st_step[b], 1)
                    dve.wait_ge(st_step[b], 2)
                    v.tensor_scalar(ST2[b][0:S, 1:2], ST2[b][0:S, 0:1], -SCALE1, None, ALU.mult)\
                        .then_inc(st_step[b], 1)
                elif s == "p2t":
                    w = ("s2", b)
                    dve.wait_ge(exp2_ready[b], 1)
                    v.reciprocal(ST2[b][0:S, 3:4], ST2[b][0:S, 2:3]).then_inc(after(w).free(w), 1)
                    dve.wait_ge(after(w).free(w), after(w).read(w))
                    v.tensor_scalar(P2[b], P2[b], ST2[b][0:S, 3:4], None, ALU.mult).then_inc(p2_ready[b], 1)
                elif s == "s2c":
                    dve.wait_ge(R.free(u), R.read(u))
                    w = ("c2s", b)
                    dve.wait_ge(after(w).free(w), after(w).read(w))
                    v.tensor_tensor(OD[b][:, :], RA[b][0][:, :], RB[b][0][:, :], ALU.subtract)\
                        .then_inc(y_step[b], 1)
                elif s == "gate":
                    dve.wait_ge(R.free(u), R.read(u))
                    dve.wait_ge(y_step[b], 3)
                    v.tensor_tensor(OD[b][:, :], OD[b][:, :], ON[b][:, :], ALU.mult).then_inc(gate_ready[b], 1)
                    dve.wait_ge(gate_ready[b], 1)
                    v.tensor_tensor(HN[b][:, :], OD[b][:, :], RB[b][0][:, :], ALU.add).then_inc(y_step[b], 1)
                    dve.wait_ge(y_step[b], 4)
                    v.scalar_tensor_tensor(out=XO[b], in0=HN[b][:, :], scalar=TG[:, 1:2], in1=XO[b],
                                           op0=ALU.mult, op1=ALU.add).then_inc(xo_ready[b], 1)
                elif s == "router":
                    choose(u, R)
                elif s == "spread":
                    dve.wait_ge(R.free(u), R.read(u))
                    v.tensor_tensor(XM[b][:, u[2], :], HN[b][:, :], me(b, u[2]), ALU.mult).then_inc(xm_ready[b], 1)
                elif s == "moe":
                    dve.wait_ge(es_ready[b], u[2] + 1)
                    v.tensor_tensor(SG[b][:, u[2], :], SG[b][:, u[2], :], R.at(u)[:, 512:1024], ALU.mult)\
                        .then_inc(R.free(u), 1)
                elif s == "edown":
                    acc, tmp, e = ON[b], OD[b], u[2]
                    dve.wait_ge(R.full(u), R.count(u))
                    v.tensor_tensor((tmp if e else acc)[:, :], me(b, e), R.at(u)[:, :], ALU.mult)\
                        .then_inc(R.free(u), 1)
                    if e:
                        dve.wait_ge(R.free(u), R.read(u))
                        v.tensor_tensor(acc[:, :], acc[:, :], tmp[:, :], ALU.add).then_inc(ey_step[b], 1)
                        dve.wait_ge(ey_step[b], e)
                    if e == NE - 1:
                        v.scalar_tensor_tensor(out=XO[b], in0=acc[:, :], scalar=TG[:, 3:4], in1=XO[b],
                                               op0=ALU.mult, op1=ALU.add).then_inc(xo_ready[b], 1)

            def choose(u, R):
                b = u[1]
                rt, n = RT[b], [0]

                def rstep(ins):
                    ins.then_inc(rt_step[b], 1)
                    n[0] += 1
                    dve.wait_ge(rt_step[b], n[0])

                dve.wait_ge(R.full(u), R.count(u))
                logits = rt[:, 0, :, :]
                v.tensor_copy(logits, R.at(u)[:, 0:NT * NE].rearrange("p (t e) -> p t e", e=NE))\
                    .then_inc(R.free(u), 1)
                dve.wait_ge(R.free(u), R.read(u))
                top = rt[:, 1, :, 0:1]
                rstep(v.tensor_reduce(top, logits, AX.X, ALU.max))
                eq = rt[:, 2, :, :]
                rstep(v.tensor_tensor(eq, logits, top.broadcast_to([P, NT, NE]), ALU.is_ge))
                left, pick = rt[:, 3, :, :], rt[:, 4, :, :]
                rstep(v.tensor_scalar(left[:, :, 0:1], eq[:, :, 0:1], -1.0, 1.0, ALU.mult, ALU.add))
                for e in range(1, NE):
                    rstep(v.tensor_tensor(pick[:, :, e:e + 1], eq[:, :, e:e + 1], left[:, :, e - 1:e], ALU.mult))
                    if e < NE - 1:
                        rstep(v.tensor_tensor(left[:, :, e:e + 1], left[:, :, e - 1:e], pick[:, :, e:e + 1],
                                              ALU.subtract))
                v.tensor_copy(OH[b][:, :, 0:1], eq[:, :, 0:1])
                rstep(v.tensor_copy(OH[b][:, :, 1:NE], pick[:, :, 1:NE]))

            turns(dve, "dve", do, rest)


def constants(BF):
    inv = (1.0 / 10000.0 ** (np.arange(0, HD, 2, dtype=np.float32) / np.float32(HD))).astype(np.float32)
    angle = np.arange(L, dtype=np.float32)[:, None] * inv[None, :]
    cos = np.cos(np.concatenate([angle, angle], 1)).astype(np.float32)
    sin = np.sin(np.concatenate([-angle, angle], 1)).astype(np.float32)
    bf = BF
    q = np.arange(P)
    pos = np.clip((np.arange(L, dtype=np.float32) + np.float32(0.5)) * np.float32(S / L) - np.float32(0.5),
                  0.0, S - 1).astype(np.float32)
    lo = np.floor(pos).astype(np.int32)
    hi = np.minimum(lo + 1, S - 1)
    w = (pos - lo.astype(np.float32)).astype(np.float32)
    interp = np.zeros((S, L), np.float32)
    np.add.at(interp, (lo, np.arange(L)), np.float32(1) - w)
    np.add.at(interp, (hi, np.arange(L)), w)
    return dict(
        cos=np.ascontiguousarray(np.repeat(cos.T, H, 0)),
        sin=np.ascontiguousarray(np.repeat(sin.T, H, 0)),
        idb=np.eye(P, dtype=bf), idf=np.eye(P, dtype=np.float32),
        onesd=np.full((P, P), 1.0 / P, np.float32),
        triq=np.where(q[None, :] <= q[:, None], 0.0, NEG).astype(bf),
        trik=np.where(q[:, None] <= q[None, :], 0.0, NEG).astype(bf),
        iota=np.broadcast_to(np.arange(S, dtype=np.float32), (P, S)).copy(),
        kidx=np.stack([q, q + LOOKBACK], 1).astype(np.float32),
        interp=interp,
    )


def kernel(**inputs):
    import numpy as _np
    import concourse.bacc as _bacc
    from concourse import mybir as _mybir
    from concourse.bass_utils import run_bass_kernel_spmd as _run

    a = {k: _np.asarray(x) for k, x in inputs.items()}
    d_h = _np.arange(P).reshape(H, HD).T.reshape(-1)
    rot = (_np.arange(HD) + HD // 2) % HD
    d_h_rot = _np.arange(P).reshape(H, HD)[:, rot].T.reshape(-1)
    out_rows = _np.arange(P).reshape(NG, HG, HD).transpose(1, 2, 0).reshape(-1)

    def cat(blocks):
        return _np.ascontiguousarray(_np.concatenate(blocks, 1))

    wqkv, bqkv = a["L0_xattn_Wqkv"], a["L0_xattn_bqkv"]
    w1, w2, w3, bv, vec = [], [], [], [], []
    for l in range(LAYERS):
        wq, wk, wv = wqkv[l, :P], wqkv[l, P:2 * P], wqkv[l, 2 * P:]
        bq, bk = bqkv[l, :P], bqkv[l, P:2 * P]
        w1.append(cat([wq[d_h].T, wq[d_h_rot].T, wk[d_h].T, wk[d_h_rot].T, wv.T]))
        bv.append(_np.broadcast_to(bqkv[l, 2 * P:], (P, P)).copy())
        wkv = a["L0_xattn_Wkv_c"][l]
        w2.append(cat([a["L0_xattn_Wo"][l][:, out_rows].T, a["L0_xattn_Wq_c"][l][d_h].T,
                       wkv[:P][d_h].T, wkv[P:].T]))
        w3.append(cat([a["L0_xattn_Wo_c"][l][:, out_rows].T, a["L0_xattn_Wg"][l].T, a["L0_xattn_Wu"][l].T]
                      + [a["L0_xattn_Wd"][l][:, c * P:(c + 1) * P].T for c in range(FC)]))
        vec += [a["L0_xattn_n1"][l], a["L0_xattn_n2"][l], a["L0_xattn_n3"][l], a["L0_xattn_bo"][l],
                bq[d_h], bq[d_h_rot], bk[d_h], bk[d_h_rot]]
    w1.append(w1[0])
    w2.append(w2[0])
    bv.append(bv[0])
    seg = a["itok_BxS_0_255"].reshape(-1)
    wg = a["L1_xattn_Wg"]
    wvx, wp = a["L1_ffn_w_v"], a["L1_ffn_w_proj"]
    arrays = dict(
        x=_np.ascontiguousarray(a["x"].transpose(0, 2, 1)),
        ctx=_np.ascontiguousarray(a["ctx_1024"].reshape(B * S, P).T),
        segr=_np.ascontiguousarray(_np.broadcast_to(seg, (S, B * L))),
        segc=_np.ascontiguousarray(seg.reshape(B * NT, P).T),
        gates=_np.broadcast_to(_np.concatenate([a["g_xattn"], a["g_ffn"]]), (P, 4)).copy(),
        w1=_np.stack(w1), w2=_np.stack(w2), w3=_np.stack(w3), bv=_np.stack(bv),
        vec=_np.ascontiguousarray(_np.stack(vec, 1)),
        uv=_np.stack([a["L0_xattn_nf"], a["L1_xattn_bq_c"], a["L1_xattn_bk_s"],
                      a["L1_xattn_bq_s"], a["L1_xattn_bk_c"], a["L1_xattn_bg"]], 1),
        qbias=_np.ascontiguousarray(a["L0_ffn_bias"].reshape(P, 1)),
        kw=_np.ascontiguousarray(a["L0_ffn_kernel"]),
        xsc=_np.broadcast_to(_np.concatenate([a["L0_ffn_input_scale"], a["L0_ffn_kernel_scale"]]), (P, 2)).copy(),
        wx=cat([a["L1_xattn_" + n].T for n in ("Wq_c", "Wk_s", "Wv_s", "Wq_s", "Wk_c", "Wv_c")]
               + [wg[:, :P].T, wg[:, P:].T]),
        bvs=_np.broadcast_to(a["L1_xattn_bv_s"], (P, P)).copy(),
        bvc=_np.broadcast_to(a["L1_xattn_bv_c"], (P, P)).copy(),
        wr=_np.ascontiguousarray(a["L1_ffn_w_router"]),
        wv=_np.ascontiguousarray(wvx.transpose(1, 0, 2).reshape(P, -1)),
        wp=_np.ascontiguousarray(wp.reshape(NE, FC, P, P).transpose(2, 0, 1, 3).reshape(P, -1)),
        **constants(a["L0_ffn_kernel"].dtype))
    nc = _bacc.Bacc("TRN2", target_bir_lowering=False, num_devices=1)
    d = {}
    for name, arr in arrays.items():
        d[name] = nc.dram_tensor(f"in_{name}", arr.shape, _mybir.dt.from_np(arr.dtype), kind="ExternalInput").ap()
    out = nc.dram_tensor("out_t", (B, P, L), _mybir.dt.float32, kind="ExternalOutput").ap()
    build(nc, d, out)
    r = _run(nc, [{f"in_{k}": x for k, x in arrays.items()}], core_ids=[0])
    return _np.ascontiguousarray(r.results[0]["out_t"].transpose(0, 2, 1))
```
